# Optimizing a Trainium2 kernel written in Bass

```python
import numpy as np
import jax
import jax.numpy as jnp

def _softmax(x, axis=-1):
    return jax.nn.softmax(x, axis=axis)

def _gelu(x):
    return jax.nn.gelu(x, approximate=True)

def _silu(x):
    return jax.nn.silu(x)

def _sigmoid(x):
    return jax.nn.sigmoid(x)

def _layernorm(x, axis=-1, eps=1e-05):
    m = jnp.mean(x, axis=axis, keepdims=True)
    v = jnp.var(x, axis=axis, keepdims=True)
    return (x - m) / jnp.sqrt(v + eps)

def _scatter_add(tgt, idx, src, axis=0):
    return tgt.at[idx].add(src)

def _segment_sum(src, seg, n):
    return jax.ops.segment_sum(src, seg, n)
kernel_name = 'mk_decoder_preln_d1_seqx_r8_c2bf46'

def setup_inputs(seed: int=0):
    np.random.seed(seed)
    _w = jnp.asarray

    def _rec_inputs():
        import jax
        import jax.numpy as jnp
        _rk = jax.random.key(seed)
        x = -0.000125 + 0.9999 * jax.random.normal(jax.random.fold_in(_rk, 1), (64, 64, 256), jnp.float32)
        _lenS = 64 - jax.random.randint(jax.random.fold_in(_rk, 7), (64,), 0, max(1, 64 // 4) + 1, jnp.int32)
        _lenS2 = 64 - jax.random.randint(jax.random.fold_in(_rk, 8), (64,), 0, max(1, 64 // 4) + 1, jnp.int32)
        _ctx_2048P = jax.random.normal(jax.random.fold_in(_rk, 11), (64, 16, 256), jnp.float32)
        _ctx_2048c = jax.random.dirichlet(jax.random.fold_in(_rk, 511), 0.3 * jnp.ones((16,), jnp.float32), (64, 64))
        _ctx_2048t = jnp.einsum('bsk,bkd->bsd', _ctx_2048c, _ctx_2048P)
        _ctx_2048t = _ctx_2048t * jax.lax.rsqrt(jnp.mean(jnp.square(_ctx_2048t)) + 1e-12) * 0.953939
        ctx_2048 = -1.52775e-05 + 0.999936 * (_ctx_2048t + 0.3 * jax.random.normal(jax.random.fold_in(_rk, 611), (64, 64, 256), jnp.float32))
        return (x, ctx_2048)
    x, ctx_2048 = _rec_inputs()

    def _L0_attn_setup():
        import jax, jax.numpy as jnp
        import numpy as np
        HIDDEN = 256
        HEAD_DIM = 64
        N_HEADS = HIDDEN // HEAD_DIM
        ROT_DIM = HEAD_DIM // 2
        THETA = 10000.0
        SCALE_BASE = 512.0
        EPS = 1e-05
        B, S = (1, 256)

        def _rotate_half(t):
            x1 = t[..., 0::2]
            x2 = t[..., 1::2]
            return jnp.stack([-x2, x1], axis=-1).reshape(t.shape)

        def _xpos_rotary(q, k, seqlen):
            dim = ROT_DIM
            inv_freq = 1.0 / THETA ** (jnp.arange(0, dim, 2, dtype=jnp.float32) / dim)
            t = jnp.arange(seqlen, dtype=jnp.float32)
            freqs = t[:, None] * inv_freq[None, :]
            freqs = jnp.repeat(freqs, 2, axis=-1)
            base_scale = (jnp.arange(0, dim, 2, dtype=jnp.float32) + 0.4 * dim) / (1.4 * dim)
            power = (t - seqlen // 2) / SCALE_BASE
            scale = base_scale[None, :] ** power[:, None]
            scale = jnp.concatenate([scale, scale], axis=-1)
            cos, sin = (jnp.cos(freqs), jnp.sin(freqs))

            def apply(x, sc):
                xr, xp = (x[..., :dim], x[..., dim:])
                xr = xr * cos * sc + _rotate_half(xr) * sin * sc
                return jnp.concatenate([xr, xp], axis=-1)
            return (apply(q, scale), apply(k, 1.0 / scale))

        def _msr_forward(x, wqkv, wg, wo, gn_weight, gn_bias):
            b, s, _ = x.shape
            qkv = x @ wqkv.T
            qkv = qkv.reshape(b, s, N_HEADS, 3 * HEAD_DIM).transpose(0, 2, 1, 3)
            q, k, v = jnp.split(qkv, 3, axis=-1)
            q, k = _xpos_rotary(q, k, s)
            gamma = 1.0 - 2.0 ** (-5.0 - jnp.arange(N_HEADS, dtype=jnp.float32))
            idx = jnp.arange(s)
            nm = idx[:, None] - idx[None, :]
            decay = jnp.where(nm >= 0, gamma[:, None, None] ** jnp.maximum(nm, 0).astype(jnp.float32), 0.0)
            scores = jnp.einsum('bhid,bhjd->bhij', q, k) * decay
            ret = jnp.einsum('bhij,bhjd->bhid', scores, v)
            mean = ret.mean(axis=(2, 3), keepdims=True)
            var = ret.var(axis=(2, 3), keepdims=True)
            ret = (ret - mean) / jnp.sqrt(var + EPS)
            ret = ret * gn_weight[None, :, None, None] + gn_bias[None, :, None, None]
            y = ret.transpose(0, 2, 1, 3).reshape(b, s, HIDDEN)
            g = x @ wg.T
            mish = g * jnp.tanh(jax.nn.softplus(g))
            return mish * y @ wo.T
        key = jax.random.key(seed)
        ks = jax.random.split(key, 4)
        std = HIDDEN ** (-0.5)
        x = jax.random.normal(ks[0], (B, S, HIDDEN), jnp.float32)
        wqkv = jax.random.normal(ks[1], (3 * HIDDEN, HIDDEN), jnp.float32) * std
        wg = jax.random.normal(ks[2], (HIDDEN, HIDDEN), jnp.float32) * std
        wo = jax.random.normal(ks[3], (HIDDEN, HIDDEN), jnp.float32) * std
        gn_weight = jnp.ones((N_HEADS,), jnp.float32)
        gn_bias = jnp.zeros((N_HEADS,), jnp.float32)
        return {'x': x, 'wqkv': wqkv, 'wg': wg, 'wo': wo, 'gn_weight': gn_weight, 'gn_bias': gn_bias}
    _L0_attn_all = _L0_attn_setup()
    _L0_attn_in = {k: v for k, v in _L0_attn_all.items() if k in ('wqkv', 'wg', 'wo', 'gn_weight', 'gn_bias')}
    del _L0_attn_all

    def _L0_xattn_setup():
        import jax, jax.numpy as jnp
        import numpy as np
        B, S, D, H = (4, 512, 256, 16)
        HD = D // H
        key = jax.random.key(seed)
        ks = jax.random.split(key, 12)
        sc = 1.0 / np.sqrt(D)
        inp = {'q': jax.random.normal(ks[0], (B, S, D), jnp.float32), 'k': jax.random.normal(ks[1], (B, S, D), jnp.float32), 'v': jax.random.normal(ks[2], (B, S, D), jnp.float32), 'Wq': jax.random.normal(ks[3], (D, D), jnp.float32) * sc, 'bq': jnp.zeros((D,), jnp.float32), 'Wk': jax.random.normal(ks[4], (D, D), jnp.float32) * sc, 'bk': jnp.zeros((D,), jnp.float32), 'Wv': jax.random.normal(ks[5], (D, D), jnp.float32) * sc, 'bv': jnp.zeros((D,), jnp.float32), 'Wo': jax.random.normal(ks[6], (D, D), jnp.float32) * sc, 'bo': jnp.zeros((D,), jnp.float32)}
        return inp
    _L0_xattn_all = _L0_xattn_setup()
    _L0_xattn_in = {k: v for k, v in _L0_xattn_all.items() if k in ('Wq', 'bq', 'Wk', 'bk', 'Wv', 'bv', 'Wo', 'bo')}
    del _L0_xattn_all

    def _L0_ffn_setup():
        import jax, jax.numpy as jnp
        import numpy as np
        H = 256
        E = 16
        K = 4
        I = 176
        SH_I = 2 * I
        B, S = (1, 128)
        key = jax.random.key(seed)
        ks = jax.random.split(key, 9)
        sc_h = 1.0 / np.sqrt(H)
        sc_i = 1.0 / np.sqrt(I)
        return {'hidden_states': jax.random.normal(ks[0], (B, S, H), dtype=jnp.float32), 'w_gate': jax.random.normal(ks[1], (E, H), dtype=jnp.float32) * sc_h, 'wg': jax.random.normal(ks[2], (E, H, I), dtype=jnp.float32) * sc_h, 'wu': jax.random.normal(ks[3], (E, H, I), dtype=jnp.float32) * sc_h, 'wd': jax.random.normal(ks[4], (E, I, H), dtype=jnp.float32) * sc_i, 'sg': jax.random.normal(ks[5], (H, SH_I), dtype=jnp.float32) * sc_h, 'su': jax.random.normal(ks[6], (H, SH_I), dtype=jnp.float32) * sc_h, 'sd': jax.random.normal(ks[7], (SH_I, H), dtype=jnp.float32) * (1.0 / np.sqrt(SH_I))}
    _L0_ffn_all = _L0_ffn_setup()
    _L0_ffn_in = {k: v for k, v in _L0_ffn_all.items() if k in ('w_gate', 'wg', 'wu', 'wd', 'sg', 'su', 'sd')}
    del _L0_ffn_all
    return {'x': x, 'ctx_2048': ctx_2048, 'L0_attn_wqkv': _L0_attn_in['wqkv'], 'L0_attn_wg': _L0_attn_in['wg'], 'L0_attn_wo': _L0_attn_in['wo'], 'L0_attn_gn_weight': _L0_attn_in['gn_weight'], 'L0_attn_gn_bias': _L0_attn_in['gn_bias'], 'L0_xattn_Wq': _L0_xattn_in['Wq'], 'L0_xattn_bq': _L0_xattn_in['bq'], 'L0_xattn_Wk': _L0_xattn_in['Wk'], 'L0_xattn_bk': _L0_xattn_in['bk'], 'L0_xattn_Wv': _L0_xattn_in['Wv'], 'L0_xattn_bv': _L0_xattn_in['bv'], 'L0_xattn_Wo': _L0_xattn_in['Wo'], 'L0_xattn_bo': _L0_xattn_in['bo'], 'L0_ffn_w_gate': _L0_ffn_in['w_gate'], 'L0_ffn_wg': _L0_ffn_in['wg'], 'L0_ffn_wu': _L0_ffn_in['wu'], 'L0_ffn_wd': _L0_ffn_in['wd'], 'L0_ffn_sg': _L0_ffn_in['sg'], 'L0_ffn_su': _L0_ffn_in['su'], 'L0_ffn_sd': _L0_ffn_in['sd']}

def reference(x, ctx_2048, L0_attn_wqkv, L0_attn_wg, L0_attn_wo, L0_attn_gn_weight, L0_attn_gn_bias, L0_xattn_Wq, L0_xattn_bq, L0_xattn_Wk, L0_xattn_bk, L0_xattn_Wv, L0_xattn_bv, L0_xattn_Wo, L0_xattn_bo, L0_ffn_w_gate, L0_ffn_wg, L0_ffn_wu, L0_ffn_wd, L0_ffn_sg, L0_ffn_su, L0_ffn_sd):
    import jax
    import jax.numpy as jnp

    def _L0_attn_ref(x, wqkv, wg, wo, gn_weight, gn_bias):
        import jax, jax.numpy as jnp
        import numpy as np
        HIDDEN = 256
        HEAD_DIM = 64
        N_HEADS = HIDDEN // HEAD_DIM
        ROT_DIM = HEAD_DIM // 2
        THETA = 10000.0
        SCALE_BASE = 512.0
        EPS = 1e-05
        B, S = (1, 256)

        def _rotate_half(t):
            x1 = t[..., 0::2]
            x2 = t[..., 1::2]
            return jnp.stack([-x2, x1], axis=-1).reshape(t.shape)

        def _xpos_rotary(q, k, seqlen):
            dim = ROT_DIM
            inv_freq = 1.0 / THETA ** (jnp.arange(0, dim, 2, dtype=jnp.float32) / dim)
            t = jnp.arange(seqlen, dtype=jnp.float32)
            freqs = t[:, None] * inv_freq[None, :]
            freqs = jnp.repeat(freqs, 2, axis=-1)
            base_scale = (jnp.arange(0, dim, 2, dtype=jnp.float32) + 0.4 * dim) / (1.4 * dim)
            power = (t - seqlen // 2) / SCALE_BASE
            scale = base_scale[None, :] ** power[:, None]
            scale = jnp.concatenate([scale, scale], axis=-1)
            cos, sin = (jnp.cos(freqs), jnp.sin(freqs))

            def apply(x, sc):
                xr, xp = (x[..., :dim], x[..., dim:])
                xr = xr * cos * sc + _rotate_half(xr) * sin * sc
                return jnp.concatenate([xr, xp], axis=-1)
            return (apply(q, scale), apply(k, 1.0 / scale))

        def _msr_forward(x, wqkv, wg, wo, gn_weight, gn_bias):
            b, s, _ = x.shape
            qkv = x @ wqkv.T
            qkv = qkv.reshape(b, s, N_HEADS, 3 * HEAD_DIM).transpose(0, 2, 1, 3)
            q, k, v = jnp.split(qkv, 3, axis=-1)
            q, k = _xpos_rotary(q, k, s)
            gamma = 1.0 - 2.0 ** (-5.0 - jnp.arange(N_HEADS, dtype=jnp.float32))
            idx = jnp.arange(s)
            nm = idx[:, None] - idx[None, :]
            decay = jnp.where(nm >= 0, gamma[:, None, None] ** jnp.maximum(nm, 0).astype(jnp.float32), 0.0)
            scores = jnp.einsum('bhid,bhjd->bhij', q, k) * decay
            ret = jnp.einsum('bhij,bhjd->bhid', scores, v)
            mean = ret.mean(axis=(2, 3), keepdims=True)
            var = ret.var(axis=(2, 3), keepdims=True)
            ret = (ret - mean) / jnp.sqrt(var + EPS)
            ret = ret * gn_weight[None, :, None, None] + gn_bias[None, :, None, None]
            y = ret.transpose(0, 2, 1, 3).reshape(b, s, HIDDEN)
            g = x @ wg.T
            mish = g * jnp.tanh(jax.nn.softplus(g))
            return mish * y @ wo.T
        return _msr_forward(x, wqkv, wg, wo, gn_weight, gn_bias)

    def _L0_xattn_ref(q, k, v, Wq, bq, Wk, bk, Wv, bv, Wo, bo):
        import jax, jax.numpy as jnp
        import numpy as np
        B, S, D, H = (4, 512, 256, 16)
        HD = D // H
        bs, sl, nf = q.shape
        Q = (q @ Wq.T + bq).reshape(bs, sl, H, HD)
        K = (k @ Wk.T + bk).reshape(bs, sl, H, HD)
        V = (v @ Wv.T + bv).reshape(bs, sl, H, HD)
        score = jnp.einsum('bshd,bsgd->bshg', Q, K)
        weight = jax.nn.softmax(score, axis=-1)
        attn = jnp.einsum('bshg,bsgd->bshd', weight, V).reshape(bs, sl, nf)
        return attn @ Wo.T + bo

    def _L0_ffn_ref(hidden_states, w_gate, wg, wu, wd, sg, su, sd):
        import jax, jax.numpy as jnp
        import numpy as np
        H = 256
        E = 16
        K = 4
        I = 176
        SH_I = 2 * I
        B, S = (1, 128)
        b, s, h = hidden_states.shape
        x = hidden_states.reshape(-1, h)
        T = x.shape[0]
        logits = x @ w_gate.T
        probs = jax.nn.softmax(logits.astype(jnp.float32), axis=-1)
        top_w, top_i = jax.lax.top_k(probs, K)
        routing_weight = jnp.zeros((T, E), dtype=probs.dtype)
        routing_weight = routing_weight.at[jnp.arange(T)[:, None], top_i].add(top_w)
        g = jnp.einsum('th,ehi->tei', x, wg)
        u = jnp.einsum('th,ehi->tei', x, wu)
        act = jax.nn.silu(g) * u
        routed = jnp.einsum('te,tei,eih->th', routing_weight, act, wd)
        shared = jax.nn.silu(x @ sg) * (x @ su) @ sd
        out = (routed + shared).astype(hidden_states.dtype)
        return out.reshape(b, s, h)
    x = x + _L0_attn_ref(_layernorm(x, axis=-1), L0_attn_wqkv, L0_attn_wg, L0_attn_wo, L0_attn_gn_weight, L0_attn_gn_bias)
    x = x + _L0_xattn_ref(_layernorm(x, axis=-1), ctx_2048, ctx_2048, L0_xattn_Wq, L0_xattn_bq, L0_xattn_Wk, L0_xattn_bk, L0_xattn_Wv, L0_xattn_bv, L0_xattn_Wo, L0_xattn_bo)
    x = x + _L0_ffn_ref(_layernorm(x, axis=-1), L0_ffn_w_gate, L0_ffn_wg, L0_ffn_wu, L0_ffn_wd, L0_ffn_sg, L0_ffn_su, L0_ffn_sd)
    return x

_drawn_inputs = setup_inputs


def setup_inputs(seed=0):
    import zlib

    import numpy as np

    out = dict(_drawn_inputs(seed))
    spreads = {'L0_attn_gn_weight': (1.0, 0.2),
     'L0_attn_gn_bias': (0.0, 0.1),
     'L0_xattn_bq': (0.0, 0.1),
     'L0_xattn_bk': (0.0, 0.1),
     'L0_xattn_bv': (0.0, 0.1),
     'L0_xattn_bo': (0.0, 0.1)}
    factors = {}
    for name, (base, spread) in spreads.items():
        noise = np.random.default_rng([zlib.crc32(name.encode()), seed]).standard_normal(out[name].shape)
        drawn = base * np.exp(spread * noise) if base else spread * noise
        out[name] = jnp.asarray(drawn.astype(out[name].dtype))
    for name, factor in factors.items():
        out[name] = (out[name] * factor).astype(out[name].dtype)
    return out
```

```python
from collections import namedtuple
from contextlib import ExitStack

import numpy as np

import concourse.bass as bass
from concourse import mybir

F32 = mybir.dt.float32
BF16 = mybir.dt.bfloat16
I32 = mybir.dt.int32
U32 = mybir.dt.uint32
ALU = mybir.AluOpType
ACT = mybir.ActivationFunctionType
AX_X = mybir.AxisListType.X

P = 128
BATCH, SEQ, D = 64, 64, 256
TOKENS = BATCH * SEQ
NT = TOKENS // P
KC = D // P
RH, RD = 4, 64
ROT = RD // 2
XH, XD = 16, 16
E, TOPK, INNER = 16, 4, 176
HI = INNER // 2
SH = 2 * INNER
SHC = [(0, 128), (128, 128), (256, 96)]
EPS = 1e-5

XB = 4
REG = TOKENS + P
NET = TOKENS * TOPK // P + E
SPARE = NET - TOKENS * TOPK // P
ROWS = E * REG + SPARE * P

QCH = 4
QH = XH // QCH
CH = QH * XH * XD

LAST = 3
LOOP0, LOOPS = 5, (NT - 6) // 2

Tile = namedtuple("Tile", "t half p")


def tile_at(n, c):
    return Tile(2 * n + c, n + c // 2, c % 2)


def constants():
    f = np.float32
    inv = f(1.0) / f(10000.0) ** (np.arange(0, ROT, 2, dtype=f) / f(ROT))
    t = np.arange(SEQ, dtype=f)
    freqs = np.repeat(t[:, None] * inv[None, :], 2, axis=-1)
    base = (np.arange(0, ROT, 2, dtype=f) + f(0.4 * ROT)) / f(1.4 * ROT)
    scale = base[None, :] ** ((t - SEQ // 2) / f(512.0))[:, None]
    scale = np.concatenate([scale, scale], axis=-1)
    cos, sin = np.cos(freqs).T, np.sin(freqs).T
    sign = np.where(np.arange(ROT) % 2 == 0, f(-1), f(1))[:, None]
    sc = scale.T
    rot = np.stack([cos * sc, cos / sc, sign * sin * sc, sign * sin / sc], axis=1)
    rot = np.tile(rot, (RH, 1, P // SEQ)).astype(f)
    gamma = f(1.0) - f(2.0) ** (f(-5.0) - np.arange(RH, dtype=f))
    j, i = np.arange(P)[:, None], np.arange(P)[None, :]
    lag = i - j
    own = (i // SEQ == j // SEQ) & (lag >= 0)
    decay = np.stack([np.where(own, g ** np.maximum(lag, 0).astype(f), f(0)) for g in gamma], axis=1)
    c = {}
    c["rot_tab"] = rot.reshape(P, 4 * P)
    c["decay_tab"] = decay.astype(f).reshape(P, RH * P)
    c["ident"] = np.eye(P, dtype=f)
    c["head_mean"] = np.where(i // RD == j // RD, f(1.0 / (RD * SEQ)), f(0)).astype(f)
    c["before"] = np.where(j < i, f(1), f(0)).astype(f)
    small = np.zeros((P, 64), f)
    small[:, 0:16] = np.arange(E)
    small[:, 16:32] = np.arange(E) * REG
    small[:, 32:36] = -0.5
    small[0:3, 36:39] = np.eye(3)
    small[:, 40:57] = np.arange(E + 1)
    c["small_tab"] = small
    c["tile_row"] = np.tile(np.arange(NET, dtype=f)[None, :], (P, 1))
    return c


def build(nc, io, out, scratch):
    with ExitStack() as ctx:
        def sb(name, shape, dt=F32):
            return ctx.enter_context(nc.sbuf_tensor(name, shape, dt))

        def sem(name):
            return ctx.enter_context(nc.semaphore(name))

        w_qk = sb("w_qk", [P, KC, 6, P])
        w_v = sb("w_v", [P, KC, D])
        w_g = sb("w_g", [P, KC, D])
        w_o = sb("w_o", [P, KC, D])
        w_xq = sb("w_xq", [P, KC, D])
        w_xkv = sb("w_xkv", [P, KC, 2 * D])
        w_xo = sb("w_xo", [P, KC, D])
        w_route = sb("w_route", [P, KC, E])
        w_sg = sb("w_sg", [P, KC, SH])
        w_su = sb("w_su", [P, KC, SH])
        w_sd = sb("w_sd", [P, len(SHC), D])
        w_gu = sb("w_gu", [P, E, KC, 2 * INNER])
        w_d = sb("w_d", [HI, E, 2, D])
        rot_tab = sb("rot_tab", [P, 4, P])
        decay_tab = sb("decay_tab", [P, RH * P])
        ident = sb("ident", [P, P])
        head_mean = sb("head_mean", [P, P])
        before_f = sb("before_f", [P, P])
        before = sb("before", [P, P], BF16)
        ones = sb("ones", [P, P], BF16)
        small = sb("small", [P, 64])
        expert_no, region0, minus_half, eye3 = small[:, 0:16], small[:, 16:32], small[:, 32:36], small[0:3, 36:39]
        gn_w = sb("gn_w", [P, 4])
        gn_b = sb("gn_b", [P, 4])
        bias3 = sb("bias3", [3, 4 * D])
        bias_hi = sb("bias_hi", [3, 4 * D], BF16)
        bias_mid = sb("bias_mid", [3, 4 * D], BF16)
        bias_lo = sb("bias_lo", [3, 4 * D], BF16)
        bias_r = sb("bias_r", [3, 4 * D])
        bias_parts = sb("bias_parts", [3, 4 * D], BF16)

        def pair(name, shape, dt=F32):
            return [sb(f"{name}{p}", shape, dt) for p in range(2)]

        xin = pair("xin", [P, D])
        ctx_t = pair("ctx_t", [P, KC, P])
        x1 = pair("x1", [P, D])
        x2 = pair("x2", [P, D])
        xn1 = sb("xn1", [P, D])
        xn2 = sb("xn2", [P, D])
        xn3 = pair("xn3", [P, D])
        stats = [sb(f"stats{s}", [P, 6]) for s in range(3)]
        mv = [sb(f"mv{s}", [P, 2]) for s in range(3)]
        var_eps = [sb(f"var_eps{s}", [P, 1]) for s in range(3)]
        rstd = [sb(f"rstd{s}", [P, 1]) for s in range(3)]
        xT1 = sb("xT1", [P, KC, P])
        xT2 = sb("xT2", [P, KC, P])
        xT3 = sb("xT3", [P, KC, P])
        cos_part = sb("cos_part", [P, 2, P])
        sin_part = sb("sin_part", [P, 2, P])
        qk_rot = sb("qk_rot", [P, 2, P])
        k_pass = sb("k_pass", [P, P])
        q_rot = sb("q_rot", [P, RH, P])
        q_pass = sb("q_pass", [P, RH, P])
        v_sb = sb("v_sb", [P, D])
        att_t = sb("att_t", [P, RH * P])
        ret_sq = sb("ret_sq", [P, D])
        sums = sb("sums", [P, 8])
        moments = sb("moments", [P, 8])
        neg_msq = sb("neg_msq", [P, 4])
        gvar = sb("gvar", [P, 4])
        grstd = sb("grstd", [P, 4])
        gscale = sb("gscale", [P, 4])
        gshift = sb("gshift", [P, 4])
        gm = sb("gm", [P, D])
        e_g = sb("e_g", [P, D])
        n_g = sb("n_g", [P, D])
        ln_g = sb("ln_g", [P, D])
        rec_g = sb("rec_g", [P, D])
        th_g = sb("th_g", [P, D])
        mish = sb("mish", [P, D])
        y_sb = sb("y_sb", [P, KC, P])
        my = sb("my", [P, KC, P])
        kv = pair("kv", [P, 2 * D])
        prod = sb("prod", [P, 2, CH])
        scores = sb("scores", [P, XH * XH])
        score_max = sb("score_max", [P, XH])
        score_sub = sb("score_sub", [P, XH * XH])
        prob = pair("prob", [P, XH * XH])
        prob_sum = sb("prob_sum", [P, XH])
        prob_rec = pair("prob_rec", [P, XH])
        av = sb("av", [P, 2, CH])
        attn = sb("attn", [P, D])
        attn_n = sb("attn_n", [P, D])
        attn_t = sb("attn_t", [P, KC, P])
        neg_max = sb("neg_max", [P, 1])
        exp_l = sb("exp_l", [P, E])
        sum_l = sb("sum_l", [P, 1])
        rec_l = sb("rec_l", [P, 1])
        prob_l = sb("prob_l", [P, E])
        top8 = sb("top8", [P, 8])
        idx8 = sb("idx8", [P, 8], U32)
        idx_f = sb("idx_f", [P, TOPK])
        pick = sb("pick", [P, TOPK, E])
        chosen = sb("chosen", [P, E], BF16)
        row_base = sb("row_base", [P, E])
        row_of = sb("row_of", [P, E])
        pick_row = sb("pick_row", [P, TOPK, E])
        row_f = sb("row_f", [P, TOPK])
        row_u = pair("row_u", [P, TOPK], U32)
        sh_s = sb("sh_s", [P, len(SHC), P])
        sh_a = sb("sh_a", [P, len(SHC), P])
        x3 = pair("x3", [P, D])
        row_all = sb("row_all", [P, NT, TOPK])
        pick_all = sb("pick_all", [P, NT, TOPK])
        shift = sb("shift", [P, NT, TOPK])
        wt_all = sb("wt_all", [P, NT, TOPK])

        NX = E + 1
        zeros = sb("zeros", [P, D])
        cnt = sb("cnt", [P, NX])
        cnt_i = sb("cnt_i", [P, NX], I32)
        cum = sb("cum", [P, NX])
        tile_no = sb("tile_no", [P, NET])
        row0 = sb("row0", [P, NX])
        e_of = sb("e_of", [P, NET])
        base_f = sb("base_f", [P, NET])
        table = sb("table", [1, 2, NET], I32)
        tail_i = sb("tail_i", [1, E], I32)

        def carve(t, q, cols):
            return t[:, q * cols // CH, (q * cols) % CH:(q * cols) % CH + cols]

        xe = [carve(prod, q, D) for q in range(XB)]
        xeT = [carve(prod, 4 + q, D).rearrange("p (k t) -> p k t", k=KC) for q in range(2)]
        he = [carve(prod, 6 + q, D)[:, 0:INNER] for q in range(2)]
        ae = [carve(av, q, D)[:, 0:INNER] for q in range(2)]
        aeT = [carve(av, 2 + q, D)[0:HI].rearrange("p (k t) -> p k t", k=KC) for q in range(2)]
        ye = [carve(av, 4 + q, D) for q in range(2)]
        yg = [[carve(prod, k, D) for k in range(TOPK)], [carve(av, k, D) for k in range(TOPK)]]
        idx_g = row_u
        acc = pair("acc", [P, D])
        tile_tmp = sb("tile_tmp", [P, NET])
        two = sb("two", [P, 1])



        bank = [ctx.enter_context(nc.psum_tensor(f"bank{b}", [P, 512], F32)) for b in range(8)]

        names = """passed tables_in weights_in bias_in consts prep
            ln1_var ln1_rstd ln1_out ln2_var ln2_rstd ln2_out ln3_var ln3_rstd ln3_out
            xT1_ps xT1_sb xT2_ps xT2_sb xT3_ps xT3_sb
            qk_ps pv_ps g_ps rot_parts rot_out qrot_out pass_out v_out sc_ps att_out ret_ps sq_out sums_out stat_ps
            gvar_out gaff_out y_out gm_out eg_out ng_out rec_out th_out mish_out my_out wo_ps x1_out
            q_ps kv_ps kv_out prod_out score_out sub_out prob_out psum_out prec_out
            av_out attn_out attnn_out aT_ps aT_sb xo_ps x2_out
            logit_ps expl_out lmax_out top_out chosen_out rank_ps rows_out
            sg_ps su_ps shs_out sha_out shd_ps xall_out chain pchain achain
            expert_w0 shift_out tab_out zero_in fill_out
            eT_ps eT_sb egu_ps eh_out ea_out eaT_ps eaT_sb ey_ps ey_out idxg_out fin_out""".split()
        S = {n: sem(n) for n in names}
        xin_in = [sem(f"xin_in{p}") for p in range(2)]
        ctx_in = [sem(f"ctx_in{p}") for p in range(2)]
        scat_done = [sem(f"scat_done{p}") for p in range(2)]
        xe_in = [sem(f"xe_in{b}") for b in range(XB)]
        ye_done = [sem(f"ye_done{p}") for p in range(2)]
        gath_done = [sem(f"gath_done{p}") for p in range(2)]
        out_done = [sem(f"out_done{p}") for p in range(2)]
        x3_done = [sem(f"x3_done{p}") for p in range(2)]
        x3_in = [sem(f"x3_in{p}") for p in range(2)]

        rows_dram, y_dram, x3_dram = scratch

        def steps(eng, body):
            for c in range(LOOP0):
                body(0, c)
            with eng.Fori(0, LOOPS) as n:
                for u in range(2):
                    body(n, LOOP0 + u)
            for c in range(LOOP0 + 2 * LOOPS, NT + LAST):
                body(0, c)

        def stage_tiles(n, c):
            peeled = type(n) is int
            return [tile_at(n, c - s) if not peeled or 0 <= c - s < NT else None for s in range(4)]

        def past(eng, s, v):
            if type(v) is int and v <= 0:
                return
            eng.wait_ge(s, v)

        def alone(eng, s, v):
            if type(v) is int and v <= 0:
                return
            eng.wait_ge(s, v)
            eng.sem_inc(S["passed"], 1)

        def groups(eng, count, body, size=2):
            for u in range(size):
                body(0, u, u)
            with eng.Fori(1, count) as n:
                for u in range(size):
                    body(n, size * n + u, u)

        block = ctx.enter_context(nc.Block())

        @block.sync
        def _(sp):
            for dst, src in ((rot_tab[:, :, :].rearrange("p a b -> p (a b)"), "rot_tab"), (decay_tab[:, :], "decay_tab"),
                             (ident[:, :], "ident"), (head_mean[:, :], "head_mean"), (before_f[:, :], "before"),
                             (small[:, :], "small_tab"), (tile_no[:, :], "tile_row"), (gn_w[:, :], "gn_w"), (gn_b[:, :], "gn_b")):
                sp.dma_start(dst, io[src]).then_inc(S["tables_in"], 16)
            sp.dma_start(bias3[:, :], io["bias"].partition_broadcast(3)).then_inc(S["bias_in"], 16)

            def flat(t):
                return t.rearrange("p a b -> p (a b)")

            sp.dma_start(w_qk[:, :, :, :].rearrange("p a b c -> p (a b c)"), io["w_qk"]).then_inc(S["weights_in"], 16)
            for dst, src in ((w_v, "w_v"), (w_g, "w_g"), (w_o, "w_o"), (w_xq, "w_xq"), (w_xkv, "w_xkv"), (w_xo, "w_xo"),
                             (w_route, "w_route"), (w_sg, "w_sg"), (w_su, "w_su")):
                sp.dma_start(flat(dst[:, :, :]), io[src]).then_inc(S["weights_in"], 16)
            for j, (r0, rows) in enumerate(SHC):
                sp.dma_start(w_sd[0:rows, j, :], io["w_sd"][r0:r0 + rows, :]).then_inc(S["weights_in"], 16)

            def load_x(T):
                past(sp, S["x1_out"], T.t - 1)
                sp.dma_start(xin[T.p][:, :], io["x"][bass.ds(T.t * P, P), :]).then_inc(xin_in[T.p], 16)

            def load_ctx(T):
                past(sp, S["kv_ps"], T.t - 1)
                sp.dma_start(ctx_t[T.p][:, :, :].rearrange("p a b -> p (a b)"),
                             io["ctx_t"][bass.ds(T.t * P, P), :]).then_inc(ctx_in[T.p], 16)

            def load_expert(e, p):
                sp.dma_start(w_gu[:, bass.ds(e, 1), :, :].rearrange("p e k n -> p (e k n)"),
                             io["w_gu"][bass.ds(e * P, P), :]).then_inc(S["expert_w0"], 16)
                sp.dma_start(w_d[:, bass.ds(e, 1), :, :].rearrange("p e k n -> p (e k n)"),
                             io["w_d"][bass.ds(e * HI, HI), :]).then_inc(S["expert_w0"], 16)

            def store_x3(T):
                sp.wait_ge(S["xall_out"], T.t + 1)
                sp.dma_start(x3_dram[bass.ds(T.t * P, P), :], x3[T.p][:, :]).then_inc(x3_done[T.p], 16)

            def step(n, c):
                peeled = type(n) is int
                A, B, C, L = stage_tiles(n, c)
                if A:
                    load_x(A)
                if B:
                    load_ctx(B)
                if L:
                    store_x3(L)
                if not peeled and c == LOOP0:
                    load_expert(n, 0)
                if peeled and LOOPS <= c - NT + LOOPS + 1 < E:
                    load_expert(c - NT + LOOPS + 1, 0)

            steps(sp, step)

            for p in range(2):
                sp.wait_ge(scat_done[p], 16 * TOPK * NT // 2)
                sp.wait_ge(x3_done[p], 16 * NT // 2)
            sp.wait_ge(S["tab_out"], 1)
            for e in range(E):
                r = sp.value_load(tail_i[0:1, e:e + 1], min_val=0, max_val=ROWS - P)
                sp.dma_start(rows_dram[bass.ds(r, P), :], zeros[:, :]).then_inc(S["fill_out"], 16)
            for j in range(SPARE):
                sp.dma_start(rows_dram[E * REG + j * P:E * REG + (j + 1) * P, :], zeros[:, :]).then_inc(S["fill_out"], 16)
            sp.wait_ge(S["fill_out"], 16 * (E + SPARE))

            def load_rows(j, turn, b):
                past(sp, S["eT_ps"], j - XB + 1)
                r = sp.value_load(table[0:1, 1, bass.ds(j, 1)], min_val=0, max_val=ROWS - P)
                sp.dma_start(xe[b], rows_dram[bass.ds(r, P), :]).then_inc(xe_in[b], 16)

            def store_rows(j, p):
                sp.wait_ge(S["ey_out"], j + 1)
                sp.dma_start(y_dram[bass.ds(j * P, P), :], ye[p]).then_inc(ye_done[p], 16)

            for j in range(XB):
                load_rows(j, 0, j)

            def row_step(n, j, b):
                load_rows(j + XB, n + 1, b)
                store_rows(j, b % 2)

            groups(sp, NET // XB - 1, row_step, XB)
            for j in range(NET - XB, NET):
                store_rows(j, j % 2)
            for p in range(2):
                sp.wait_ge(ye_done[p], 16 * NET // 2)
            def load_x3(t, half, p):
                past(sp, S["fin_out"], t - 1)
                sp.dma_start(x3[p][:, :], x3_dram[bass.ds(t * P, P), :]).then_inc(x3_in[p], 16)

            def store_out(t, half, p):
                sp.wait_ge(S["fin_out"], t + 1)
                sp.dma_start(out[bass.ds(t * P, P), :], acc[p][:, :]).then_inc(out_done[p], 16)

            load_x3(0, 0, 0)
            load_x3(1, 0, 1)

            def out_step(n, t, p):
                store_out(t, n, p)
                load_x3(t + 2, n + 1, p)

            groups(sp, NT // 2 - 1, out_step)
            store_out(NT - 2, 0, 0)
            store_out(NT - 1, 0, 1)
            for p in range(2):
                sp.wait_ge(out_done[p], 16 * NT // 2)

        @block.gpsimd
        def _(pl):
            nc.gpsimd.memset(q_rot[:, :, :], 0.0)
            nc.gpsimd.memset(q_pass[:, :, :], 0.0)
            nc.gpsimd.memset(zeros[:, :], 0.0)
            nc.gpsimd.memset(ones[:, :], 1.0).then_inc(S["consts"], 1)
            pl.wait_ge(S["tables_in"], 16 * 9)

            def rstd_of(s, T, ready, done):
                pl.wait_ge(ready, T.t + 1)
                nc.gpsimd.tensor_tensor(rstd[s][:, :], var_eps[s][:, :], minus_half[:, 0:1], ALU.pow).then_inc(done, 1)

            def rot_sum(T):
                pl.wait_ge(S["rot_parts"], T.t + 1)
                past(pl, S["sc_ps"], T.t)
                past(pl, S["qrot_out"], T.t)
                nc.gpsimd.tensor_tensor(qk_rot[:, :, :], cos_part[:, :, :], sin_part[:, :, :], ALU.add
                                        ).then_inc(S["rot_out"], 1)

            def values(T, q):
                pl.wait_ge(S["prob_out"], T.t + 1)
                past(pl, S["attn_out"], QCH * T.t + q - 1)
                pr = prob[T.p][:, q * QH * XH:(q + 1) * QH * XH].rearrange("p (h g) -> p h g", g=XH)
                vv = kv[T.p][:, D:2 * D].rearrange("p (g d) -> p d g", g=XH)
                o = av[:, q % 2, :].rearrange("p (h d g) -> p h d g", h=QH, d=XD)
                nc.gpsimd.tensor_tensor(o, pr.unsqueeze(2).to_broadcast([P, QH, XD, XH]),
                                        vv.unsqueeze(1).to_broadcast([P, QH, XD, XH]), ALU.mult).then_inc(S["av_out"], 1)

            def tanh_part(T):
                pl.wait_ge(S["rec_out"], T.t + 1)
                past(pl, S["mish_out"], T.t)
                nc.gpsimd.tensor_tensor(th_g[:, :], n_g[:, :], rec_g[:, :], ALU.mult).then_inc(S["th_out"], 1)

            def group_affine(T):
                pl.wait_ge(S["gvar_out"], T.t + 1)
                past(pl, S["y_out"], T.t)
                nc.gpsimd.tensor_tensor(grstd[:, :], gvar[:, :], minus_half, ALU.pow).then_inc(S["pchain"], 1)
                pl.wait_ge(S["pchain"], 3 * T.t + 1)
                nc.gpsimd.tensor_tensor(gscale[:, :], grstd[:, :], gn_w[:, :], ALU.mult).then_inc(S["pchain"], 1)
                pl.wait_ge(S["pchain"], 3 * T.t + 2)
                nc.gpsimd.tensor_tensor(grstd[:, :], moments[:, 0:4], gscale[:, :], ALU.mult).then_inc(S["pchain"], 1)
                pl.wait_ge(S["pchain"], 3 * T.t + 3)
                nc.gpsimd.tensor_tensor(gshift[:, :], gn_b[:, :], grstd[:, :], ALU.subtract).then_inc(S["gaff_out"], 1)

            def gate(T):
                pl.wait_ge(S["y_out"], T.t + 1)
                pl.wait_ge(S["mish_out"], T.t + 1)
                nc.gpsimd.tensor_tensor(my[:, :, :], mish[:, :].rearrange("p (k t) -> p k t", k=KC), y_sb[:, :, :],
                                        ALU.mult).then_inc(S["my_out"], 1)

            def scatter(T):
                for k in range(TOPK):
                    if k == 0:
                        alone(pl, S["rows_out"], T.t + 1)
                    pl.indirect_dma_start(rows_dram, bass.IndirectOffsetOnAxis(ap=row_u[T.p][:, k:k + 1], axis=0),
                                          xn3[T.p][:, :], None).then_inc(scat_done[T.p], 16)

            def step(n, c):
                A, B, C, L = stage_tiles(n, c)
                if C:
                    values(C, 0)
                if B:
                    rstd_of(1, B, S["ln2_var"], S["ln2_rstd"])
                if L:
                    rstd_of(2, L, S["ln3_var"], S["ln3_rstd"])
                if A:
                    rstd_of(0, A, S["ln1_var"], S["ln1_rstd"])
                if C:
                    values(C, 1)
                    values(C, 2)
                if A:
                    rot_sum(A)
                if C:
                    values(C, 3)
                if L:
                    scatter(L)
                if A:
                    tanh_part(A)
                    group_affine(A)
                    gate(A)

            steps(pl, step)

            pl.wait_ge(S["tab_out"], 1)
            for e in range(E):
                nc.gpsimd.tensor_scalar(shift[:, :, :], pick_all[:, :, :], float(e), row0[:, e:e + 1], ALU.is_equal, ALU.mult
                                        ).then_inc(S["shift_out"], 1)
                pl.wait_ge(S["shift_out"], 2 * e + 1)
                nc.gpsimd.tensor_tensor(row_all[:, :, :], row_all[:, :, :], shift[:, :, :], ALU.subtract
                                        ).then_inc(S["shift_out"], 1)
                pl.wait_ge(S["shift_out"], 2 * e + 2)

            for p in range(2):
                pl.wait_ge(ye_done[p], 16 * NET // 2)
            with pl.Fori(0, NT // 2) as n:
                for p in range(2):
                    for k in range(TOPK):
                        if k == 0:
                            alone(pl, S["idxg_out"], 2 * n + p + 1)
                        pl.indirect_dma_start(yg[p][k], None, y_dram,
                                              bass.IndirectOffsetOnAxis(ap=idx_g[p][:, k:k + 1], axis=0)
                                              ).then_inc(gath_done[p], 16)

        @block.scalar
        def _(act):
            def copy_t(T, src, dst, ready, done, used=None, used_v=0):
                act.wait_ge(ready, T.t + 1)
                if used is not None:
                    past(act, used, used_v)
                nc.scalar.activation(dst, src, ACT.Copy).then_inc(done, 1)

            act.wait_ge(S["consts"], 1)

            def step(n, c):
                A, B, C, L = stage_tiles(n, c)
                if B:
                    copy_t(B, bank[0][:, 0:D], xT2[:, :, :].rearrange("p a b -> p (a b)"), S["xT2_ps"], S["xT2_sb"])
                if L:
                    copy_t(L, bank[0][:, 0:D], xT3[:, :, :].rearrange("p a b -> p (a b)"), S["xT3_ps"], S["xT3_sb"])
                if B:
                    act.wait_ge(S["kv_ps"], B.t + 1)
                    past(act, S["av_out"], QCH * (B.t - 1))
                    nc.scalar.activation(kv[B.p][:, :], bank[6][:, :], ACT.Copy).then_inc(S["kv_out"], 1)
                if L:
                    act.wait_ge(S["lmax_out"], L.t + 1)
                    nc.scalar.activation(exp_l[:, :], bank[3][:, 0:E], ACT.Exp, bias=neg_max[:, 0:1],
                                         accum_out=sum_l[:, 0:1]).then_inc(S["expl_out"], 1)
                if A:
                    copy_t(A, bank[0][:, 0:D], xT1[:, :, :].rearrange("p a b -> p (a b)"), S["xT1_ps"], S["xT1_sb"])
                    act.wait_ge(S["pv_ps"], A.t + 1)
                    past(act, S["sc_ps"], A.t)
                    for h in range(RH):
                        r = slice(ROT * h, ROT * h + ROT)
                        nc.scalar.activation(q_pass[r, h, :], bank[2][r, 0:P], ACT.Copy)
                    nc.scalar.activation(k_pass[:, :], bank[2][:, P:2 * P], ACT.Copy).then_inc(S["pass_out"], 1)
                    past(act, S["ret_ps"], A.t)
                    nc.scalar.activation(v_sb[:, :], bank[2][:, D:2 * D], ACT.Copy).then_inc(S["v_out"], 1)
                if A:
                    act.wait_ge(S["rot_out"], A.t + 1)
                    for h in range(RH):
                        r = slice(ROT * h, ROT * h + ROT)
                        last = nc.scalar.activation(q_rot[r, h, :], qk_rot[r, 0, :], ACT.Copy)
                    last.then_inc(S["qrot_out"], 1)
                if C:
                    copy_t(C, bank[0][:, 0:D], attn_t[:, :, :].rearrange("p a b -> p (a b)"), S["aT_ps"], S["aT_sb"])
                if A:
                    act.wait_ge(S["gm_out"], A.t + 1)
                    past(act, S["ng_out"], A.t)
                    nc.scalar.activation(e_g[:, :], gm[:, :], ACT.Exp).then_inc(S["eg_out"], 1)
                    act.wait_ge(S["ng_out"], A.t + 1)
                    nc.scalar.activation(ln_g[:, :], n_g[:, :], ACT.Ln, bias=two[:, 0:1]).then_inc(S["achain"], 1)
                    act.wait_ge(S["achain"], A.t + 1)
                    past(act, S["th_out"], A.t)
                    nc.scalar.activation(rec_g[:, :], ln_g[:, :], ACT.Exp, scale=-1.0).then_inc(S["rec_out"], 1)
                if L:
                    act.wait_ge(S["sg_ps"], L.t + 1)
                    past(act, S["sha_out"], L.t)
                    nc.scalar.activation(sh_s[:, 0:2, :], bank[1][:, 0:2 * P].rearrange("p (a b) -> p a b", a=2), ACT.Silu)
                    nc.scalar.activation(sh_s[0:96, 2, :], bank[1][0:96, 2 * P:3 * P], ACT.Silu).then_inc(S["shs_out"], 1)
                if A:
                    act.wait_ge(S["ret_ps"], A.t + 1)
                    past(act, S["sums_out"], A.t)
                    nc.scalar.activation(ret_sq[:, :], bank[6][:, 0:D], ACT.Square).then_inc(S["sq_out"], 1)
                if B:
                    act.wait_ge(S["sub_out"], B.t + 1)
                    past(act, S["av_out"], QCH * (B.t - 1))
                    nc.scalar.activation(prob[B.p][:, :], score_sub[:, :], ACT.Exp).then_inc(S["prob_out"], 1)
                if A:
                    act.wait_ge(S["gaff_out"], A.t + 1)
                    past(act, S["my_out"], A.t)
                    for j in range(4):
                        last = nc.scalar.activation(
                            y_sb[:, j // 2, SEQ * (j % 2):SEQ * (j % 2) + SEQ], bank[6][:, SEQ * j:SEQ * j + SEQ],
                            ACT.Identity, bias=gshift[:, j:j + 1], scale=gscale[:, j:j + 1])
                    last.then_inc(S["y_out"], 1)

            steps(act, step)

            def xT_out(j, p):
                act.wait_ge(S["eT_ps"], j + 1)
                past(act, S["egu_ps"], j - 1)
                nc.scalar.activation(xeT[p].rearrange("p a b -> p (a b)"), bank[p][:, 0:D], ACT.Copy).then_inc(S["eT_sb"], 1)

            def silu(j, p):
                act.wait_ge(S["egu_ps"], j + 1)
                past(act, S["ea_out"], j - 1)
                nc.scalar.activation(he[p], bank[2 + p][:, 0:INNER], ACT.Silu).then_inc(S["eh_out"], 1)

            def y_copy(j, half, p):
                act.wait_ge(S["ey_ps"], j + 1)
                past(act, ye_done[p], 16 * half)
                nc.scalar.activation(ye[p], bank[6 + p][:, 0:D], ACT.Copy).then_inc(S["ey_out"], 1)

            xT_out(0, 0)
            silu(0, 0)
            xT_out(1, 1)
            silu(1, 1)
            xT_out(2, 0)

            def expert_step(n, j, u):
                silu(j + 1, 1 - (u + 1) % 2)
                xT_out(j + 2, (u + 1) % 2)
                y_copy(j - 1, n, u)

            groups(act, (NET - 4) // 2, lambda n, j, u: expert_step(n, j + 1, u))
            for j in range(NET - 3, NET):
                if j + 1 < NET:
                    silu(j + 1, (j + 1) % 2)
                if j + 2 < NET:
                    xT_out(j + 2, j % 2)
                y_copy(j - 1, (j - 1) // 2, (j - 1) % 2)
            y_copy(NET - 1, NET // 2 - 1, 1)

        @block.tensor
        def _(pe):
            pe.wait_ge(S["tables_in"], 16 * 9)
            pe.wait_ge(S["weights_in"], 16 * 13)
            pe.wait_ge(S["prep"], 1)
            mm = nc.tensor.matmul

            def turn(T, src, ready, done):
                pe.wait_ge(ready, T.t + 1)
                for k in range(KC):
                    last = nc.tensor.transpose(bank[0][:, k * P:(k + 1) * P], src[:, k * P:(k + 1) * P], ident[:, :])
                last.then_inc(done, 1)

            def add_bias(dst, c0, cols, stop):
                return mm(dst, ones[0:3, :], bias_parts[:, c0:c0 + cols], start=False, stop=stop)

            def cross_in(T):
                pe.wait_ge(S["xT2_sb"], T.t + 1)
                past(pe, S["prod_out"], QCH * T.t)
                for k in range(KC):
                    mm(bank[5][:, 0:D], xT2[:, k, :], w_xq[:, k, :], start=(k == 0), stop=False)
                add_bias(bank[5][:, 0:D], 0, D, True).then_inc(S["q_ps"], 1)
                pe.wait_ge(ctx_in[T.p], 16 * (T.half + 1))
                pe.wait_ge(S["y_out"], T.t + 1)
                for k in range(KC):
                    mm(bank[6][:, :], ctx_t[T.p][:, k, :], w_xkv[:, k, :], start=(k == 0), stop=False)
                add_bias(bank[6][:, :], D, 2 * D, True).then_inc(S["kv_ps"], 1)

            def logits(T, prev):
                pe.wait_ge(S["xT3_sb"], T.t + 1)
                if prev is not None:
                    past(pe, *prev)
                for k in range(KC):
                    last = mm(bank[3][:, 0:E], xT3[:, k, :], w_route[:, k, :], start=(k == 0), stop=(k == KC - 1))
                last.then_inc(S["logit_ps"], 1)

            def ret_in(T, L):
                pe.wait_ge(S["xT1_sb"], T.t + 1)
                past(pe, S["rot_parts"], T.t)
                if L is not None:
                    past(pe, S["sha_out"], L.t)
                elif type(T.t) is int and T.t >= 4:
                    past(pe, S["sha_out"], T.t - LAST)
                for f in range(4):
                    for k in range(KC):
                        last = mm(bank[1][:, f * P:(f + 1) * P], w_qk[:, k, f, :], xT1[:, k, :], start=(k == 0), stop=(k == KC - 1))
                last.then_inc(S["qk_ps"], 1)
                past(pe, S["v_out"], T.t)
                for f in range(2):
                    for k in range(KC):
                        mm(bank[2][:, f * P:(f + 1) * P], w_qk[:, k, 4 + f, :], xT1[:, k, :], start=(k == 0), stop=(k == KC - 1))
                for k in range(KC):
                    last = mm(bank[2][:, D:2 * D], xT1[:, k, :], w_v[:, k, :], start=(k == 0), stop=(k == KC - 1))
                last.then_inc(S["pv_ps"], 1)
                past(pe, S["mish_out"], T.t)
                for f in range(KC):
                    for k in range(KC):
                        last = mm(bank[4][:, f * P:(f + 1) * P], w_g[:, k, f * P:(f + 1) * P], xT1[:, k, :],
                                  start=(k == 0), stop=(k == KC - 1))
                last.then_inc(S["g_ps"], 1)

            def cross_out(T):
                pe.wait_ge(S["aT_sb"], T.t + 1)
                for k in range(KC):
                    mm(bank[7][:, 0:D], attn_t[:, k, :], w_xo[:, k, :], start=(k == 0), stop=False)
                add_bias(bank[7][:, 0:D], 3 * D, D, True).then_inc(S["xo_ps"], 1)

            def ranks(T):
                pe.wait_ge(S["chosen_out"], T.t + 1)
                mm(bank[3][:, 0:E], before[:, :], chosen[:, :], start=True, stop=True)
                mm(bank[3][:, E:2 * E], ones[:, :], chosen[:, :], start=True, stop=True).then_inc(S["rank_ps"], 1)

            def ret_scores(T, L):
                pe.wait_ge(S["qrot_out"], T.t + 1)
                pe.wait_ge(S["pass_out"], T.t + 1)
                if L is not None:
                    pe.wait_ge(S["rows_out"], L.t + 1)
                past(pe, S["gvar_out"], T.t)
                mm(bank[3][:, :], qk_rot[:, 1, :], q_rot[:, :, :].rearrange("p h t -> p (h t)"), start=True, stop=False)
                mm(bank[3][:, :], k_pass[:, :], q_pass[:, :, :].rearrange("p h t -> p (h t)"), start=False,
                   stop=True).then_inc(S["sc_ps"], 1)

            def shared_in(T, A):
                pe.wait_ge(S["xT3_sb"], T.t + 1)
                if A is not None:
                    pe.wait_ge(S["rot_parts"], A.t + 1)
                else:
                    pe.wait_ge(S["sha_out"], T.t)
                for w, b, done in ((w_sg, 1, "sg_ps"), (w_su, 2, "su_ps")):
                    if b == 2 and A is not None:
                        pe.wait_ge(S["v_out"], A.t + 1)
                    for j, (r0, rows) in enumerate(SHC):
                        for k in range(KC):
                            last = mm(bank[b][0:rows, j * P:(j + 1) * P], w[:, k, r0:r0 + rows], xT3[:, k, :],
                                      start=(k == 0), stop=(k == KC - 1))
                    last.then_inc(S[done], 1)

            def retain(T, B):
                pe.wait_ge(S["att_out"], T.t + 1)
                if B is not None:
                    pe.wait_ge(S["kv_out"], B.t + 1)
                for h in range(RH):
                    last = mm(bank[6][RD * (h % 2):RD * (h % 2) + RD, (h // 2) * P:(h // 2 + 1) * P],
                              v_sb[:, h * RD:(h + 1) * RD], att_t[:, h * P:(h + 1) * P], start=True, stop=True)
                last.then_inc(S["ret_ps"], 1)

            def group_moments(T):
                pe.wait_ge(S["sums_out"], T.t + 1)
                mm(bank[3][:, 0:8], head_mean[:, :], sums[:, :], start=True, stop=True).then_inc(S["stat_ps"], 1)

            def shared_out(T, C):
                pe.wait_ge(S["sha_out"], T.t + 1)
                if C is not None:
                    pe.wait_ge(S["x2_out"], C.t + 1)
                past(pe, S["xall_out"], T.t)
                for j, (r0, rows) in enumerate(SHC):
                    last = mm(bank[7][:, 0:D], sh_a[0:rows, j, :], w_sd[0:rows, j, :], start=(j == 0), stop=(j == len(SHC) - 1))
                last.then_inc(S["shd_ps"], 1)

            def ret_out(T, L, C):
                pe.wait_ge(S["my_out"], T.t + 1)
                if L is not None:
                    pe.wait_ge(S["xall_out"], L.t + 1)
                elif C is not None:
                    pe.wait_ge(S["x2_out"], C.t + 1)
                past(pe, S["x1_out"], T.t)
                for k in range(KC):
                    last = mm(bank[7][:, 0:D], my[:, k, :], w_o[:, k, :], start=(k == 0), stop=(k == KC - 1))
                last.then_inc(S["wo_ps"], 1)

            def step(n, c):
                A, B, C, L = stage_tiles(n, c)
                if B:
                    if c >= 3:
                        past(pe, S["aT_sb"], C.t if C else NT)
                    if c < NT:
                        pe.wait_ge(S["xT1_sb"], B.t + 1)
                    turn(B, xn2, S["ln2_out"], S["xT2_ps"])
                    cross_in(B)
                if L:
                    if B:
                        pe.wait_ge(S["xT2_sb"], B.t + 1)
                    elif C:
                        pe.wait_ge(S["aT_sb"], C.t)
                    else:
                        pe.wait_ge(S["aT_sb"], NT)
                    turn(L, xn3[L.p], S["ln3_out"], S["xT3_ps"])
                    if A or c == NT:
                        prev = (S["gvar_out"], A.t if A else NT)
                    else:
                        prev = (S["rows_out"], L.t)
                    logits(L, prev)
                if A:
                    if L:
                        pe.wait_ge(S["xT3_sb"], L.t + 1)
                    elif B:
                        pe.wait_ge(S["xT2_sb"], B.t + 1)
                    turn(A, xn1, S["ln1_out"], S["xT1_ps"])
                    ret_in(A, L)
                if C:
                    if A:
                        pe.wait_ge(S["xT1_sb"], A.t + 1)
                    elif L:
                        pe.wait_ge(S["xT3_sb"], L.t + 1)
                    turn(C, attn_n, S["attnn_out"], S["aT_ps"])
                    if A:
                        past(pe, S["x1_out"], A.t)
                    elif L:
                        pe.wait_ge(S["x1_out"], NT)
                        pe.wait_ge(S["xall_out"], L.t)
                    cross_out(C)
                if L:
                    ranks(L)
                if A:
                    ret_scores(A, L)
                if L:
                    shared_in(L, A)
                if A:
                    retain(A, B)
                    group_moments(A)
                if L:
                    shared_out(L, C)
                if A:
                    ret_out(A, L, C)

            steps(pe, step)

            pe.wait_ge(S["expert_w0"], 2 * 16 * E)
            pe.wait_ge(S["xall_out"], NT)
            pe.wait_ge(S["tab_out"], 1)

            def e_turn(j, turn, b):
                p = b % 2
                pe.wait_ge(xe_in[b], 16 * (turn + 1))
                past(pe, S["eT_sb"], j - 1)
                for k in range(KC):
                    last = nc.tensor.transpose(bank[p][:, k * P:(k + 1) * P], xe[b][:, k * P:(k + 1) * P], ident[:, :])
                last.then_inc(S["eT_ps"], 1)

            def e_up(j, p):
                e = pe.value_load(table[0:1, 0, bass.ds(j, 1)], min_val=0, max_val=E - 1)
                pe.wait_ge(S["eT_sb"], j + 1)
                past(pe, S["ea_out"], j - 1)
                for k in range(KC):
                    last = mm(bank[2 + p][:, 0:2 * INNER], xeT[p][:, k, :],
                              w_gu[:, bass.ds(e, 1), k, :].rearrange("p e n -> p (e n)"), start=(k == 0), stop=(k == KC - 1))
                last.then_inc(S["egu_ps"], 1)

            def e_turn2(j, p):
                pe.wait_ge(S["ea_out"], j + 1)
                past(pe, S["eaT_sb"], j - 1)
                for k in range(2):
                    last = nc.tensor.transpose(bank[4 + p][0:HI, k * P:(k + 1) * P], ae[p][:, k * HI:(k + 1) * HI], ident[:, :])
                last.then_inc(S["eaT_ps"], 1)

            def e_down(j, p):
                e = pe.value_load(table[0:1, 0, bass.ds(j, 1)], min_val=0, max_val=E - 1)
                pe.wait_ge(S["eaT_sb"], j + 1)
                past(pe, S["ey_out"], j - 1)
                for k in range(2):
                    last = mm(bank[6 + p][:, 0:D], aeT[p][:, k, :],
                              w_d[:, bass.ds(e, 1), k, :].rearrange("p e n -> p (e n)"), start=(k == 0), stop=(k == 1))
                last.then_inc(S["ey_ps"], 1)

            def expert_step(n, j, b, first=False, turn=True, up=True):
                if up:
                    e_up(j + 1, (b + 1) % 2)
                if turn:
                    e_turn(j + 2, n + (b + 2) // XB, (b + 2) % XB)
                e_turn2(j, b % 2)
                if not first:
                    e_down(j - 1, (b + 1) % 2)

            e_turn(0, 0, 0)
            e_up(0, 0)
            e_turn(1, 0, 1)
            groups(pe, NET // XB - 1, lambda n, j, b: expert_step(n, j, b, first=type(j) is int and j == 0), XB)
            for b in range(XB):
                expert_step(NET // XB - 1, NET - XB + b, b, turn=b < XB - 2, up=b < XB - 1)
            e_down(NET - 1, 1)

        @block.vector
        def _(dve):
            v = nc.vector
            links = [0]

            def link(ins):
                links[0] += 1
                ins.then_inc(S["chain"], 1)
                dve.wait_ge(S["chain"], links[0])

            dve.wait_ge(S["tables_in"], 16 * 9)
            dve.wait_ge(S["bias_in"], 16)
            link(v.tensor_copy(bias_hi[:, :], bias3[:, :]))
            link(v.tensor_tensor(bias_r[:, :], bias3[:, :], bias_hi[:, :], ALU.subtract))
            link(v.tensor_copy(bias_mid[:, :], bias_r[:, :]))
            link(v.tensor_tensor(bias_r[:, :], bias_r[:, :], bias_mid[:, :], ALU.subtract))
            link(v.tensor_copy(bias_lo[:, :], bias_r[:, :]))
            link(v.tensor_scalar(bias_r[:, :], bias_hi[:, :], eye3[:, 0:1], None, ALU.mult))
            link(v.scalar_tensor_tensor(out=bias_r[:, :], in0=bias_mid[:, :], scalar=eye3[:, 1:2], in1=bias_r[:, :],
                                        op0=ALU.mult, op1=ALU.add))
            link(v.scalar_tensor_tensor(out=bias_parts[:, :], in0=bias_lo[:, :], scalar=eye3[:, 2:3], in1=bias_r[:, :],
                                        op0=ALU.mult, op1=ALU.add))
            link(v.tensor_copy(before[:, :], before_f[:, :]))
            link(v.memset(two[:, :], 2.0))
            dve.wait_ge(S["consts"], 1)
            link(v.tensor_copy(row_base[:, :], region0))
            v.memset(chosen[:, :], 0.0).then_inc(S["prep"], 1)
            link0 = links[0]
            ch = {k: sem(f"chain_{k}") for k in ("ln1", "ln2", "ln3", "gn", "top", "rows", "soft")}

            def ln_stats(s, src, done, name, T):
                c = ch[name]
                v.bn_stats(stats[s][:, :], src).then_inc(c, 1)
                alone(dve, c, 2 * T.t + 1)
                v.bn_aggr(mv[s][:, :], stats[s][:, :]).then_inc(c, 1)
                dve.wait_ge(c, 2 * T.t + 2)
                v.tensor_scalar(var_eps[s][:, :], mv[s][:, 1:2], EPS, None, ALU.add).then_inc(done, 1)

            def ln_out(s, src, dst, ready, done, T):
                dve.wait_ge(ready, T.t + 1)
                v.tensor_scalar(dst, src, mv[s][:, 0:1], rstd[s][:, 0:1], ALU.subtract, ALU.mult).then_inc(done, 1)

            def residual1(T):
                dve.wait_ge(S["wo_ps"], T.t + 1)
                v.tensor_tensor(x1[T.p][:, :], bank[7][:, 0:D], xin[T.p][:, :], ALU.add).then_inc(S["x1_out"], 1)
                dve.wait_ge(S["x1_out"], T.t + 1)
                ln_stats(1, x1[T.p][:, :], S["ln2_var"], "ln2", T)

            def q_prod(T, q):
                if q == 0:
                    dve.wait_ge(S["q_ps"], T.t + 1)
                    dve.wait_ge(S["kv_out"], T.t + 1)
                past(dve, S["score_out"], QCH * T.t + q - 1)
                qq = bank[5][:, q * QH * XD:(q + 1) * QH * XD].rearrange("p (h d) -> p h d", d=XD)
                kk = kv[T.p][:, 0:D].rearrange("p (g d) -> p g d", d=XD)
                v.tensor_tensor(prod[:, q % 2, :].rearrange("p (h g d) -> p h g d", h=QH, g=XH),
                                qq.unsqueeze(2).to_broadcast([P, QH, XH, XD]),
                                kk.unsqueeze(1).to_broadcast([P, QH, XH, XD]), ALU.mult).then_inc(S["prod_out"], 1)

            def q_sum(T, q):
                dve.wait_ge(S["prod_out"], QCH * T.t + q + 1)
                v.tensor_reduce(scores[:, q * QH * XH:(q + 1) * QH * XH],
                                prod[:, q % 2, :].rearrange("p (a d) -> p a d", d=XD), AX_X, ALU.add
                                ).then_inc(S["score_out"], 1)

            def soft_max(T):
                dve.wait_ge(S["score_out"], QCH * (T.t + 1))
                s3 = scores[:, :].rearrange("p (h g) -> p h g", g=XH)
                v.tensor_reduce(score_max[:, :], s3, AX_X, ALU.max).then_inc(ch["soft"], 1)
                dve.wait_ge(ch["soft"], T.t + 1)
                v.tensor_tensor(score_sub[:, :].rearrange("p (h g) -> p h g", g=XH), s3,
                                score_max[:, :].unsqueeze(2).to_broadcast([P, XH, XH]), ALU.subtract
                                ).then_inc(S["sub_out"], 1)

            def soft_sum(T):
                dve.wait_ge(S["prob_out"], T.t + 1)
                v.tensor_reduce(prob_sum[:, :], prob[T.p][:, :].rearrange("p (h g) -> p h g", g=XH), AX_X, ALU.add
                                ).then_inc(S["psum_out"], 1)
                dve.wait_ge(S["psum_out"], T.t + 1)
                v.reciprocal(prob_rec[T.p][:, :], prob_sum[:, :]).then_inc(S["prec_out"], 1)

            def a_sum(T, q):
                dve.wait_ge(S["av_out"], QCH * T.t + q + 1)
                v.tensor_reduce(attn[:, q * QH * XD:(q + 1) * QH * XD],
                                av[:, q % 2, :].rearrange("p (a g) -> p a g", g=XH), AX_X, ALU.add
                                ).then_inc(S["attn_out"], 1)

            def a_norm(T):
                dve.wait_ge(S["attn_out"], QCH * (T.t + 1))
                dve.wait_ge(S["prec_out"], T.t + 1)
                v.tensor_tensor(attn_n[:, :].rearrange("p (h d) -> p h d", d=XD),
                                attn[:, :].rearrange("p (h d) -> p h d", d=XD),
                                prob_rec[T.p][:, :].unsqueeze(2).to_broadcast([P, XH, XD]), ALU.mult
                                ).then_inc(S["attnn_out"], 1)

            def rotate(T):
                dve.wait_ge(S["qk_ps"], T.t + 1)
                past(dve, S["rot_out"], T.t)
                b3 = bank[1][:, :].rearrange("p (f t) -> p f t", f=4)
                v.tensor_tensor(cos_part[:, :, :], b3[:, 0:2, :], rot_tab[:, 0:2, :], ALU.mult)
                v.tensor_tensor(sin_part[:, :, :], b3[:, 2:4, :], rot_tab[:, 2:4, :], ALU.mult).then_inc(S["rot_parts"], 1)

            def gate_min(T):
                dve.wait_ge(S["g_ps"], T.t + 1)
                past(dve, S["eg_out"], T.t)
                v.tensor_scalar(gm[:, :], bank[4][:, 0:D], 18.0, None, ALU.min).then_inc(S["gm_out"], 1)

            def gate_n(T):
                dve.wait_ge(S["eg_out"], T.t + 1)
                past(dve, S["th_out"], T.t)
                v.scalar_tensor_tensor(out=n_g[:, :], in0=e_g[:, :], scalar=2.0, in1=e_g[:, :], op0=ALU.add,
                                       op1=ALU.mult).then_inc(S["ng_out"], 1)

            def gate_mish(T):
                dve.wait_ge(S["th_out"], T.t + 1)
                past(dve, S["my_out"], T.t)
                v.tensor_tensor(mish[:, :], bank[4][:, 0:D], th_g[:, :], ALU.mult).then_inc(S["mish_out"], 1)

            def decay(T):
                dve.wait_ge(S["sc_ps"], T.t + 1)
                v.tensor_tensor(att_t[:, :], bank[3][:, :], decay_tab[:, :], ALU.mult).then_inc(S["att_out"], 1)

            def ret_sums(T):
                dve.wait_ge(S["sq_out"], T.t + 1)
                v.tensor_reduce(sums[:, 0:4], bank[6][:, 0:D].rearrange("p (a s) -> p a s", s=SEQ), AX_X, ALU.add)
                v.tensor_reduce(sums[:, 4:8], ret_sq[:, :].rearrange("p (a s) -> p a s", s=SEQ), AX_X, ALU.add
                                ).then_inc(S["sums_out"], 1)

            def ret_var(T):
                c = ch["gn"]
                dve.wait_ge(S["stat_ps"], T.t + 1)
                past(dve, S["gaff_out"], T.t)
                v.tensor_copy(moments[:, :], bank[3][:, 0:8]).then_inc(c, 1)
                dve.wait_ge(c, 2 * T.t + 1)
                v.scalar_tensor_tensor(out=neg_msq[:, :], in0=moments[:, 0:4], scalar=-1.0, in1=moments[:, 0:4],
                                       op0=ALU.mult, op1=ALU.mult).then_inc(c, 1)
                dve.wait_ge(c, 2 * T.t + 2)
                v.scalar_tensor_tensor(out=gvar[:, :], in0=moments[:, 4:8], scalar=EPS, in1=neg_msq[:, :],
                                       op0=ALU.add, op1=ALU.add).then_inc(S["gvar_out"], 1)

            def residual2(T):
                dve.wait_ge(S["xo_ps"], T.t + 1)
                v.tensor_tensor(x2[T.p][:, :], bank[7][:, 0:D], x1[T.p][:, :], ALU.add).then_inc(S["x2_out"], 1)

            def ln3_in(T):
                dve.wait_ge(S["x2_out"], T.t + 1)
                ln_stats(2, x2[T.p][:, :], S["ln3_var"], "ln3", T)

            def route_max(T):
                dve.wait_ge(S["logit_ps"], T.t + 1)
                v.tensor_reduce(neg_max[:, :], bank[3][:, 0:E], AX_X, ALU.max, negate=True).then_inc(S["lmax_out"], 1)

            def route_top(T):
                c = ch["top"]
                dve.wait_ge(S["expl_out"], T.t + 1)
                v.reciprocal(rec_l[:, :], sum_l[:, :]).then_inc(c, 1)
                dve.wait_ge(c, 8 * T.t + 1)
                v.tensor_scalar(prob_l[:, :], exp_l[:, :], rec_l[:, 0:1], None, ALU.mult).then_inc(c, 1)
                alone(dve, c, 8 * T.t + 2)
                v.max(top8[:, :], prob_l[:, :]).then_inc(c, 1)
                alone(dve, c, 8 * T.t + 3)
                v.max_index(idx8[:, :], top8[:, :], prob_l[:, :]).then_inc(c, 1)
                alone(dve, c, 8 * T.t + 4)
                v.tensor_copy(wt_all[:, bass.ds(T.t, 1), :].rearrange("p a k -> p (a k)"), top8[:, 0:TOPK]).then_inc(c, 1)
                v.tensor_copy(idx_f[:, :], idx8[:, 0:TOPK]).then_inc(c, 1)
                alone(dve, c, 8 * T.t + 6)
                v.tensor_copy(pick_all[:, bass.ds(T.t, 1), :].rearrange("p a k -> p (a k)"), idx_f[:, :]).then_inc(c, 1)
                v.tensor_tensor(pick[:, :, :], expert_no.unsqueeze(1).to_broadcast([P, TOPK, E]),
                                idx_f[:, :].unsqueeze(2).to_broadcast([P, TOPK, E]), ALU.is_equal).then_inc(c, 1)
                dve.wait_ge(c, 8 * T.t + 8)
                with nc.allow_low_precision(reason="zeros and ones"):
                    v.tensor_reduce(chosen[:, :], pick[:, :, :].rearrange("p k e -> p e k"), AX_X, ALU.add
                                    ).then_inc(S["chosen_out"], 1)

            def route_rows(T):
                c = ch["rows"]
                dve.wait_ge(S["rank_ps"], T.t + 1)
                v.tensor_tensor(row_of[:, :], bank[3][:, 0:E], row_base[:, :], ALU.add).then_inc(c, 1)
                dve.wait_ge(c, 5 * T.t + 1)
                v.tensor_tensor(row_base[:, :], bank[3][:, E:2 * E], row_base[:, :], ALU.add).then_inc(c, 1)
                v.tensor_tensor(pick_row[:, :, :], pick[:, :, :], row_of[:, :].unsqueeze(1).to_broadcast([P, TOPK, E]),
                                ALU.mult).then_inc(c, 1)
                dve.wait_ge(c, 5 * T.t + 3)
                v.tensor_reduce(row_f[:, :], pick_row[:, :, :], AX_X, ALU.add).then_inc(c, 1)
                past(dve, scat_done[T.p], 16 * TOPK * T.half)
                dve.wait_ge(c, 5 * T.t + 4)
                v.tensor_copy(row_u[T.p][:, :], row_f[:, :])
                v.tensor_copy(row_all[:, bass.ds(T.t, 1), :].rearrange("p a k -> p (a k)"), row_f[:, :]).then_inc(c, 1)
                dve.wait_ge(c, 5 * T.t + 5)
                v.engine_nop().then_inc(S["rows_out"], 1) if False else v.tensor_copy(row_f[:, :], row_f[:, :]).then_inc(S["rows_out"], 1)

            def shared_mul(T):
                dve.wait_ge(S["shs_out"], T.t + 1)
                dve.wait_ge(S["su_ps"], T.t + 1)
                v.tensor_tensor(sh_a[:, 0:2, :], bank[2][:, 0:2 * P].rearrange("p (a b) -> p a b", a=2), sh_s[:, 0:2, :], ALU.mult)
                v.tensor_tensor(sh_a[0:96, 2, :], bank[2][0:96, 2 * P:3 * P], sh_s[0:96, 2, :], ALU.mult
                                ).then_inc(S["sha_out"], 1)

            def residual3(T):
                dve.wait_ge(S["shd_ps"], T.t + 1)
                past(dve, x3_done[T.p], 16 * T.half)
                v.tensor_tensor(x3[T.p][:, :], bank[7][:, 0:D], x2[T.p][:, :], ALU.add).then_inc(S["xall_out"], 1)

            def step(n, c):
                A, B, C, L = stage_tiles(n, c)
                if L:
                    ln3_in(L)
                if A:
                    alone(dve, xin_in[A.p], 16 * (A.half + 1))
                    ln_stats(0, xin[A.p][:, :], S["ln1_var"], "ln1", A)
                if C:
                    a_sum(C, 0)
                if B:
                    residual1(B)
                if L:
                    past(dve, scat_done[L.p], 16 * TOPK * L.half)
                    ln_out(2, x2[L.p][:, :], xn3[L.p][:, :], S["ln3_rstd"], S["ln3_out"], L)
                if A:
                    ln_out(0, xin[A.p][:, :], xn1[:, :], S["ln1_rstd"], S["ln1_out"], A)
                if B:
                    ln_out(1, x1[B.p][:, :], xn2[:, :], S["ln2_rstd"], S["ln2_out"], B)
                if C:
                    a_sum(C, 1)
                    a_sum(C, 2)
                if L:
                    route_max(L)
                if B:
                    q_prod(B, 0)
                if L:
                    route_top(L)
                if B:
                    q_prod(B, 1)
                if A:
                    rotate(A)
                    gate_min(A)
                if C:
                    a_sum(C, 3)
                    a_norm(C)
                if B:
                    q_sum(B, 0)
                if L:
                    route_rows(L)
                if A:
                    gate_n(A)
                if B:
                    q_sum(B, 1)
                    q_prod(B, 2)
                if A:
                    decay(A)
                if C:
                    residual2(C)
                if B:
                    q_prod(B, 3)
                if L:
                    shared_mul(L)
                if B:
                    q_sum(B, 2)
                if A:
                    ret_sums(A)
                if B:
                    q_sum(B, 3)
                    soft_max(B)
                if L:
                    residual3(L)
                if A:
                    ret_var(A)
                if B:
                    soft_sum(B)
                if A:
                    gate_mish(A)

            steps(dve, step)

            def all_of(c):
                dve.wait_ge(c[0], c[1])

            dve.wait_ge(ch["rows"], 5 * NT)
            link(v.tensor_tensor(cnt[:, 0:E], row_base[:, :], region0, ALU.subtract))
            link(v.memset(cnt[:, E:E + 1], 0.0))
            link(v.tensor_copy(tail_i[0:1, :], row_base[0:1, :]))
            link(v.tensor_scalar(cnt[:, :], cnt[:, :], float(P - 1), None, ALU.add))
            link(v.tensor_copy(cnt_i[:, :], cnt[:, :]))
            link(v.tensor_scalar(cnt_i[:, :], cnt_i[:, :], 7, None, ALU.arith_shift_right))
            link(v.tensor_copy(cnt[:, :], cnt_i[:, :]))
            link(v.memset(row0[:, :], 1.0))
            link(v.tensor_tensor_scan(cum[:, :], row0[:, :], cnt[:, :], 0.0, ALU.mult, ALU.add))
            link(v.tensor_tensor(cnt[:, :], cum[:, :], cnt[:, :], ALU.subtract))
            link(v.tensor_scalar(row0[:, :], small[:, 40:40 + NX], float(REG), None, ALU.mult))
            link(v.scalar_tensor_tensor(out=row0[:, :], in0=cnt[:, :], scalar=float(-P), in1=row0[:, :], op0=ALU.mult,
                                        op1=ALU.add))
            link(v.memset(e_of[:, :], 0.0))
            for e in range(E):
                link(v.scalar_tensor_tensor(out=e_of[:, :], in0=tile_no[:, :], scalar=cum[:, e:e + 1], in1=e_of[:, :],
                                            op0=ALU.is_ge, op1=ALU.add))
            link(v.tensor_scalar(base_f[:, :], tile_no[:, :], float(P), None, ALU.mult))
            for e in range(NX):
                link(v.tensor_scalar(tile_tmp[:, :], e_of[:, :], float(e), row0[:, e:e + 1], ALU.is_equal, ALU.mult))
                link(v.tensor_tensor(base_f[:, :], base_f[:, :], tile_tmp[:, :], ALU.add))
            link(v.tensor_scalar(e_of[:, :], e_of[:, :], float(E - 1), None, ALU.min))
            link(v.tensor_copy(table[0:1, 0, :], e_of[0:1, :]))
            v.tensor_copy(table[0:1, 1, :], base_f[0:1, :]).then_inc(S["tab_out"], 1)

            def e_mul(j, p):
                dve.wait_ge(S["eh_out"], j + 1)
                past(dve, S["eaT_ps"], j - 1)
                v.tensor_tensor(ae[p], bank[2 + p][:, INNER:2 * INNER], he[p], ALU.mult).then_inc(S["ea_out"], 1)

            def e_turned(j, p):
                dve.wait_ge(S["eaT_ps"], j + 1)
                past(dve, S["ey_ps"], j - 1)
                v.tensor_copy(aeT[p].rearrange("p a b -> p (a b)"), bank[4 + p][0:HI, 0:D]).then_inc(S["eaT_sb"], 1)

            e_mul(0, 0)

            def expert_step(n, j, p):
                e_turned(j, p)
                e_mul(j + 1, 1 - p)

            groups(dve, (NET - 2) // 2, expert_step)
            e_turned(NET - 2, 0)
            e_mul(NET - 1, 1)
            e_turned(NET - 1, 1)

            def indices(t, half, p):
                past(dve, gath_done[p], 16 * TOPK * half)
                v.tensor_copy(idx_g[p][:, :], row_all[:, bass.ds(t, 1), :].rearrange("p a k -> p (a k)")
                              ).then_inc(S["idxg_out"], 1)

            def combine(t, half, p):
                dve.wait_ge(gath_done[p], 16 * TOPK * (half + 1))
                past(dve, out_done[p], 16 * half)
                dve.wait_ge(x3_in[p], 16 * (half + 1))
                for k in range(TOPK):
                    ins = v.scalar_tensor_tensor(
                        out=acc[p][:, :], in0=yg[p][k], scalar=wt_all[:, bass.ds(t, 1), k:k + 1].rearrange("p a k -> p (a k)"),
                        in1=x3[p][:, :] if k == 0 else acc[p][:, :], op0=ALU.mult, op1=ALU.add)
                    if k < TOPK - 1:
                        ins.then_inc(ch["fin"], 1)
                        dve.wait_ge(ch["fin"], (TOPK - 1) * t + k + 1)
                    else:
                        ins.then_inc(S["fin_out"], 1)

            ch["fin"] = sem("chain_fin")
            dve.wait_ge(ye_done[0], 16 * NET // 2)
            dve.wait_ge(ye_done[1], 16 * NET // 2)
            dve.wait_ge(S["shift_out"], 2 * E)
            indices(0, 0, 0)

            def out_step(n, t, p):
                indices(t + 1, n + p, 1 - p)
                combine(t, n, p)

            groups(dve, NT // 2 - 1, out_step)
            indices(NT - 1, NT // 2 - 1, 1)
            combine(NT - 2, NT // 2 - 1, 0)
            combine(NT - 1, NT // 2 - 1, 1)


def layouts(x, ctx_2048, L0_attn_wqkv, L0_attn_wg, L0_attn_wo, L0_attn_gn_weight, L0_attn_gn_bias, L0_xattn_Wq,
            L0_xattn_bq, L0_xattn_Wk, L0_xattn_bk, L0_xattn_Wv, L0_xattn_bv, L0_xattn_Wo, L0_xattn_bo, L0_ffn_w_gate,
            L0_ffn_wg, L0_ffn_wu, L0_ffn_wd, L0_ffn_sg, L0_ffn_su, L0_ffn_sd):
    def chunks(w):
        return w.reshape(KC, P, -1).transpose(1, 0, 2).reshape(P, -1)

    a = {}
    a["x"] = x.reshape(TOKENS, D)
    a["ctx_t"] = ctx_2048.reshape(NT, P, KC, P).transpose(0, 3, 2, 1).reshape(NT * P, KC * P)
    w = L0_attn_wqkv.reshape(RH, 3, RD, D)
    q, k, v = w[:, 0], w[:, 1], w[:, 2]

    def turned(r):
        return r.reshape(RH, ROT // 2, 2, D)[:, :, ::-1, :].reshape(RH, ROT, D)

    six = [q[:, :ROT], k[:, :ROT], turned(q[:, :ROT]), turned(k[:, :ROT]), q[:, ROT:], k[:, ROT:]]
    six = np.stack([s.reshape(P, D) for s in six])
    a["w_qk"] = six.reshape(6, P, KC, P).transpose(3, 2, 0, 1).reshape(P, -1)
    a["w_v"] = chunks(v.reshape(D, D).T)
    a["w_g"] = chunks(L0_attn_wg.T)
    a["w_o"] = chunks(L0_attn_wo.T)
    for name, g in (("gn_w", L0_attn_gn_weight), ("gn_b", L0_attn_gn_bias)):
        a[name] = np.repeat(np.repeat(g.reshape(2, 2).T, RD, axis=0), 2, axis=1)
    a["w_xq"] = chunks(L0_xattn_Wq.T)
    a["w_xkv"] = chunks(np.concatenate([L0_xattn_Wk.T, L0_xattn_Wv.T], axis=1))
    a["w_xo"] = chunks(L0_xattn_Wo.T)
    a["bias"] = np.concatenate([L0_xattn_bq, L0_xattn_bk, L0_xattn_bv, L0_xattn_bo])
    a["w_route"] = chunks(L0_ffn_w_gate.T)
    a["w_sg"], a["w_su"], a["w_sd"] = chunks(L0_ffn_sg), chunks(L0_ffn_su), L0_ffn_sd
    gu = np.concatenate([L0_ffn_wg, L0_ffn_wu], axis=2)
    a["w_gu"] = gu.reshape(E, KC, P, 2 * INNER).transpose(0, 2, 1, 3).reshape(E * P, -1)
    a["w_d"] = L0_ffn_wd.reshape(E, 2, HI, D).transpose(0, 2, 1, 3).reshape(E * HI, -1)
    return a


def kernel(**inputs):
    import concourse.bacc as bacc
    from concourse.bass_utils import run_bass_kernel_spmd

    nc = bacc.Bacc("TRN2", target_bir_lowering=False, num_devices=1)
    arrays = layouts(**{k: np.asarray(a) for k, a in inputs.items()})
    arrays.update(constants())
    arrays = {k: np.ascontiguousarray(a) for k, a in arrays.items()}
    io = {k: nc.dram_tensor(f"in_{k}", a.shape, mybir.dt.from_np(a.dtype), kind="ExternalInput").ap() for k, a in arrays.items()}
    out = nc.dram_tensor("out_x", (TOKENS, D), F32, kind="ExternalOutput").ap()
    scratch = [nc.dram_tensor(n, (rows, D), F32, kind="Internal").ap()
               for n, rows in (("expert_rows", ROWS), ("expert_out", NET * P), ("residual", TOKENS))]
    build(nc, io, out, scratch)
    r = run_bass_kernel_spmd(nc, [{f"in_{k}": a for k, a in arrays.items()}], core_ids=[0])
    return r.results[0]["out_x"].reshape(BATCH, SEQ, D)
```

```python
from collections import namedtuple
from contextlib import ExitStack

import numpy as np

import concourse.bass as bass
from concourse import mybir

F32 = mybir.dt.float32
BF16 = mybir.dt.bfloat16
I32 = mybir.dt.int32
U32 = mybir.dt.uint32
ALU = mybir.AluOpType
ACT = mybir.ActivationFunctionType
AX_X = mybir.AxisListType.X

P = 128
BATCH, SEQ, D = 64, 64, 256
TOKENS = BATCH * SEQ
NT = TOKENS // P
KC = D // P
RH, RD = 4, 64
ROT = RD // 2
XH, XD = 16, 16
E, TOPK, INNER = 16, 4, 176
HI = INNER // 2
SH = 2 * INNER
SHC = [(0, 128), (128, 128), (256, 96)]
EPS = 1e-5

XB = 4
REG = TOKENS + P
NET = TOKENS * TOPK // P + E
SPARE = NET - TOKENS * TOPK // P
ROWS = E * REG + SPARE * P

QCH = 4
QH = XH // QCH
CH = QH * XH * XD

STAGES = 5
LOOP0 = 6
LOOPS = (NT - 1 - LOOP0) // 2

Tile = namedtuple("Tile", "t half p")


def tile_at(n, c):
    return Tile(2 * n + c, n + c // 2, c % 2)


def constants():
    f = np.float32
    inv = f(1.0) / f(10000.0) ** (np.arange(0, ROT, 2, dtype=f) / f(ROT))
    t = np.arange(SEQ, dtype=f)
    freqs = np.repeat(t[:, None] * inv[None, :], 2, axis=-1)
    base = (np.arange(0, ROT, 2, dtype=f) + f(0.4 * ROT)) / f(1.4 * ROT)
    scale = base[None, :] ** ((t - SEQ // 2) / f(512.0))[:, None]
    scale = np.concatenate([scale, scale], axis=-1)
    cos, sin = np.cos(freqs).T, np.sin(freqs).T
    sign = np.where(np.arange(ROT) % 2 == 0, f(-1), f(1))[:, None]
    sc = scale.T
    rot = np.stack([cos * sc, cos / sc, sign * sin * sc, sign * sin / sc], axis=1)
    rot = np.tile(rot, (RH, 1, P // SEQ)).astype(f)
    gamma = f(1.0) - f(2.0) ** (f(-5.0) - np.arange(RH, dtype=f))
    j, i = np.arange(P)[:, None], np.arange(P)[None, :]
    lag = i - j
    own = (i // SEQ == j // SEQ) & (lag >= 0)
    decay = np.stack([np.where(own, g ** np.maximum(lag, 0).astype(f), f(0)) for g in gamma], axis=1)
    c = {}
    c["rot_tab"] = rot.reshape(P, 4 * P)
    c["decay_tab"] = decay.astype(f).reshape(P, RH * P)
    c["ident"] = np.eye(P, dtype=f)
    c["head_mean"] = np.where(i // RD == j // RD, f(1.0 / (RD * SEQ)), f(0)).astype(f)
    c["before"] = np.where(j < i, f(1), f(0)).astype(f)
    small = np.zeros((P, 64), f)
    small[:, 0:16] = np.arange(E)
    small[:, 16:32] = np.arange(E) * REG
    small[:, 32:36] = -0.5
    small[0:3, 36:39] = np.eye(3)
    small[:, 40:57] = np.arange(E + 1)
    c["small_tab"] = small
    c["tile_row"] = np.tile(np.arange(NET, dtype=f)[None, :], (P, 1))
    return c


def build(nc, io, out, scratch):
    with ExitStack() as ctx:
        def sb(name, shape, dt=F32):
            return ctx.enter_context(nc.sbuf_tensor(name, shape, dt))

        def sem(name):
            return ctx.enter_context(nc.semaphore(name))

        w_qk = sb("w_qk", [P, KC, 6, P])
        w_v = sb("w_v", [P, KC, D])
        w_g = sb("w_g", [P, KC, D])
        w_o = sb("w_o", [P, KC, D])
        w_xq = sb("w_xq", [P, KC, D])
        w_xkv = sb("w_xkv", [P, KC, 2 * D])
        w_xo = sb("w_xo", [P, KC, D])
        w_route = sb("w_route", [P, KC, E])
        w_sg = sb("w_sg", [P, KC, SH])
        w_su = sb("w_su", [P, KC, SH])
        w_sd = sb("w_sd", [P, len(SHC), D])
        w_gu = sb("w_gu", [P, E, KC, 2 * INNER])
        w_d = sb("w_d", [HI, E, 2, D])
        rot_tab = sb("rot_tab", [P, 4, P])
        decay_tab = sb("decay_tab", [P, RH * P])
        ident = sb("ident", [P, P])
        head_mean = sb("head_mean", [P, P])
        before_f = sb("before_f", [P, P])
        before = sb("before", [P, P], BF16)
        ones = sb("ones", [P, P], BF16)
        small = sb("small", [P, 64])
        expert_no, region0, minus_half, eye3 = small[:, 0:16], small[:, 16:32], small[:, 32:36], small[0:3, 36:39]
        gn_w = sb("gn_w", [P, 4])
        gn_b = sb("gn_b", [P, 4])
        bias3 = sb("bias3", [3, 4 * D])
        bias_hi = sb("bias_hi", [3, 4 * D], BF16)
        bias_mid = sb("bias_mid", [3, 4 * D], BF16)
        bias_lo = sb("bias_lo", [3, 4 * D], BF16)
        bias_r = sb("bias_r", [3, 4 * D])
        bias_parts = sb("bias_parts", [3, 4 * D], BF16)

        def pair(name, shape, dt=F32):
            return [sb(f"{name}{p}", shape, dt) for p in range(2)]

        xin = pair("xin", [P, D])
        ctx_t = pair("ctx_t", [P, KC, P])
        x1 = pair("x1", [P, D])
        x2 = pair("x2", [P, D])
        xn1 = sb("xn1", [P, D])
        xn2 = sb("xn2", [P, D])
        xn3 = pair("xn3", [P, D])
        stats = [sb(f"stats{s}", [P, 6]) for s in range(3)]
        mv = [sb(f"mv{s}", [P, 2]) for s in range(3)]
        var_eps = [sb(f"var_eps{s}", [P, 1]) for s in range(3)]
        rstd = [sb(f"rstd{s}", [P, 1]) for s in range(3)]
        xT1 = sb("xT1", [P, KC, P])
        xT2 = sb("xT2", [P, KC, P])
        xT3 = sb("xT3", [P, KC, P])
        cos_part = sb("cos_part", [P, 2, P])
        sin_part = sb("sin_part", [P, 2, P])
        qk_rot = sb("qk_rot", [P, 2, P])
        k_pass = sb("k_pass", [P, P])
        q_rot = sb("q_rot", [P, RH, P])
        q_pass = sb("q_pass", [P, RH, P])
        v_sb = sb("v_sb", [P, D])
        att_t = sb("att_t", [P, RH * P])
        ret_sq = sb("ret_sq", [P, D])
        sums = sb("sums", [P, 8])
        moments = sb("moments", [P, 8])
        neg_msq = sb("neg_msq", [P, 4])
        gvar = sb("gvar", [P, 4])
        grstd = sb("grstd", [P, 4])
        gscale = sb("gscale", [P, 4])
        gshift = sb("gshift", [P, 4])
        gm = sb("gm", [P, D])
        e_g = sb("e_g", [P, D])
        n_g = sb("n_g", [P, D])
        ln_g = sb("ln_g", [P, D])
        rec_g = sb("rec_g", [P, D])
        th_g = sb("th_g", [P, D])
        mish = sb("mish", [P, D])
        y_sb = sb("y_sb", [P, KC, P])
        my = sb("my", [P, KC, P])
        kv = pair("kv", [P, 2 * D])
        prod = sb("prod", [P, 2, CH])
        scores = sb("scores", [P, XH * XH])
        score_max = sb("score_max", [P, XH])
        score_sub = sb("score_sub", [P, XH * XH])
        prob = pair("prob", [P, XH * XH])
        prob_sum = sb("prob_sum", [P, XH])
        prob_rec = pair("prob_rec", [P, XH])
        av = sb("av", [P, 2, CH])
        attn = sb("attn", [P, D])
        attn_n = sb("attn_n", [P, D])
        attn_t = sb("attn_t", [P, KC, P])
        neg_max = sb("neg_max", [P, 1])
        exp_l = sb("exp_l", [P, E])
        sum_l = sb("sum_l", [P, 1])
        rec_l = sb("rec_l", [P, 1])
        prob_l = sb("prob_l", [P, E])
        top8 = sb("top8", [P, 8])
        idx8 = sb("idx8", [P, 8], U32)
        idx_f = sb("idx_f", [P, TOPK])
        pick = sb("pick", [P, TOPK, E])
        chosen = sb("chosen", [P, E], BF16)
        row_base = sb("row_base", [P, E])
        row_of = sb("row_of", [P, E])
        pick_row = sb("pick_row", [P, TOPK, E])
        row_f = sb("row_f", [P, TOPK])
        row_u = pair("row_u", [P, TOPK], U32)
        sh_s = sb("sh_s", [P, len(SHC), P])
        sh_a = sb("sh_a", [P, len(SHC), P])
        x3 = pair("x3", [P, D])
        row_all = sb("row_all", [P, NT, TOPK])
        pick_all = sb("pick_all", [P, NT, TOPK])
        shift = sb("shift", [P, NT, TOPK])
        wt_all = sb("wt_all", [P, NT, TOPK])

        NX = E + 1
        zeros = sb("zeros", [P, D])
        cnt = sb("cnt", [P, NX])
        cnt_i = sb("cnt_i", [P, NX], I32)
        cum = sb("cum", [P, NX])
        tile_no = sb("tile_no", [P, NET])
        row0 = sb("row0", [P, NX])
        e_of = sb("e_of", [P, NET])
        base_f = sb("base_f", [P, NET])
        table = sb("table", [1, 2, NET], I32)
        tail_i = sb("tail_i", [1, E], I32)

        def carve(t, q, cols):
            return t[:, q * cols // CH, (q * cols) % CH:(q * cols) % CH + cols]

        xe = [carve(prod, q, D) for q in range(XB)]
        xeT = [carve(prod, 4 + q, D).rearrange("p (k t) -> p k t", k=KC) for q in range(2)]
        he = [carve(prod, 6 + q, D)[:, 0:INNER] for q in range(2)]
        ae = [carve(av, q, D)[:, 0:INNER] for q in range(2)]
        aeT = [carve(av, 2 + q, D)[0:HI].rearrange("p (k t) -> p k t", k=KC) for q in range(2)]
        ye = [carve(av, 4 + q, D) for q in range(2)]
        yg = [[carve(prod, k, D) for k in range(TOPK)], [carve(av, k, D) for k in range(TOPK)]]
        idx_g = row_u
        acc = pair("acc", [P, D])
        tile_tmp = sb("tile_tmp", [P, NET])
        two = sb("two", [P, 1])



        bank = [ctx.enter_context(nc.psum_tensor(f"bank{b}", [P, 512], F32)) for b in range(8)]

        names = """passed tables_in weights_in bias_in consts prep
            ln1_var ln1_rstd ln1_out ln2_var ln2_rstd ln2_out ln3_var ln3_rstd ln3_out
            xT1_ps xT1_sb xT2_ps xT2_sb xT3_ps xT3_sb
            qk_ps pv_ps g_ps rot_parts rot_out qrot_out pass_out v_out sc_ps att_out ret_ps sq_out sums_out stat_ps
            gvar_out gaff_out y_out gm_out eg_out ng_out rec_out th_out mish_out my_out wo_ps x1_out
            q_ps kv_ps kv_out prod_out score_out sub_out prob_out psum_out prec_out
            av_out attn_out attnn_out aT_ps aT_sb xo_ps x2_out
            logit_ps expl_out lmax_out top_out chosen_out rank_ps rows_out
            sg_ps su_ps shs_out sha_out shd_ps xall_out chain pchain achain
            expert_w0 shift_out tab_out zero_in fill_out
            eT_ps eT_sb egu_ps eh_out ea_out eaT_ps eaT_sb ey_ps ey_out idxg_out fin_out""".split()
        S = {n: sem(n) for n in names}
        xin_in = [sem(f"xin_in{p}") for p in range(2)]
        ctx_in = [sem(f"ctx_in{p}") for p in range(2)]
        scat_done = [sem(f"scat_done{p}") for p in range(2)]
        xe_in = [sem(f"xe_in{b}") for b in range(XB)]
        ye_done = [sem(f"ye_done{p}") for p in range(2)]
        gath_done = [sem(f"gath_done{p}") for p in range(2)]
        out_done = [sem(f"out_done{p}") for p in range(2)]
        x3_done = [sem(f"x3_done{p}") for p in range(2)]
        x3_in = [sem(f"x3_in{p}") for p in range(2)]

        rows_dram, y_dram, x3_dram = scratch

        def steps(eng, body):
            for c in range(LOOP0):
                body(0, c)
            with eng.Fori(0, LOOPS) as n:
                for u in range(2):
                    body(n, LOOP0 + u)
            for c in range(LOOP0 + 2 * LOOPS, NT + STAGES - 1):
                body(0, c)

        def stage_tiles(n, c):
            peeled = type(n) is int
            return [tile_at(n, c - s) if not peeled or 0 <= c - s < NT else None for s in range(STAGES)]

        def through(n, c, s):
            t = tile_at(n, c - s).t + 1
            return min(max(t, 0), NT) if type(n) is int else t

        def at(T, op, *more):
            if T:
                op(T, *more)

        def past(eng, s, v):
            if type(v) is int and v <= 0:
                return
            eng.wait_ge(s, v)

        def alone(eng, s, v):
            if type(v) is int and v <= 0:
                return
            eng.wait_ge(s, v)
            eng.sem_inc(S["passed"], 1)

        def groups(eng, count, body, size=2):
            for u in range(size):
                body(0, u, u)
            with eng.Fori(1, count) as n:
                for u in range(size):
                    body(n, size * n + u, u)

        block = ctx.enter_context(nc.Block())

        @block.sync
        def _(sp):
            for dst, src in ((rot_tab[:, :, :].rearrange("p a b -> p (a b)"), "rot_tab"), (decay_tab[:, :], "decay_tab"),
                             (ident[:, :], "ident"), (head_mean[:, :], "head_mean"), (before_f[:, :], "before"),
                             (small[:, :], "small_tab"), (tile_no[:, :], "tile_row"), (gn_w[:, :], "gn_w"), (gn_b[:, :], "gn_b")):
                sp.dma_start(dst, io[src]).then_inc(S["tables_in"], 16)
            sp.dma_start(bias3[:, :], io["bias"].partition_broadcast(3)).then_inc(S["bias_in"], 16)

            def flat(t):
                return t.rearrange("p a b -> p (a b)")

            sp.dma_start(w_qk[:, :, :, :].rearrange("p a b c -> p (a b c)"), io["w_qk"]).then_inc(S["weights_in"], 16)
            for dst, src in ((w_v, "w_v"), (w_g, "w_g"), (w_o, "w_o"), (w_xq, "w_xq"), (w_xkv, "w_xkv"), (w_xo, "w_xo"),
                             (w_route, "w_route"), (w_sg, "w_sg"), (w_su, "w_su")):
                sp.dma_start(flat(dst[:, :, :]), io[src]).then_inc(S["weights_in"], 16)
            for j, (r0, rows) in enumerate(SHC):
                sp.dma_start(w_sd[0:rows, j, :], io["w_sd"][r0:r0 + rows, :]).then_inc(S["weights_in"], 16)

            def load_x(T):
                past(sp, S["x1_out"], T.t - 1)
                sp.dma_start(xin[T.p][:, :], io["x"][bass.ds(T.t * P, P), :]).then_inc(xin_in[T.p], 16)

            def load_ctx(T):
                past(sp, S["kv_ps"], T.t - 1)
                sp.dma_start(ctx_t[T.p][:, :, :].rearrange("p a b -> p (a b)"),
                             io["ctx_t"][bass.ds(T.t * P, P), :]).then_inc(ctx_in[T.p], 16)

            def load_expert(e):
                sp.dma_start(w_gu[:, bass.ds(e, 1), :, :].rearrange("p e k n -> p (e k n)"),
                             io["w_gu"][bass.ds(e * P, P), :]).then_inc(S["expert_w0"], 16)
                sp.dma_start(w_d[:, bass.ds(e, 1), :, :].rearrange("p e k n -> p (e k n)"),
                             io["w_d"][bass.ds(e * HI, HI), :]).then_inc(S["expert_w0"], 16)

            def store_x3(T):
                sp.wait_ge(S["xall_out"], T.t + 1)
                sp.dma_start(x3_dram[bass.ds(T.t * P, P), :], x3[T.p][:, :]).then_inc(x3_done[T.p], 16)

            def step(n, c):
                peeled = type(n) is int
                T = stage_tiles(n, c)
                if not peeled or c + 1 < NT:
                    load_x(tile_at(n, c + 1))
                at(T[0], load_ctx)
                at(T[4], store_x3)
                if not peeled and c == LOOP0:
                    load_expert(n)
                if peeled and LOOPS <= c - LOOP0 - 2 * LOOPS + LOOPS < E:
                    load_expert(c - LOOP0 - LOOPS)

            load_x(tile_at(0, 0))
            steps(sp, step)

            for p in range(2):
                sp.wait_ge(scat_done[p], 16 * TOPK * NT // 2)
                sp.wait_ge(x3_done[p], 16 * NT // 2)
            sp.wait_ge(S["tab_out"], 1)
            for e in range(E):
                r = sp.value_load(tail_i[0:1, e:e + 1], min_val=0, max_val=ROWS - P)
                sp.dma_start(rows_dram[bass.ds(r, P), :], zeros[:, :]).then_inc(S["fill_out"], 16)
            for j in range(SPARE):
                sp.dma_start(rows_dram[E * REG + j * P:E * REG + (j + 1) * P, :], zeros[:, :]).then_inc(S["fill_out"], 16)
            sp.wait_ge(S["fill_out"], 16 * (E + SPARE))

            def load_rows(j, turn, b):
                past(sp, S["eT_ps"], j - XB + 1)
                r = sp.value_load(table[0:1, 1, bass.ds(j, 1)], min_val=0, max_val=ROWS - P)
                sp.dma_start(xe[b], rows_dram[bass.ds(r, P), :]).then_inc(xe_in[b], 16)

            def store_rows(j, p):
                sp.wait_ge(S["ey_out"], j + 1)
                sp.dma_start(y_dram[bass.ds(j * P, P), :], ye[p]).then_inc(ye_done[p], 16)

            for j in range(XB):
                load_rows(j, 0, j)

            def row_step(n, j, b):
                load_rows(j + XB, n + 1, b)
                store_rows(j, b % 2)

            groups(sp, NET // XB - 1, row_step, XB)
            for j in range(NET - XB, NET):
                store_rows(j, j % 2)
            for p in range(2):
                sp.wait_ge(ye_done[p], 16 * NET // 2)
            def load_x3(t, half, p):
                past(sp, S["fin_out"], t - 1)
                sp.dma_start(x3[p][:, :], x3_dram[bass.ds(t * P, P), :]).then_inc(x3_in[p], 16)

            def store_out(t, half, p):
                sp.wait_ge(S["fin_out"], t + 1)
                sp.dma_start(out[bass.ds(t * P, P), :], acc[p][:, :]).then_inc(out_done[p], 16)

            load_x3(0, 0, 0)
            load_x3(1, 0, 1)

            def out_step(n, t, p):
                store_out(t, n, p)
                load_x3(t + 2, n + 1, p)

            groups(sp, NT // 2 - 1, out_step)
            store_out(NT - 2, 0, 0)
            store_out(NT - 1, 0, 1)
            for p in range(2):
                sp.wait_ge(out_done[p], 16 * NT // 2)

        @block.gpsimd
        def _(pl):
            nc.gpsimd.memset(q_rot[:, :, :], 0.0)
            nc.gpsimd.memset(q_pass[:, :, :], 0.0)
            nc.gpsimd.memset(zeros[:, :], 0.0)
            nc.gpsimd.memset(ones[:, :], 1.0).then_inc(S["consts"], 1)
            pl.wait_ge(S["tables_in"], 16 * 9)

            def rstd_of(T, s, ready, done):
                pl.wait_ge(ready, T.t + 1)
                nc.gpsimd.tensor_tensor(rstd[s][:, :], var_eps[s][:, :], minus_half[:, 0:1], ALU.pow).then_inc(done, 1)

            def rot_sum(T):
                pl.wait_ge(S["rot_parts"], T.t + 1)
                past(pl, S["sc_ps"], T.t)
                past(pl, S["qrot_out"], T.t)
                nc.gpsimd.tensor_tensor(qk_rot[:, :, :], cos_part[:, :, :], sin_part[:, :, :], ALU.add
                                        ).then_inc(S["rot_out"], 1)

            def values(T, q):
                pl.wait_ge(S["prob_out"], T.t + 1)
                past(pl, S["attn_out"], QCH * T.t + q - 1)
                pr = prob[T.p][:, q * QH * XH:(q + 1) * QH * XH].rearrange("p (h g) -> p h g", g=XH)
                vv = kv[T.p][:, D:2 * D].rearrange("p (g d) -> p d g", g=XH)
                o = av[:, q % 2, :].rearrange("p (h d g) -> p h d g", h=QH, d=XD)
                nc.gpsimd.tensor_tensor(o, pr.unsqueeze(2).to_broadcast([P, QH, XD, XH]),
                                        vv.unsqueeze(1).to_broadcast([P, QH, XD, XH]), ALU.mult).then_inc(S["av_out"], 1)

            def tanh_part(T):
                pl.wait_ge(S["rec_out"], T.t + 1)
                past(pl, S["mish_out"], T.t)
                nc.gpsimd.tensor_tensor(th_g[:, :], n_g[:, :], rec_g[:, :], ALU.mult).then_inc(S["th_out"], 1)

            def group_affine(T):
                pl.wait_ge(S["gvar_out"], T.t + 1)
                past(pl, S["y_out"], T.t)
                nc.gpsimd.tensor_tensor(grstd[:, :], gvar[:, :], minus_half, ALU.pow).then_inc(S["pchain"], 1)
                pl.wait_ge(S["pchain"], 3 * T.t + 1)
                nc.gpsimd.tensor_tensor(gscale[:, :], grstd[:, :], gn_w[:, :], ALU.mult).then_inc(S["pchain"], 1)
                pl.wait_ge(S["pchain"], 3 * T.t + 2)
                nc.gpsimd.tensor_tensor(grstd[:, :], moments[:, 0:4], gscale[:, :], ALU.mult).then_inc(S["pchain"], 1)
                pl.wait_ge(S["pchain"], 3 * T.t + 3)
                nc.gpsimd.tensor_tensor(gshift[:, :], gn_b[:, :], grstd[:, :], ALU.subtract).then_inc(S["gaff_out"], 1)

            def gate(T):
                pl.wait_ge(S["y_out"], T.t + 1)
                pl.wait_ge(S["mish_out"], T.t + 1)
                nc.gpsimd.tensor_tensor(my[:, :, :], mish[:, :].rearrange("p (k t) -> p k t", k=KC), y_sb[:, :, :],
                                        ALU.mult).then_inc(S["my_out"], 1)

            def scatter(T):
                for k in range(TOPK):
                    if k == 0:
                        alone(pl, S["rows_out"], T.t + 1)
                    pl.indirect_dma_start(rows_dram, bass.IndirectOffsetOnAxis(ap=row_u[T.p][:, k:k + 1], axis=0),
                                          xn3[T.p][:, :], None).then_inc(scat_done[T.p], 16)

            def step(n, c):
                T = stage_tiles(n, c)
                at(T[1], tanh_part)
                at(T[3], rstd_of, 2, S["ln3_var"], S["ln3_rstd"])
                at(T[1], group_affine)
                at(T[1], gate)
                at(T[0], rstd_of, 0, S["ln1_var"], S["ln1_rstd"])
                at(T[2], values, 0)
                at(T[1], rstd_of, 1, S["ln2_var"], S["ln2_rstd"])
                at(T[2], values, 1)
                at(T[2], values, 2)
                at(T[0], rot_sum)
                at(T[2], values, 3)
                at(T[4], scatter)

            steps(pl, step)

            pl.wait_ge(S["tab_out"], 1)
            for e in range(E):
                nc.gpsimd.tensor_scalar(shift[:, :, :], pick_all[:, :, :], float(e), row0[:, e:e + 1], ALU.is_equal, ALU.mult
                                        ).then_inc(S["shift_out"], 1)
                pl.wait_ge(S["shift_out"], 2 * e + 1)
                nc.gpsimd.tensor_tensor(row_all[:, :, :], row_all[:, :, :], shift[:, :, :], ALU.subtract
                                        ).then_inc(S["shift_out"], 1)
                pl.wait_ge(S["shift_out"], 2 * e + 2)

            for p in range(2):
                pl.wait_ge(ye_done[p], 16 * NET // 2)
            with pl.Fori(0, NT // 2) as n:
                for p in range(2):
                    for k in range(TOPK):
                        if k == 0:
                            alone(pl, S["idxg_out"], 2 * n + p + 1)
                        pl.indirect_dma_start(yg[p][k], None, y_dram,
                                              bass.IndirectOffsetOnAxis(ap=idx_g[p][:, k:k + 1], axis=0)
                                              ).then_inc(gath_done[p], 16)

        @block.scalar
        def _(act):
            def copy_t(T, dst, ready, done):
                act.wait_ge(ready, T.t + 1)
                nc.scalar.activation(dst.rearrange("p a b -> p (a b)"), bank[0][:, 0:D], ACT.Copy).then_inc(done, 1)

            def kv_copy(T):
                act.wait_ge(S["kv_ps"], T.t + 1)
                past(act, S["av_out"], QCH * (T.t - 1))
                nc.scalar.activation(kv[T.p][:, :], bank[6][:, :], ACT.Copy).then_inc(S["kv_out"], 1)

            def route_exp(T):
                act.wait_ge(S["lmax_out"], T.t + 1)
                nc.scalar.activation(exp_l[:, :], bank[3][:, 0:E], ACT.Exp, bias=neg_max[:, 0:1],
                                     accum_out=sum_l[:, 0:1]).then_inc(S["expl_out"], 1)

            def value_copy(T):
                act.wait_ge(S["pv_ps"], T.t + 1)
                past(act, S["ret_ps"], T.t)
                nc.scalar.activation(v_sb[:, :], bank[2][:, D:2 * D], ACT.Copy).then_inc(S["v_out"], 1)

            def pass_copy(T):
                past(act, S["sc_ps"], T.t)
                for h in range(RH):
                    r = slice(ROT * h, ROT * h + ROT)
                    nc.scalar.activation(q_pass[r, h, :], bank[2][r, 0:P], ACT.Copy)
                nc.scalar.activation(k_pass[:, :], bank[2][:, P:2 * P], ACT.Copy).then_inc(S["pass_out"], 1)

            def rot_copy(T):
                act.wait_ge(S["rot_out"], T.t + 1)
                for h in range(RH):
                    r = slice(ROT * h, ROT * h + ROT)
                    last = nc.scalar.activation(q_rot[r, h, :], qk_rot[r, 0, :], ACT.Copy)
                last.then_inc(S["qrot_out"], 1)

            def gate_exp(T):
                act.wait_ge(S["gm_out"], T.t + 1)
                past(act, S["ng_out"], T.t)
                nc.scalar.activation(e_g[:, :], gm[:, :], ACT.Exp).then_inc(S["eg_out"], 1)

            def gate_rec(T):
                act.wait_ge(S["ng_out"], T.t + 1)
                nc.scalar.activation(ln_g[:, :], n_g[:, :], ACT.Ln, bias=two[:, 0:1]).then_inc(S["achain"], 1)
                act.wait_ge(S["achain"], T.t + 1)
                past(act, S["th_out"], T.t)
                nc.scalar.activation(rec_g[:, :], ln_g[:, :], ACT.Exp, scale=-1.0).then_inc(S["rec_out"], 1)

            def shared_silu(T):
                act.wait_ge(S["sg_ps"], T.t + 1)
                past(act, S["sha_out"], T.t)
                nc.scalar.activation(sh_s[:, 0:2, :], bank[1][:, 0:2 * P].rearrange("p (a b) -> p a b", a=2), ACT.Silu)
                nc.scalar.activation(sh_s[0:96, 2, :], bank[1][0:96, 2 * P:3 * P], ACT.Silu).then_inc(S["shs_out"], 1)
                nc.scalar.preload_act_table_set("natural_log_exp_and_others")

            def square(T):
                act.wait_ge(S["ret_ps"], T.t + 1)
                past(act, S["sums_out"], T.t)
                nc.scalar.activation(ret_sq[:, :], bank[6][:, 0:D], ACT.Square).then_inc(S["sq_out"], 1)

            def soft_exp(T):
                act.wait_ge(S["sub_out"], T.t + 1)
                past(act, S["av_out"], QCH * (T.t - 1))
                nc.scalar.activation(prob[T.p][:, :], score_sub[:, :], ACT.Exp).then_inc(S["prob_out"], 1)

            def group_norm(T):
                act.wait_ge(S["gaff_out"], T.t + 1)
                past(act, S["my_out"], T.t)
                for j in range(4):
                    last = nc.scalar.activation(
                        y_sb[:, j // 2, SEQ * (j % 2):SEQ * (j % 2) + SEQ], bank[6][:, SEQ * j:SEQ * j + SEQ],
                        ACT.Identity, bias=gshift[:, j:j + 1], scale=gscale[:, j:j + 1])
                last.then_inc(S["y_out"], 1)

            act.wait_ge(S["consts"], 1)
            nc.scalar.preload_act_table_set("natural_log_exp_and_others")

            def step(n, c):
                T = stage_tiles(n, c)
                at(T[1], group_norm)
                at(T[3], copy_t, xT3[:, :, :], S["xT3_ps"], S["xT3_sb"])
                at(T[2], soft_exp)
                at(T[3], shared_silu)
                at(T[0], copy_t, xT1[:, :, :], S["xT1_ps"], S["xT1_sb"])
                at(T[3], route_exp)
                at(T[1], copy_t, xT2[:, :, :], S["xT2_ps"], S["xT2_sb"])
                at(T[1], kv_copy)
                at(T[0], value_copy)
                at(T[0], pass_copy)
                at(T[0], rot_copy)
                at(T[0], gate_exp)
                at(T[2], copy_t, attn_t[:, :, :], S["aT_ps"], S["aT_sb"])
                at(T[0], gate_rec)
                at(T[0], square)

            steps(act, step)

            def xT_out(j, p):
                act.wait_ge(S["eT_ps"], j + 1)
                past(act, S["egu_ps"], j - 1)
                nc.scalar.activation(xeT[p].rearrange("p a b -> p (a b)"), bank[p][:, 0:D], ACT.Copy).then_inc(S["eT_sb"], 1)

            def silu(j, p):
                act.wait_ge(S["egu_ps"], j + 1)
                past(act, S["ea_out"], j - 1)
                nc.scalar.activation(he[p], bank[2 + p][:, 0:INNER], ACT.Silu).then_inc(S["eh_out"], 1)

            def y_copy(j, half, p):
                act.wait_ge(S["ey_ps"], j + 1)
                past(act, ye_done[p], 16 * half)
                nc.scalar.activation(ye[p], bank[6 + p][:, 0:D], ACT.Copy).then_inc(S["ey_out"], 1)

            xT_out(0, 0)
            silu(0, 0)
            xT_out(1, 1)
            silu(1, 1)
            xT_out(2, 0)

            def expert_step(n, j, u):
                silu(j + 1, 1 - (u + 1) % 2)
                xT_out(j + 2, (u + 1) % 2)
                y_copy(j - 1, n, u)

            groups(act, (NET - 4) // 2, lambda n, j, u: expert_step(n, j + 1, u))
            for j in range(NET - 3, NET):
                if j + 1 < NET:
                    silu(j + 1, (j + 1) % 2)
                if j + 2 < NET:
                    xT_out(j + 2, j % 2)
                y_copy(j - 1, (j - 1) // 2, (j - 1) % 2)
            y_copy(NET - 1, NET // 2 - 1, 1)

        @block.tensor
        def _(pe):
            pe.wait_ge(S["tables_in"], 16 * 9)
            pe.wait_ge(S["weights_in"], 16 * 13)
            pe.wait_ge(S["prep"], 1)
            mm = nc.tensor.matmul

            def bank_free(n, *users):
                for s, v in users if type(n) is int else users[:1]:
                    past(pe, s, v)

            def turn(T, src, ready, done):
                pe.wait_ge(ready, T.t + 1)
                for k in range(KC):
                    last = nc.tensor.transpose(bank[0][:, k * P:(k + 1) * P], src[:, k * P:(k + 1) * P], ident[:, :])
                last.then_inc(done, 1)

            def add_bias(dst, c0, cols, stop):
                return mm(dst, ones[0:3, :], bias_parts[:, c0:c0 + cols], start=False, stop=stop)

            def queries(T):
                pe.wait_ge(S["xT2_sb"], T.t + 1)
                past(pe, S["prod_out"], QCH * T.t)
                for k in range(KC):
                    mm(bank[5][:, 0:D], xT2[:, k, :], w_xq[:, k, :], start=(k == 0), stop=False)
                add_bias(bank[5][:, 0:D], 0, D, True).then_inc(S["q_ps"], 1)

            def keys_values(T):
                pe.wait_ge(ctx_in[T.p], 16 * (T.half + 1))
                for k in range(KC):
                    mm(bank[6][:, :], ctx_t[T.p][:, k, :], w_xkv[:, k, :], start=(k == 0), stop=False)
                add_bias(bank[6][:, :], D, 2 * D, True).then_inc(S["kv_ps"], 1)

            def logits(T):
                pe.wait_ge(S["xT3_sb"], T.t + 1)
                for k in range(KC):
                    last = mm(bank[3][:, 0:E], xT3[:, k, :], w_route[:, k, :], start=(k == 0), stop=(k == KC - 1))
                last.then_inc(S["logit_ps"], 1)

            def rot_in(T):
                pe.wait_ge(S["xT1_sb"], T.t + 1)
                for f in range(4):
                    for k in range(KC):
                        last = mm(bank[1][:, f * P:(f + 1) * P], w_qk[:, k, f, :], xT1[:, k, :], start=(k == 0), stop=(k == KC - 1))
                last.then_inc(S["qk_ps"], 1)

            def pass_in(T):
                for f in range(2):
                    for k in range(KC):
                        mm(bank[2][:, f * P:(f + 1) * P], w_qk[:, k, 4 + f, :], xT1[:, k, :], start=(k == 0), stop=(k == KC - 1))
                for k in range(KC):
                    last = mm(bank[2][:, D:2 * D], xT1[:, k, :], w_v[:, k, :], start=(k == 0), stop=(k == KC - 1))
                last.then_inc(S["pv_ps"], 1)

            def gate_in(T):
                past(pe, S["mish_out"], T.t)
                for f in range(KC):
                    for k in range(KC):
                        last = mm(bank[4][:, f * P:(f + 1) * P], w_g[:, k, f * P:(f + 1) * P], xT1[:, k, :],
                                  start=(k == 0), stop=(k == KC - 1))
                last.then_inc(S["g_ps"], 1)

            def cross_out(T):
                pe.wait_ge(S["aT_sb"], T.t + 1)
                for k in range(KC):
                    mm(bank[7][:, 0:D], attn_t[:, k, :], w_xo[:, k, :], start=(k == 0), stop=False)
                add_bias(bank[7][:, 0:D], 3 * D, D, True).then_inc(S["xo_ps"], 1)

            def ranks(T):
                pe.wait_ge(S["chosen_out"], T.t + 1)
                mm(bank[3][:, 0:E], before[:, :], chosen[:, :], start=True, stop=True)
                mm(bank[3][:, E:2 * E], ones[:, :], chosen[:, :], start=True, stop=True).then_inc(S["rank_ps"], 1)

            def ret_scores(T):
                pe.wait_ge(S["qrot_out"], T.t + 1)
                pe.wait_ge(S["pass_out"], T.t + 1)
                mm(bank[3][:, :], qk_rot[:, 1, :], q_rot[:, :, :].rearrange("p h t -> p (h t)"), start=True, stop=False)
                mm(bank[3][:, :], k_pass[:, :], q_pass[:, :, :].rearrange("p h t -> p (h t)"), start=False,
                   stop=True).then_inc(S["sc_ps"], 1)

            def shared_in(T, w, b, done):
                pe.wait_ge(S["xT3_sb"], T.t + 1)
                for j, (r0, rows) in enumerate(SHC):
                    for k in range(KC):
                        last = mm(bank[b][0:rows, j * P:(j + 1) * P], w[:, k, r0:r0 + rows], xT3[:, k, :],
                                  start=(k == 0), stop=(k == KC - 1))
                last.then_inc(done, 1)

            def retain(T):
                pe.wait_ge(S["att_out"], T.t + 1)
                pe.wait_ge(S["v_out"], T.t + 1)
                for h in range(RH):
                    last = mm(bank[6][RD * (h % 2):RD * (h % 2) + RD, (h // 2) * P:(h // 2 + 1) * P],
                              v_sb[:, h * RD:(h + 1) * RD], att_t[:, h * P:(h + 1) * P], start=True, stop=True)
                last.then_inc(S["ret_ps"], 1)

            def group_moments(T):
                pe.wait_ge(S["sums_out"], T.t + 1)
                mm(bank[3][:, 0:8], head_mean[:, :], sums[:, :], start=True, stop=True).then_inc(S["stat_ps"], 1)

            def shared_out(T):
                pe.wait_ge(S["sha_out"], T.t + 1)
                for j, (r0, rows) in enumerate(SHC):
                    last = mm(bank[7][:, 0:D], sh_a[0:rows, j, :], w_sd[0:rows, j, :], start=(j == 0), stop=(j == len(SHC) - 1))
                last.then_inc(S["shd_ps"], 1)

            def ret_out(T):
                pe.wait_ge(S["my_out"], T.t + 1)
                for k in range(KC):
                    last = mm(bank[7][:, 0:D], my[:, k, :], w_o[:, k, :], start=(k == 0), stop=(k == KC - 1))
                last.then_inc(S["wo_ps"], 1)

            def step(n, c):
                T = stage_tiles(n, c)

                def read(name, stage, this_step=False):
                    return S[name], through(n, c if this_step else c - 1, stage)

                if T[3]:
                    bank_free(n, read("xall_out", 3), read("x1_out", 1), read("x2_out", 3))
                    cross_out(T[3])
                if T[1]:
                    bank_free(n, read("att_out", 0), read("rows_out", 4), read("expl_out", 3), read("gvar_out", 1))
                    group_moments(T[1])
                if T[3]:
                    bank_free(n, read("aT_sb", 2), read("xT2_sb", 1), read("xT1_sb", 0), read("xT3_sb", 3))
                    turn(T[3], xn3[T[3].p], S["ln3_out"], S["xT3_ps"])
                    bank_free(n, read("rot_parts", 0), read("shs_out", 3))
                    shared_in(T[3], w_sg, 1, S["sg_ps"])
                if T[0]:
                    bank_free(n, read("xT3_sb", 3, True), read("aT_sb", 2), read("xT2_sb", 1), read("xT1_sb", 0))
                    turn(T[0], xn1, S["ln1_out"], S["xT1_ps"])
                if T[1]:
                    bank_free(n, read("x2_out", 3, True), read("xall_out", 3), read("x1_out", 1))
                    ret_out(T[1])
                if T[3]:
                    bank_free(n, read("pass_out", 0), read("sha_out", 3))
                    shared_in(T[3], w_su, 2, S["su_ps"])
                    bank_free(n, read("gvar_out", 1, True), read("att_out", 0), read("rows_out", 4), read("expl_out", 3))
                    logits(T[3])
                if T[1]:
                    bank_free(n, read("y_out", 0), read("kv_out", 1))
                    keys_values(T[1])
                if T[4]:
                    bank_free(n, read("expl_out", 3, True), read("gvar_out", 1, True), read("att_out", 0), read("rows_out", 4))
                    ranks(T[4])
                if T[0]:
                    bank_free(n, read("shs_out", 3, True), read("rot_parts", 0))
                    rot_in(T[0])
                if T[1]:
                    bank_free(n, read("xT1_sb", 0, True), read("xT3_sb", 3, True), read("aT_sb", 2), read("xT2_sb", 1))
                    turn(T[1], xn2, S["ln2_out"], S["xT2_ps"])
                    queries(T[1])
                if T[0]:
                    bank_free(n, read("sha_out", 3, True), read("pass_out", 0))
                    pass_in(T[0])
                if T[3]:
                    bank_free(n, read("x1_out", 1, True), read("x2_out", 3, True), read("xall_out", 3))
                    shared_out(T[3])
                if T[0]:
                    gate_in(T[0])
                    bank_free(n, read("rows_out", 4, True), read("expl_out", 3, True), read("gvar_out", 1, True), read("att_out", 0))
                    ret_scores(T[0])
                if T[2]:
                    bank_free(n, read("xT2_sb", 1, True), read("xT1_sb", 0, True), read("xT3_sb", 3, True), read("aT_sb", 2))
                    turn(T[2], attn_n, S["attnn_out"], S["aT_ps"])
                if T[0]:
                    bank_free(n, read("kv_out", 1, True), read("y_out", 0))
                    retain(T[0])

            steps(pe, step)

            pe.wait_ge(S["expert_w0"], 2 * 16 * E)
            pe.wait_ge(S["xall_out"], NT)
            pe.wait_ge(S["tab_out"], 1)

            def e_turn(j, turn, b):
                p = b % 2
                pe.wait_ge(xe_in[b], 16 * (turn + 1))
                past(pe, S["eT_sb"], j - 1)
                for k in range(KC):
                    last = nc.tensor.transpose(bank[p][:, k * P:(k + 1) * P], xe[b][:, k * P:(k + 1) * P], ident[:, :])
                last.then_inc(S["eT_ps"], 1)

            def e_up(j, p):
                e = pe.value_load(table[0:1, 0, bass.ds(j, 1)], min_val=0, max_val=E - 1)
                pe.wait_ge(S["eT_sb"], j + 1)
                past(pe, S["ea_out"], j - 1)
                for k in range(KC):
                    last = mm(bank[2 + p][:, 0:2 * INNER], xeT[p][:, k, :],
                              w_gu[:, bass.ds(e, 1), k, :].rearrange("p e n -> p (e n)"), start=(k == 0), stop=(k == KC - 1))
                last.then_inc(S["egu_ps"], 1)

            def e_turn2(j, p):
                pe.wait_ge(S["ea_out"], j + 1)
                past(pe, S["eaT_sb"], j - 1)
                for k in range(2):
                    last = nc.tensor.transpose(bank[4 + p][0:HI, k * P:(k + 1) * P], ae[p][:, k * HI:(k + 1) * HI], ident[:, :])
                last.then_inc(S["eaT_ps"], 1)

            def e_down(j, p):
                e = pe.value_load(table[0:1, 0, bass.ds(j, 1)], min_val=0, max_val=E - 1)
                pe.wait_ge(S["eaT_sb"], j + 1)
                past(pe, S["ey_out"], j - 1)
                for k in range(2):
                    last = mm(bank[6 + p][:, 0:D], aeT[p][:, k, :],
                              w_d[:, bass.ds(e, 1), k, :].rearrange("p e n -> p (e n)"), start=(k == 0), stop=(k == 1))
                last.then_inc(S["ey_ps"], 1)

            def expert_step(n, j, b, first=False, turn=True, up=True):
                if up:
                    e_up(j + 1, (b + 1) % 2)
                if turn:
                    e_turn(j + 2, n + (b + 2) // XB, (b + 2) % XB)
                e_turn2(j, b % 2)
                if not first:
                    e_down(j - 1, (b + 1) % 2)

            e_turn(0, 0, 0)
            e_up(0, 0)
            e_turn(1, 0, 1)
            groups(pe, NET // XB - 1, lambda n, j, b: expert_step(n, j, b, first=type(j) is int and j == 0), XB)
            for b in range(XB):
                expert_step(NET // XB - 1, NET - XB + b, b, turn=b < XB - 2, up=b < XB - 1)
            e_down(NET - 1, 1)

        @block.vector
        def _(dve):
            v = nc.vector
            links = [0]

            def link(ins):
                links[0] += 1
                ins.then_inc(S["chain"], 1)
                dve.wait_ge(S["chain"], links[0])

            dve.wait_ge(S["tables_in"], 16 * 9)
            dve.wait_ge(S["bias_in"], 16)
            link(v.tensor_copy(bias_hi[:, :], bias3[:, :]))
            link(v.tensor_tensor(bias_r[:, :], bias3[:, :], bias_hi[:, :], ALU.subtract))
            link(v.tensor_copy(bias_mid[:, :], bias_r[:, :]))
            link(v.tensor_tensor(bias_r[:, :], bias_r[:, :], bias_mid[:, :], ALU.subtract))
            link(v.tensor_copy(bias_lo[:, :], bias_r[:, :]))
            link(v.tensor_scalar(bias_r[:, :], bias_hi[:, :], eye3[:, 0:1], None, ALU.mult))
            link(v.scalar_tensor_tensor(out=bias_r[:, :], in0=bias_mid[:, :], scalar=eye3[:, 1:2], in1=bias_r[:, :],
                                        op0=ALU.mult, op1=ALU.add))
            link(v.scalar_tensor_tensor(out=bias_parts[:, :], in0=bias_lo[:, :], scalar=eye3[:, 2:3], in1=bias_r[:, :],
                                        op0=ALU.mult, op1=ALU.add))
            link(v.tensor_copy(before[:, :], before_f[:, :]))
            link(v.memset(two[:, :], 2.0))
            dve.wait_ge(S["consts"], 1)
            link(v.tensor_copy(row_base[:, :], region0))
            v.memset(chosen[:, :], 0.0).then_inc(S["prep"], 1)
            ch = {k: sem(f"chain_{k}") for k in ("ln1", "ln2", "ln3", "gn", "top", "rows", "soft")}

            def ln_stats(s, src, done, name, T):
                c = ch[name]
                v.bn_stats(stats[s][:, :], src).then_inc(c, 1)
                alone(dve, c, 2 * T.t + 1)
                v.bn_aggr(mv[s][:, :], stats[s][:, :]).then_inc(c, 1)
                dve.wait_ge(c, 2 * T.t + 2)
                v.tensor_scalar(var_eps[s][:, :], mv[s][:, 1:2], EPS, None, ALU.add).then_inc(done, 1)

            def ln_out(T, s, src, dst, ready, done):
                dve.wait_ge(ready, T.t + 1)
                v.tensor_scalar(dst, src, mv[s][:, 0:1], rstd[s][:, 0:1], ALU.subtract, ALU.mult).then_inc(done, 1)

            def ln1_in(T):
                alone(dve, xin_in[T.p], 16 * (T.half + 1))
                ln_stats(0, xin[T.p][:, :], S["ln1_var"], "ln1", T)

            def ln1_out(T):
                ln_out(T, 0, xin[T.p][:, :], xn1[:, :], S["ln1_rstd"], S["ln1_out"])

            def ln2_out(T):
                ln_out(T, 1, x1[T.p][:, :], xn2[:, :], S["ln2_rstd"], S["ln2_out"])

            def ln3_out(T):
                past(dve, scat_done[T.p], 16 * TOPK * T.half)
                ln_out(T, 2, x2[T.p][:, :], xn3[T.p][:, :], S["ln3_rstd"], S["ln3_out"])

            def residual1(T):
                dve.wait_ge(S["wo_ps"], T.t + 1)
                v.tensor_tensor(x1[T.p][:, :], bank[7][:, 0:D], xin[T.p][:, :], ALU.add).then_inc(S["x1_out"], 1)
                dve.wait_ge(S["x1_out"], T.t + 1)
                ln_stats(1, x1[T.p][:, :], S["ln2_var"], "ln2", T)

            def q_prod(T, q):
                if q == 0:
                    dve.wait_ge(S["q_ps"], T.t + 1)
                    dve.wait_ge(S["kv_out"], T.t + 1)
                past(dve, S["score_out"], QCH * T.t + q - 1)
                qq = bank[5][:, q * QH * XD:(q + 1) * QH * XD].rearrange("p (h d) -> p h d", d=XD)
                kk = kv[T.p][:, 0:D].rearrange("p (g d) -> p g d", d=XD)
                v.tensor_tensor(prod[:, q % 2, :].rearrange("p (h g d) -> p h g d", h=QH, g=XH),
                                qq.unsqueeze(2).to_broadcast([P, QH, XH, XD]),
                                kk.unsqueeze(1).to_broadcast([P, QH, XH, XD]), ALU.mult).then_inc(S["prod_out"], 1)

            def q_sum(T, q):
                dve.wait_ge(S["prod_out"], QCH * T.t + q + 1)
                v.tensor_reduce(scores[:, q * QH * XH:(q + 1) * QH * XH],
                                prod[:, q % 2, :].rearrange("p (a d) -> p a d", d=XD), AX_X, ALU.add
                                ).then_inc(S["score_out"], 1)

            def soft_max(T):
                dve.wait_ge(S["score_out"], QCH * (T.t + 1))
                s3 = scores[:, :].rearrange("p (h g) -> p h g", g=XH)
                v.tensor_reduce(score_max[:, :], s3, AX_X, ALU.max).then_inc(ch["soft"], 1)
                dve.wait_ge(ch["soft"], T.t + 1)
                v.tensor_tensor(score_sub[:, :].rearrange("p (h g) -> p h g", g=XH), s3,
                                score_max[:, :].unsqueeze(2).to_broadcast([P, XH, XH]), ALU.subtract
                                ).then_inc(S["sub_out"], 1)

            def soft_sum(T):
                dve.wait_ge(S["prob_out"], T.t + 1)
                v.tensor_reduce(prob_sum[:, :], prob[T.p][:, :].rearrange("p (h g) -> p h g", g=XH), AX_X, ALU.add
                                ).then_inc(S["psum_out"], 1)
                dve.wait_ge(S["psum_out"], T.t + 1)
                v.reciprocal(prob_rec[T.p][:, :], prob_sum[:, :]).then_inc(S["prec_out"], 1)

            def a_sum(T, q):
                dve.wait_ge(S["av_out"], QCH * T.t + q + 1)
                v.tensor_reduce(attn[:, q * QH * XD:(q + 1) * QH * XD],
                                av[:, q % 2, :].rearrange("p (a g) -> p a g", g=XH), AX_X, ALU.add
                                ).then_inc(S["attn_out"], 1)

            def a_norm(T):
                dve.wait_ge(S["attn_out"], QCH * (T.t + 1))
                dve.wait_ge(S["prec_out"], T.t + 1)
                v.tensor_tensor(attn_n[:, :].rearrange("p (h d) -> p h d", d=XD),
                                attn[:, :].rearrange("p (h d) -> p h d", d=XD),
                                prob_rec[T.p][:, :].unsqueeze(2).to_broadcast([P, XH, XD]), ALU.mult
                                ).then_inc(S["attnn_out"], 1)

            def rotate(T):
                dve.wait_ge(S["qk_ps"], T.t + 1)
                past(dve, S["rot_out"], T.t)
                b3 = bank[1][:, :].rearrange("p (f t) -> p f t", f=4)
                v.tensor_tensor(cos_part[:, :, :], b3[:, 0:2, :], rot_tab[:, 0:2, :], ALU.mult)
                v.tensor_tensor(sin_part[:, :, :], b3[:, 2:4, :], rot_tab[:, 2:4, :], ALU.mult).then_inc(S["rot_parts"], 1)

            def gate_min(T):
                dve.wait_ge(S["g_ps"], T.t + 1)
                past(dve, S["eg_out"], T.t)
                v.tensor_scalar(gm[:, :], bank[4][:, 0:D], 18.0, None, ALU.min).then_inc(S["gm_out"], 1)

            def gate_n(T):
                dve.wait_ge(S["eg_out"], T.t + 1)
                past(dve, S["th_out"], T.t)
                v.scalar_tensor_tensor(out=n_g[:, :], in0=e_g[:, :], scalar=2.0, in1=e_g[:, :], op0=ALU.add,
                                       op1=ALU.mult).then_inc(S["ng_out"], 1)

            def gate_mish(T):
                dve.wait_ge(S["th_out"], T.t + 1)
                past(dve, S["my_out"], T.t)
                v.tensor_tensor(mish[:, :], bank[4][:, 0:D], th_g[:, :], ALU.mult).then_inc(S["mish_out"], 1)

            def decay(T):
                dve.wait_ge(S["sc_ps"], T.t + 1)
                v.tensor_tensor(att_t[:, :], bank[3][:, :], decay_tab[:, :], ALU.mult).then_inc(S["att_out"], 1)

            def ret_sums(T):
                dve.wait_ge(S["sq_out"], T.t + 1)
                v.tensor_reduce(sums[:, 0:4], bank[6][:, 0:D].rearrange("p (a s) -> p a s", s=SEQ), AX_X, ALU.add)
                v.tensor_reduce(sums[:, 4:8], ret_sq[:, :].rearrange("p (a s) -> p a s", s=SEQ), AX_X, ALU.add
                                ).then_inc(S["sums_out"], 1)

            def ret_var(T):
                c = ch["gn"]
                dve.wait_ge(S["stat_ps"], T.t + 1)
                past(dve, S["gaff_out"], T.t)
                v.tensor_copy(moments[:, :], bank[3][:, 0:8]).then_inc(c, 1)
                dve.wait_ge(c, 2 * T.t + 1)
                v.scalar_tensor_tensor(out=neg_msq[:, :], in0=moments[:, 0:4], scalar=-1.0, in1=moments[:, 0:4],
                                       op0=ALU.mult, op1=ALU.mult).then_inc(c, 1)
                dve.wait_ge(c, 2 * T.t + 2)
                v.scalar_tensor_tensor(out=gvar[:, :], in0=moments[:, 4:8], scalar=EPS, in1=neg_msq[:, :],
                                       op0=ALU.add, op1=ALU.add).then_inc(S["gvar_out"], 1)

            def residual2(T):
                dve.wait_ge(S["xo_ps"], T.t + 1)
                v.tensor_tensor(x2[T.p][:, :], bank[7][:, 0:D], x1[T.p][:, :], ALU.add).then_inc(S["x2_out"], 1)

            def ln3_in(T):
                dve.wait_ge(S["x2_out"], T.t + 1)
                ln_stats(2, x2[T.p][:, :], S["ln3_var"], "ln3", T)

            def route_max(T):
                dve.wait_ge(S["logit_ps"], T.t + 1)
                v.tensor_reduce(neg_max[:, :], bank[3][:, 0:E], AX_X, ALU.max, negate=True).then_inc(S["lmax_out"], 1)

            def route_top(T):
                c = ch["top"]
                dve.wait_ge(S["expl_out"], T.t + 1)
                v.reciprocal(rec_l[:, :], sum_l[:, :]).then_inc(c, 1)
                dve.wait_ge(c, 8 * T.t + 1)
                v.tensor_scalar(prob_l[:, :], exp_l[:, :], rec_l[:, 0:1], None, ALU.mult).then_inc(c, 1)
                alone(dve, c, 8 * T.t + 2)
                v.max(top8[:, :], prob_l[:, :]).then_inc(c, 1)
                alone(dve, c, 8 * T.t + 3)
                v.max_index(idx8[:, :], top8[:, :], prob_l[:, :]).then_inc(c, 1)
                alone(dve, c, 8 * T.t + 4)
                v.tensor_copy(wt_all[:, bass.ds(T.t, 1), :].rearrange("p a k -> p (a k)"), top8[:, 0:TOPK]).then_inc(c, 1)
                v.tensor_copy(idx_f[:, :], idx8[:, 0:TOPK]).then_inc(c, 1)
                alone(dve, c, 8 * T.t + 6)
                v.tensor_copy(pick_all[:, bass.ds(T.t, 1), :].rearrange("p a k -> p (a k)"), idx_f[:, :]).then_inc(c, 1)
                v.tensor_tensor(pick[:, :, :], expert_no.unsqueeze(1).to_broadcast([P, TOPK, E]),
                                idx_f[:, :].unsqueeze(2).to_broadcast([P, TOPK, E]), ALU.is_equal).then_inc(c, 1)
                dve.wait_ge(c, 8 * T.t + 8)
                with nc.allow_low_precision(reason="zeros and ones"):
                    v.tensor_reduce(chosen[:, :], pick[:, :, :].rearrange("p k e -> p e k"), AX_X, ALU.add
                                    ).then_inc(S["chosen_out"], 1)

            def route_rows(T):
                c = ch["rows"]
                dve.wait_ge(S["rank_ps"], T.t + 1)
                v.tensor_tensor(row_of[:, :], bank[3][:, 0:E], row_base[:, :], ALU.add).then_inc(c, 1)
                dve.wait_ge(c, 4 * T.t + 1)
                v.tensor_tensor(row_base[:, :], bank[3][:, E:2 * E], row_base[:, :], ALU.add).then_inc(c, 1)
                v.tensor_tensor(pick_row[:, :, :], pick[:, :, :], row_of[:, :].unsqueeze(1).to_broadcast([P, TOPK, E]),
                                ALU.mult).then_inc(c, 1)
                dve.wait_ge(c, 4 * T.t + 3)
                v.tensor_reduce(row_f[:, :], pick_row[:, :, :], AX_X, ALU.add).then_inc(c, 1)
                past(dve, scat_done[T.p], 16 * TOPK * T.half)
                dve.wait_ge(c, 4 * T.t + 4)
                v.tensor_copy(row_all[:, bass.ds(T.t, 1), :].rearrange("p a k -> p (a k)"), row_f[:, :])
                v.tensor_copy(row_u[T.p][:, :], row_f[:, :]).then_inc(S["rows_out"], 1)

            def shared_mul(T):
                dve.wait_ge(S["shs_out"], T.t + 1)
                dve.wait_ge(S["su_ps"], T.t + 1)
                v.tensor_tensor(sh_a[:, 0:2, :], bank[2][:, 0:2 * P].rearrange("p (a b) -> p a b", a=2), sh_s[:, 0:2, :], ALU.mult)
                v.tensor_tensor(sh_a[0:96, 2, :], bank[2][0:96, 2 * P:3 * P], sh_s[0:96, 2, :], ALU.mult
                                ).then_inc(S["sha_out"], 1)

            def residual3(T):
                dve.wait_ge(S["shd_ps"], T.t + 1)
                past(dve, x3_done[T.p], 16 * T.half)
                v.tensor_tensor(x3[T.p][:, :], bank[7][:, 0:D], x2[T.p][:, :], ALU.add).then_inc(S["xall_out"], 1)

            def step(n, c):
                T = stage_tiles(n, c)
                at(T[2], q_prod, 2)
                at(T[1], ret_sums)
                at(T[3], residual2)
                at(T[3], ln3_in)
                at(T[2], q_sum, 1)
                at(T[1], ret_var)
                at(T[2], q_sum, 2)
                at(T[1], gate_mish)
                at(T[3], ln3_out)
                at(T[2], q_prod, 3)
                at(T[0], ln1_in)
                at(T[2], q_sum, 3)
                at(T[0], ln1_out)
                at(T[2], soft_max)
                at(T[4], route_top)
                at(T[1], residual1)
                at(T[3], route_max)
                at(T[2], soft_sum)
                at(T[2], a_sum, 0)
                at(T[3], shared_mul)
                at(T[1], ln2_out)
                at(T[4], route_rows)
                at(T[0], rotate)
                at(T[2], a_sum, 1)
                at(T[1], q_prod, 0)
                at(T[1], q_prod, 1)
                at(T[2], a_sum, 2)
                at(T[1], q_sum, 0)
                at(T[2], a_sum, 3)
                at(T[0], gate_min)
                at(T[2], a_norm)
                at(T[0], decay)
                at(T[0], gate_n)
                at(T[3], residual3)

            steps(dve, step)

            dve.wait_ge(S["rows_out"], NT)
            link(v.tensor_tensor(cnt[:, 0:E], row_base[:, :], region0, ALU.subtract))
            link(v.memset(cnt[:, E:E + 1], 0.0))
            link(v.tensor_copy(tail_i[0:1, :], row_base[0:1, :]))
            link(v.tensor_scalar(cnt[:, :], cnt[:, :], float(P - 1), None, ALU.add))
            link(v.tensor_copy(cnt_i[:, :], cnt[:, :]))
            link(v.tensor_scalar(cnt_i[:, :], cnt_i[:, :], 7, None, ALU.arith_shift_right))
            link(v.tensor_copy(cnt[:, :], cnt_i[:, :]))
            link(v.memset(row0[:, :], 1.0))
            link(v.tensor_tensor_scan(cum[:, :], row0[:, :], cnt[:, :], 0.0, ALU.mult, ALU.add))
            link(v.tensor_tensor(cnt[:, :], cum[:, :], cnt[:, :], ALU.subtract))
            link(v.tensor_scalar(row0[:, :], small[:, 40:40 + NX], float(REG), None, ALU.mult))
            link(v.scalar_tensor_tensor(out=row0[:, :], in0=cnt[:, :], scalar=float(-P), in1=row0[:, :], op0=ALU.mult,
                                        op1=ALU.add))
            link(v.memset(e_of[:, :], 0.0))
            for e in range(E):
                link(v.scalar_tensor_tensor(out=e_of[:, :], in0=tile_no[:, :], scalar=cum[:, e:e + 1], in1=e_of[:, :],
                                            op0=ALU.is_ge, op1=ALU.add))
            link(v.tensor_scalar(base_f[:, :], tile_no[:, :], float(P), None, ALU.mult))
            for e in range(NX):
                link(v.tensor_scalar(tile_tmp[:, :], e_of[:, :], float(e), row0[:, e:e + 1], ALU.is_equal, ALU.mult))
                link(v.tensor_tensor(base_f[:, :], base_f[:, :], tile_tmp[:, :], ALU.add))
            link(v.tensor_scalar(e_of[:, :], e_of[:, :], float(E - 1), None, ALU.min))
            link(v.tensor_copy(table[0:1, 0, :], e_of[0:1, :]))
            v.tensor_copy(table[0:1, 1, :], base_f[0:1, :]).then_inc(S["tab_out"], 1)

            def e_mul(j, p):
                dve.wait_ge(S["eh_out"], j + 1)
                past(dve, S["eaT_ps"], j - 1)
                v.tensor_tensor(ae[p], bank[2 + p][:, INNER:2 * INNER], he[p], ALU.mult).then_inc(S["ea_out"], 1)

            def e_turned(j, p):
                dve.wait_ge(S["eaT_ps"], j + 1)
                past(dve, S["ey_ps"], j - 1)
                v.tensor_copy(aeT[p].rearrange("p a b -> p (a b)"), bank[4 + p][0:HI, 0:D]).then_inc(S["eaT_sb"], 1)

            e_mul(0, 0)

            def expert_step(n, j, p):
                e_turned(j, p)
                e_mul(j + 1, 1 - p)

            groups(dve, (NET - 2) // 2, expert_step)
            e_turned(NET - 2, 0)
            e_mul(NET - 1, 1)
            e_turned(NET - 1, 1)

            def indices(t, half, p):
                past(dve, gath_done[p], 16 * TOPK * half)
                v.tensor_copy(idx_g[p][:, :], row_all[:, bass.ds(t, 1), :].rearrange("p a k -> p (a k)")
                              ).then_inc(S["idxg_out"], 1)

            def combine(t, half, p):
                dve.wait_ge(gath_done[p], 16 * TOPK * (half + 1))
                past(dve, out_done[p], 16 * half)
                dve.wait_ge(x3_in[p], 16 * (half + 1))
                for k in range(TOPK):
                    ins = v.scalar_tensor_tensor(
                        out=acc[p][:, :], in0=yg[p][k], scalar=wt_all[:, bass.ds(t, 1), k:k + 1].rearrange("p a k -> p (a k)"),
                        in1=x3[p][:, :] if k == 0 else acc[p][:, :], op0=ALU.mult, op1=ALU.add)
                    if k < TOPK - 1:
                        ins.then_inc(ch["fin"], 1)
                        dve.wait_ge(ch["fin"], (TOPK - 1) * t + k + 1)
                    else:
                        ins.then_inc(S["fin_out"], 1)

            ch["fin"] = sem("chain_fin")
            dve.wait_ge(ye_done[0], 16 * NET // 2)
            dve.wait_ge(ye_done[1], 16 * NET // 2)
            dve.wait_ge(S["shift_out"], 2 * E)
            indices(0, 0, 0)

            def out_step(n, t, p):
                indices(t + 1, n + p, 1 - p)
                combine(t, n, p)

            groups(dve, NT // 2 - 1, out_step)
            indices(NT - 1, NT // 2 - 1, 1)
            combine(NT - 2, NT // 2 - 1, 0)
            combine(NT - 1, NT // 2 - 1, 1)


def layouts(x, ctx_2048, L0_attn_wqkv, L0_attn_wg, L0_attn_wo, L0_attn_gn_weight, L0_attn_gn_bias, L0_xattn_Wq,
            L0_xattn_bq, L0_xattn_Wk, L0_xattn_bk, L0_xattn_Wv, L0_xattn_bv, L0_xattn_Wo, L0_xattn_bo, L0_ffn_w_gate,
            L0_ffn_wg, L0_ffn_wu, L0_ffn_wd, L0_ffn_sg, L0_ffn_su, L0_ffn_sd):
    def chunks(w):
        return w.reshape(KC, P, -1).transpose(1, 0, 2).reshape(P, -1)

    a = {}
    a["x"] = x.reshape(TOKENS, D)
    a["ctx_t"] = ctx_2048.reshape(NT, P, KC, P).transpose(0, 3, 2, 1).reshape(NT * P, KC * P)
    w = L0_attn_wqkv.reshape(RH, 3, RD, D)
    q, k, v = w[:, 0], w[:, 1], w[:, 2]

    def turned(r):
        return r.reshape(RH, ROT // 2, 2, D)[:, :, ::-1, :].reshape(RH, ROT, D)

    six = [q[:, :ROT], k[:, :ROT], turned(q[:, :ROT]), turned(k[:, :ROT]), q[:, ROT:], k[:, ROT:]]
    six = np.stack([s.reshape(P, D) for s in six])
    a["w_qk"] = six.reshape(6, P, KC, P).transpose(3, 2, 0, 1).reshape(P, -1)
    a["w_v"] = chunks(v.reshape(D, D).T)
    a["w_g"] = chunks(L0_attn_wg.T)
    a["w_o"] = chunks(L0_attn_wo.T)
    for name, g in (("gn_w", L0_attn_gn_weight), ("gn_b", L0_attn_gn_bias)):
        a[name] = np.repeat(np.repeat(g.reshape(2, 2).T, RD, axis=0), 2, axis=1)
    a["w_xq"] = chunks(L0_xattn_Wq.T)
    a["w_xkv"] = chunks(np.concatenate([L0_xattn_Wk.T, L0_xattn_Wv.T], axis=1))
    a["w_xo"] = chunks(L0_xattn_Wo.T)
    a["bias"] = np.concatenate([L0_xattn_bq, L0_xattn_bk, L0_xattn_bv, L0_xattn_bo])
    a["w_route"] = chunks(L0_ffn_w_gate.T)
    a["w_sg"], a["w_su"], a["w_sd"] = chunks(L0_ffn_sg), chunks(L0_ffn_su), L0_ffn_sd
    gu = np.concatenate([L0_ffn_wg, L0_ffn_wu], axis=2)
    a["w_gu"] = gu.reshape(E, KC, P, 2 * INNER).transpose(0, 2, 1, 3).reshape(E * P, -1)
    a["w_d"] = L0_ffn_wd.reshape(E, 2, HI, D).transpose(0, 2, 1, 3).reshape(E * HI, -1)
    return a


def kernel(**inputs):
    import concourse.bacc as bacc
    from concourse.bass_utils import run_bass_kernel_spmd

    nc = bacc.Bacc("TRN2", target_bir_lowering=False, num_devices=1)
    arrays = layouts(**{k: np.asarray(a) for k, a in inputs.items()})
    arrays.update(constants())
    arrays = {k: np.ascontiguousarray(a) for k, a in arrays.items()}
    io = {k: nc.dram_tensor(f"in_{k}", a.shape, mybir.dt.from_np(a.dtype), kind="ExternalInput").ap() for k, a in arrays.items()}
    out = nc.dram_tensor("out_x", (TOKENS, D), F32, kind="ExternalOutput").ap()
    scratch = [nc.dram_tensor(n, (rows, D), F32, kind="Internal").ap()
               for n, rows in (("expert_rows", ROWS), ("expert_out", NET * P), ("residual", TOKENS))]
    build(nc, io, out, scratch)
    r = run_bass_kernel_spmd(nc, [{f"in_{k}": a for k, a in arrays.items()}], core_ids=[0])
    return r.results[0]["out_x"].reshape(BATCH, SEQ, D)
```

```python
from collections import namedtuple
from contextlib import ExitStack

import numpy as np

import concourse.bass as bass
from concourse import mybir

F32 = mybir.dt.float32
BF16 = mybir.dt.bfloat16
I32 = mybir.dt.int32
U32 = mybir.dt.uint32
ALU = mybir.AluOpType
ACT = mybir.ActivationFunctionType
AX_X = mybir.AxisListType.X

P = 128
BATCH, SEQ, D = 64, 64, 256
TOKENS = BATCH * SEQ
NT = TOKENS // P
KC = D // P
RH, RD = 4, 64
ROT = RD // 2
XH, XD = 16, 16
E, TOPK, INNER = 16, 4, 176
HI = INNER // 2
SH = 2 * INNER
SHC = [(0, 128), (128, 128), (256, 96)]
EPS = 1e-5

XB = 4
GROUP = 8
REG = TOKENS + P
NET = TOKENS * TOPK // P + E
SPARE = NET - TOKENS * TOPK // P
RW = D + E + 1
ROWS = E * REG + SPARE * P

QCH = 4
QH = XH // QCH
CH = QH * XH * XD

STAGES = 5
LOOP0 = 6
LOOPS = (NT - 1 - LOOP0) // 2

Tile = namedtuple("Tile", "t half p")


def tile_at(n, c):
    return Tile(2 * n + c, n + c // 2, c % 2)


def constants():
    f = np.float32
    inv = f(1.0) / f(10000.0) ** (np.arange(0, ROT, 2, dtype=f) / f(ROT))
    t = np.arange(SEQ, dtype=f)
    freqs = np.repeat(t[:, None] * inv[None, :], 2, axis=-1)
    base = (np.arange(0, ROT, 2, dtype=f) + f(0.4 * ROT)) / f(1.4 * ROT)
    scale = base[None, :] ** ((t - SEQ // 2) / f(512.0))[:, None]
    scale = np.concatenate([scale, scale], axis=-1)
    cos, sin = np.cos(freqs).T, np.sin(freqs).T
    sign = np.where(np.arange(ROT) % 2 == 0, f(-1), f(1))[:, None]
    sc = scale.T
    rot = np.stack([cos * sc, cos / sc, sign * sin * sc, sign * sin / sc], axis=1)
    rot = np.tile(rot, (RH, 1, P // SEQ)).astype(f)
    gamma = f(1.0) - f(2.0) ** (f(-5.0) - np.arange(RH, dtype=f))
    j, i = np.arange(P)[:, None], np.arange(P)[None, :]
    lag = i - j
    own = (i // SEQ == j // SEQ) & (lag >= 0)
    decay = np.stack([np.where(own, g ** np.maximum(lag, 0).astype(f), f(0)) for g in gamma], axis=1)
    c = {}
    c["rot_tab"] = rot.reshape(P, 4 * P)
    c["decay_tab"] = decay.astype(f).reshape(P, RH * P)
    c["ident"] = np.eye(P, dtype=f)
    c["head_mean"] = np.where(i // RD == j // RD, f(1.0 / (RD * SEQ)), f(0)).astype(f)
    c["before"] = np.where(j < i, f(1), f(0)).astype(f)
    small = np.zeros((P, 64), f)
    small[:, 0:16] = np.arange(E)
    small[:, 16:32] = np.arange(E) * REG
    small[:, 32:36] = -0.5
    small[0:3, 36:39] = np.eye(3)
    small[:, 40] = 1.0
    small[:, 57] = TOKENS + np.arange(P)
    c["small_tab"] = small
    c["token_no"] = (np.arange(P, dtype=f)[:, None] + f(P) * np.arange(NT, dtype=f)[None, :])
    c["tile_row"] = np.tile(np.arange(NET, dtype=f)[None, :], (P, 1))
    return c


def build(nc, io, out, rows_dram):
    with ExitStack() as ctx:
        def sb(name, shape, dt=F32):
            return ctx.enter_context(nc.sbuf_tensor(name, shape, dt))

        def sem(name):
            return ctx.enter_context(nc.semaphore(name))

        w_qk = sb("w_qk", [P, KC, 6, P])
        w_v = sb("w_v", [P, KC, D])
        w_g = sb("w_g", [P, KC, D])
        w_o = sb("w_o", [P, KC, D])
        w_xq = sb("w_xq", [P, KC, D])
        w_xkv = sb("w_xkv", [P, KC, 2 * D])
        w_xo = sb("w_xo", [P, KC, D])
        w_route = sb("w_route", [P, KC, E])
        w_sg = sb("w_sg", [P, KC, SH])
        w_su = sb("w_su", [P, KC, SH])
        w_sd = sb("w_sd", [P, len(SHC), D])
        w_gu = sb("w_gu", [P, E, KC, 2 * INNER])
        w_d = sb("w_d", [HI, E, 2, D])
        rot_tab = sb("rot_tab", [P, 4, P])
        decay_tab = sb("decay_tab", [P, RH * P])
        ident = sb("ident", [P, P])
        head_mean = sb("head_mean", [P, P])
        before_f = sb("before_f", [P, P])
        before = sb("before", [P, P], BF16)
        ones = sb("ones", [P, P], BF16)
        small = sb("small", [P, 64])
        expert_no, region0, minus_half, eye3 = small[:, 0:16], small[:, 16:32], small[:, 32:36], small[0:3, 36:39]
        one = small[0:E, 40:41]
        gn_w = sb("gn_w", [P, 4])
        gn_b = sb("gn_b", [P, 4])
        bias3 = sb("bias3", [3, 4 * D])
        bias_hi = sb("bias_hi", [3, 4 * D], BF16)
        bias_mid = sb("bias_mid", [3, 4 * D], BF16)
        bias_lo = sb("bias_lo", [3, 4 * D], BF16)
        bias_r = sb("bias_r", [3, 4 * D])
        bias_parts = sb("bias_parts", [3, 4 * D], BF16)

        def pair(name, shape, dt=F32):
            return [sb(f"{name}{p}", shape, dt) for p in range(2)]

        xin = pair("xin", [P, D])
        ctx_t = pair("ctx_t", [P, KC, P])
        x1 = pair("x1", [P, D])
        x2 = pair("x2", [P, D])
        xn1 = sb("xn1", [P, D])
        xn2 = sb("xn2", [P, D])
        add_done = [sem(f"add_done{p}") for p in range(2)]
        row3 = pair("row3", [P, RW])
        xn3 = [r[:, 0:D] for r in row3]
        token_no = sb("token_no", [P, NT])
        stats = [sb(f"stats{s}", [P, 6]) for s in range(3)]
        mv = [sb(f"mv{s}", [P, 2]) for s in range(3)]
        var_eps = [sb(f"var_eps{s}", [P, 1]) for s in range(3)]
        rstd = [sb(f"rstd{s}", [P, 1]) for s in range(3)]
        ln_bias = [sb(f"ln_bias{s}", [P, 1]) for s in range(3)]
        xT1 = sb("xT1", [P, KC, P])
        xT2 = sb("xT2", [P, KC, P])
        xT3 = sb("xT3", [P, KC, P])
        cos_part = sb("cos_part", [P, 2, P])
        sin_part = sb("sin_part", [P, 2, P])
        qk_rot = sb("qk_rot", [P, 2, P])
        k_pass = sb("k_pass", [P, P])
        q_rot = sb("q_rot", [P, RH, P])
        q_pass = sb("q_pass", [P, RH, P])
        v_sb = sb("v_sb", [P, D])
        att_t = sb("att_t", [P, RH * P])
        ret_terms = sb("ret_terms", [P, 2, D])
        sums = sb("sums", [P, 8])
        moments = sb("moments", [P, 8])
        neg_msq = sb("neg_msq", [P, 4])
        gvar = sb("gvar", [P, 4])
        grstd = sb("grstd", [P, 4])
        gscale = sb("gscale", [P, 4])
        gshift = sb("gshift", [P, 4])
        gm = sb("gm", [P, D])
        e_g = sb("e_g", [P, D])
        n_g = sb("n_g", [P, D])
        ln_g = sb("ln_g", [P, D])
        rec_g = sb("rec_g", [P, D])
        th_g = sb("th_g", [P, D])
        mish = sb("mish", [P, D])
        y_sb = sb("y_sb", [P, KC, P])
        my = sb("my", [P, KC, P])
        kv = pair("kv", [P, 2 * D])
        prod = sb("prod", [P, 2, CH])
        scores = sb("scores", [P, XH * XH])
        score_max = sb("score_max", [P, XH])
        score_sub = sb("score_sub", [P, XH * XH])
        prob = pair("prob", [P, XH * XH])
        prob_sum = sb("prob_sum", [P, XH])
        prob_rec = pair("prob_rec", [P, XH])
        av = sb("av", [P, 2, CH])
        attn = sb("attn", [P, D])
        attn_n = sb("attn_n", [P, D])
        attn_t = sb("attn_t", [P, KC, P])
        neg_max = sb("neg_max", [P, 1])
        exp_l = sb("exp_l", [P, E])
        sum_l = sb("sum_l", [P, 1])
        rec_l = sb("rec_l", [P, 1])
        top8 = sb("top8", [P, 8])
        idx8 = sb("idx8", [P, 8], U32)
        pick = sb("pick", [P, TOPK, E])
        chosen = sb("chosen", [P, E], BF16)
        row_base = sb("row_base", [P, E])
        row_of = sb("row_of", [P, E])
        pick_row = sb("pick_row", [P, TOPK, E])
        row_f = sb("row_f", [P, TOPK])
        row_u = pair("row_u", [P, TOPK], U32)
        sh_s = sb("sh_s", [P, len(SHC), P])
        sh_a = sb("sh_a", [P, len(SHC), P])
        x3 = pair("x3", [P, D])

        padding = sb("padding", [P, RW])
        cnt = sb("cnt", [P, E])
        cnt_i = sb("cnt_i", [P, E], I32)
        cum = sb("cum", [P, E])
        ones_row = sb("ones_row", [P, E])
        own = sb("own", [E, 2, E])
        per_expert = sb("per_expert", [E, 2])
        past_it = sb("past_it", [E, 2, NET])
        region_of = sb("region_of", [1, NET])
        first_row = sb("first_row", [1, NET])
        past_end = sb("past_end", [1, NET])
        before_it = sb("before_it", [1, NET])
        tile_no = sb("tile_no", [P, NET])
        table = sb("table", [1, 4, NET], I32)
        tail_i = sb("tail_i", [1, E], I32)

        def carve(t, widths):
            flat, lists, at = t[:, :, :].rearrange("p a b -> p (a b)"), [], 0
            for number, cols in widths:
                lists.append([flat[:, at + q * cols:at + (q + 1) * cols] for q in range(number)])
                at += number * cols
            return lists

        xe, xeT, he = carve(prod, ((XB, RW), (2, D), (2, INNER)))
        ae, aeT, ye = carve(av, ((2, INNER), (2, D), (2, D)))
        xeT = [t.rearrange("p (k t) -> p k t", k=KC) for t in xeT]
        aeT = [t[0:HI].rearrange("p (k t) -> p k t", k=KC) for t in aeT]
        pad_token = sb("pad_token", [P, 1], U32)
        weight = [sb(f"weight{b}", [P, 1]) for b in range(XB)]
        token = [sb(f"token{b}", [P, 1], U32) for b in range(XB)]
        two = sb("two", [P, 1])

        bank = [ctx.enter_context(nc.psum_tensor(f"bank{b}", [P, 512], F32)) for b in range(8)]

        names = """passed tables_in ret_weights_in weights_in bias_in consts prep
            ln1_var ln1_rstd ln1_out ln2_var ln2_rstd ln2_out ln3_var ln3_rstd ln3_out
            xT1_ps xT1_sb xT2_ps xT2_sb xT3_ps xT3_sb
            qk_ps pv_ps g_ps rot_parts rot_out qrot_out pass_out v_out sc_ps att_out ret_ps sums_out stat_ps
            gvar_out gaff_out y_out gm_out eg_out ng_out rec_out th_out mish_out my_out wo_ps x1_out
            q_ps kv_ps kv_out prod_out score_out sub_out prob_out psum_out prec_out
            av_out attn_out attnn_out aT_ps aT_sb xo_ps x2_out
            logit_ps expl_out lmax_out chosen_out rank_ps rows_out
            sg_ps su_ps shs_out sha_out shd_ps xall_out chain pchain achain ln_chain0 ln_chain1 ln_chain2
            expert_w0 tail_out tab_out padding_in padding_out fill_out meta_out dump_in pad_token_out past_out past_ps tail_in
            eT_ps eT_sb egu_ps eh_out ea_out eaT_ps eaT_sb ey_ps ey_out""".split()
        S = {n: sem(n) for n in names}
        xin_in = [sem(f"xin_in{p}") for p in range(2)]
        ctx_in = [sem(f"ctx_in{p}") for p in range(2)]
        scat_done = [sem(f"scat_done{p}") for p in range(2)]
        xe_in = [sem(f"xe_in{b}") for b in range(XB)]
        x3_done = [sem(f"x3_done{p}") for p in range(2)]


        def steps(eng, body):
            for c in range(LOOP0):
                body(0, c)
            with eng.Fori(0, LOOPS) as n:
                for u in range(2):
                    body(n, LOOP0 + u)
            for c in range(LOOP0 + 2 * LOOPS, NT + STAGES - 1):
                body(0, c)

        def stage_tiles(n, c):
            peeled = type(n) is int
            return [tile_at(n, c - s) if not peeled or 0 <= c - s < NT else None for s in range(STAGES)]

        def through(n, c, s):
            t = tile_at(n, c - s).t + 1
            return min(max(t, 0), NT) if type(n) is int else t

        def at(T, op, *more):
            if T:
                op(T, *more)

        def past(eng, s, v):
            if type(v) is int and v <= 0:
                return
            eng.wait_ge(s, v)

        def alone(eng, s, v):
            if type(v) is int and v <= 0:
                return
            eng.wait_ge(s, v)
            eng.sem_inc(S["passed"], 1)

        def groups(eng, count, body, size=2):
            for u in range(size):
                body(0, u, u)
            with eng.Fori(1, count) as n:
                for u in range(size):
                    body(n, size * n + u, u)

        block = ctx.enter_context(nc.Block())

        @block.sync
        def _(sp):
            def load_x(T):
                past(sp, S["x1_out"], T.t - 1)
                sp.dma_start(xin[T.p][:, :], io["x"][bass.ds(T.t * P, P), :]).then_inc(xin_in[T.p], 16)

            def load_ctx(T):
                past(sp, S["kv_ps"], T.t - 1)
                sp.dma_start(ctx_t[T.p][:, :, :].rearrange("p a b -> p (a b)"),
                             io["ctx_t"][bass.ds(T.t * P, P), :]).then_inc(ctx_in[T.p], 16)

            load_x(tile_at(0, 0))
            for dst, src in ((rot_tab[:, :, :].rearrange("p a b -> p (a b)"), "rot_tab"), (decay_tab[:, :], "decay_tab"),
                             (ident[:, :], "ident"), (head_mean[:, :], "head_mean"), (before_f[:, :], "before"),
                             (small[:, :], "small_tab"), (token_no[:, :], "token_no"), (tile_no[:, :], "tile_row"), (gn_w[:, :], "gn_w"), (gn_b[:, :], "gn_b")):
                sp.dma_start(dst, io[src]).then_inc(S["tables_in"], 16)
            sp.dma_start(bias3[:, :], io["bias"].partition_broadcast(3)).then_inc(S["bias_in"], 16)

            def flat(t):
                return t.rearrange("p a b -> p (a b)")

            sp.dma_start(w_qk[:, :, :, :].rearrange("p a b c -> p (a b c)"), io["w_qk"]).then_inc(S["ret_weights_in"], 16)
            for dst, src in ((w_v, "w_v"), (w_g, "w_g"), (w_o, "w_o")):
                sp.dma_start(flat(dst[:, :, :]), io[src]).then_inc(S["ret_weights_in"], 16)
            for dst, src in ((w_xq, "w_xq"), (w_xkv, "w_xkv"), (w_xo, "w_xo"), (w_route, "w_route"), (w_sg, "w_sg"), (w_su, "w_su")):
                sp.dma_start(flat(dst[:, :, :]), io[src]).then_inc(S["weights_in"], 16)
            for j, (r0, rows) in enumerate(SHC):
                sp.dma_start(w_sd[0:rows, j, :], io["w_sd"][r0:r0 + rows, :]).then_inc(S["weights_in"], 16)
            sp.wait_ge(S["padding_out"], 1)
            for j in range(SPARE):
                sp.dma_start(rows_dram[E * REG + j * P:E * REG + (j + 1) * P, :], padding[:, :]).then_inc(S["fill_out"], 16)
            sp.dma_start(out[TOKENS:TOKENS + P, :], padding[:, 0:D]).then_inc(S["dump_in"], 16)

            def load_expert(e):
                sp.dma_start(w_gu[:, bass.ds(e, 1), :, :].rearrange("p e k n -> p (e k n)"),
                             io["w_gu"][bass.ds(e * P, P), :]).then_inc(S["expert_w0"], 16)
                sp.dma_start(w_d[:, bass.ds(e, 1), :, :].rearrange("p e k n -> p (e k n)"),
                             io["w_d"][bass.ds(e * HI, HI), :]).then_inc(S["expert_w0"], 16)

            def store_x3(T):
                sp.wait_ge(S["xall_out"], T.t + 1)
                sp.dma_start(out[bass.ds(T.t * P, P), :], x3[T.p][:, :]).then_inc(x3_done[T.p], 16)

            def step(n, c):
                peeled = type(n) is int
                T = stage_tiles(n, c)
                if not peeled or c > 0:
                    at(T[0], load_x)
                at(T[1], load_ctx)
                at(T[4], store_x3)
                if not peeled and c == LOOP0:
                    load_expert(n)
                expert = c - LOOP0 - LOOPS
                if peeled and LOOPS <= expert < E:
                    load_expert(expert)

            steps(sp, step)

            for p in range(2):
                sp.wait_ge(scat_done[p], 16 * TOPK * NT // 2)
            sp.wait_ge(S["tail_out"], 1)
            for e in range(0, E, 2):
                r = sp.value_load(tail_i[0:1, e:e + 1], min_val=0, max_val=ROWS - P)
                sp.dma_start(rows_dram[bass.ds(r, P), :], padding[:, :]).then_inc(S["fill_out"], 16)
            sp.wait_ge(S["fill_out"], 16 * (E // 2 + SPARE))
            sp.wait_ge(S["tail_in"], 16 * E // 2)
            sp.wait_ge(S["tab_out"], 1)

            def load_rows(j, turn, b):
                past(sp, S["eT_ps"], j - XB + 1)
                past(sp, S["meta_out"], j - XB + 1)
                r = sp.value_load(table[0:1, 1, bass.ds(j, 1)], min_val=0, max_val=ROWS - P)
                sp.dma_start(xe[b], rows_dram[bass.ds(r, P), :]).then_inc(xe_in[b], 16)

            for j in range(XB):
                load_rows(j, 0, j)
            groups(sp, NET // XB - 1, lambda n, j, b: load_rows(j + XB, n + 1, b), XB)
            for p in range(2):
                sp.wait_ge(add_done[p], 16 * (NET // 2 + 1))
            for p in range(2):
                sp.wait_ge(x3_done[p], 16 * NT // 2)

        @block.gpsimd
        def _(pl):
            nc.gpsimd.memset(q_rot[:, :, :], 0.0)
            nc.gpsimd.memset(q_pass[:, :, :], 0.0)
            nc.gpsimd.memset(padding[:, :], 0.0).then_inc(S["padding_in"], 1)
            nc.gpsimd.memset(ones[:, :], 1.0).then_inc(S["consts"], 1)
            pl.wait_ge(S["tables_in"], 16 * 10)

            def ln_scale(T, s, ready, done, used):
                pl.wait_ge(ready, T.t + 1)
                past(pl, used, T.t)
                nc.gpsimd.tensor_tensor(rstd[s][:, :], var_eps[s][:, :], minus_half[:, 0:1], ALU.pow
                                        ).then_inc(S[f"ln_chain{s}"], 1)
                alone(pl, S[f"ln_chain{s}"], T.t + 1)
                nc.gpsimd.tensor_scalar(ln_bias[s][:, :], mv[s][:, 0:1], rstd[s][:, 0:1], -1.0, ALU.mult, ALU.mult
                                        ).then_inc(done, 1)

            def rot_sum(T):
                pl.wait_ge(S["rot_parts"], T.t + 1)
                past(pl, S["sc_ps"], T.t)
                past(pl, S["qrot_out"], T.t)
                nc.gpsimd.tensor_tensor(qk_rot[:, :, :], cos_part[:, :, :], sin_part[:, :, :], ALU.add
                                        ).then_inc(S["rot_out"], 1)

            def values(T, q):
                pl.wait_ge(S["prob_out"], T.t + 1)
                past(pl, S["attn_out"], QCH * T.t + q - 1)
                pr = prob[T.p][:, q * QH * XH:(q + 1) * QH * XH].rearrange("p (h g) -> p h g", g=XH)
                vv = kv[T.p][:, D:2 * D].rearrange("p (g d) -> p d g", g=XH)
                o = av[:, q % 2, :].rearrange("p (h d g) -> p h d g", h=QH, d=XD)
                nc.gpsimd.tensor_tensor(o, pr.unsqueeze(2).to_broadcast([P, QH, XD, XH]),
                                        vv.unsqueeze(1).to_broadcast([P, QH, XD, XH]), ALU.mult).then_inc(S["av_out"], 1)

            def tanh_part(T):
                pl.wait_ge(S["rec_out"], T.t + 1)
                past(pl, S["mish_out"], T.t)
                nc.gpsimd.tensor_tensor(th_g[:, :], n_g[:, :], rec_g[:, :], ALU.mult).then_inc(S["th_out"], 1)

            def group_affine(T):
                pl.wait_ge(S["gvar_out"], T.t + 1)
                past(pl, S["y_out"], T.t)
                nc.gpsimd.tensor_tensor(grstd[:, :], gvar[:, :], minus_half, ALU.pow).then_inc(S["pchain"], 1)
                pl.wait_ge(S["pchain"], 3 * T.t + 1)
                nc.gpsimd.tensor_tensor(gscale[:, :], grstd[:, :], gn_w[:, :], ALU.mult).then_inc(S["pchain"], 1)
                pl.wait_ge(S["pchain"], 3 * T.t + 2)
                nc.gpsimd.tensor_tensor(grstd[:, :], moments[:, 0:4], gscale[:, :], ALU.mult).then_inc(S["pchain"], 1)
                pl.wait_ge(S["pchain"], 3 * T.t + 3)
                nc.gpsimd.tensor_tensor(gshift[:, :], gn_b[:, :], grstd[:, :], ALU.subtract).then_inc(S["gaff_out"], 1)

            def gate(T):
                pl.wait_ge(S["y_out"], T.t + 1)
                pl.wait_ge(S["mish_out"], T.t + 1)
                nc.gpsimd.tensor_tensor(my[:, :, :], mish[:, :].rearrange("p (k t) -> p k t", k=KC), y_sb[:, :, :],
                                        ALU.mult).then_inc(S["my_out"], 1)

            def scatter(T):
                alone(pl, S["rows_out"], T.t + 1)
                for k in range(TOPK):
                    pl.indirect_dma_start(rows_dram, bass.IndirectOffsetOnAxis(ap=row_u[T.p][:, k:k + 1], axis=0),
                                          row3[T.p][:, :], None).then_inc(scat_done[T.p], 16)

            def step(n, c):
                T = stage_tiles(n, c)
                at(T[3], values, 0)
                at(T[2], ln_scale, 1, S["ln2_var"], S["ln2_rstd"], S["ln2_out"])
                at(T[3], values, 1)
                at(T[3], values, 2)
                at(T[3], values, 3)
                at(T[0], ln_scale, 0, S["ln1_var"], S["ln1_rstd"], S["ln1_out"])
                at(T[4], scatter)
                at(T[1], tanh_part)
                at(T[1], group_affine)
                at(T[3], ln_scale, 2, S["ln3_var"], S["ln3_rstd"], S["ln3_out"])
                at(T[1], gate)
                at(T[0], rot_sum)

            steps(pl, step)

            def row_meta(j, turn, b):
                e = pl.value_load(table[0:1, 0, bass.ds(j, 1)], min_val=0, max_val=E - 1)
                alone(pl, xe_in[b], 16 * (turn + 1))
                alone(pl, add_done[b % 2], 16 * (2 * turn + b // 2))
                nc.gpsimd.tensor_copy(token[b][:, :], xe[b][:, D + E:RW])
                nc.gpsimd.tensor_copy(weight[b][:, :], xe[b][:, bass.ds(e + D, 1)]).then_inc(S["meta_out"], 1)

            def add_rows(j, b):
                for p in range(2):
                    done = pl.value_load(table[0:1, 2 + p, bass.ds(j, 1)], min_val=16, max_val=16 * (NET // 2 + 1))
                    alone(pl, add_done[p], done)
                alone(pl, S["ey_out"], j + 1)
                pl.indirect_dma_start(out, bass.IndirectOffsetOnAxis(ap=token[b][:, :], axis=0), ye[b % 2], None,
                                      compute_op=ALU.add).then_inc(add_done[b % 2], 16)

            pl.wait_ge(S["tab_out"], 1)
            pl.wait_ge(S["dump_in"], 16)
            nc.gpsimd.tensor_copy(pad_token[:, :], padding[:, D + E:RW]).then_inc(S["pad_token_out"], 1)
            pl.wait_ge(S["pad_token_out"], 1)
            for p in range(2):
                pl.indirect_dma_start(out, bass.IndirectOffsetOnAxis(ap=pad_token[:, :], axis=0), padding[:, 0:D], None,
                                      compute_op=ALU.add).then_inc(add_done[p], 16)
                pl.wait_ge(add_done[p], 16)
            for p in range(2):
                pl.wait_ge(x3_done[p], 16 * NT // 2)
            row_meta(0, 0, 0)
            row_meta(1, 0, 1)

            def expert_step(n, j, b, more=True):
                if more:
                    row_meta(j + 2, n + (b + 2) // XB, (b + 2) % XB)
                add_rows(j, b)

            groups(pl, NET // XB - 1, expert_step, XB)
            for b in range(XB):
                expert_step(NET // XB - 1, NET - XB + b, b, more=b < XB - 2)

        @block.scalar
        def _(act):
            def copy_t(T, dst, ready, done):
                act.wait_ge(ready, T.t + 1)
                nc.scalar.activation(dst.rearrange("p a b -> p (a b)"), bank[0][:, 0:D], ACT.Copy).then_inc(done, 1)

            def kv_copy(T):
                act.wait_ge(S["kv_ps"], T.t + 1)
                past(act, S["av_out"], QCH * (T.t - 1))
                nc.scalar.activation(kv[T.p][:, :], bank[6][:, :], ACT.Copy).then_inc(S["kv_out"], 1)

            def route_exp(T):
                act.wait_ge(S["lmax_out"], T.t + 1)
                nc.scalar.activation(exp_l[:, :], bank[3][:, 0:E], ACT.Exp, bias=neg_max[:, 0:1],
                                     accum_out=sum_l[:, 0:1]).then_inc(S["expl_out"], 1)

            def value_copy(T):
                act.wait_ge(S["pv_ps"], T.t + 1)
                past(act, S["ret_ps"], T.t)
                nc.scalar.activation(v_sb[:, :], bank[2][:, D:2 * D], ACT.Copy).then_inc(S["v_out"], 1)

            def pass_copy(T):
                past(act, S["sc_ps"], T.t)
                for h in range(RH):
                    r = slice(ROT * h, ROT * h + ROT)
                    nc.scalar.activation(q_pass[r, h, :], bank[2][r, 0:P], ACT.Copy)
                nc.scalar.activation(k_pass[:, :], bank[2][:, P:2 * P], ACT.Copy).then_inc(S["pass_out"], 1)

            def rot_copy(T):
                act.wait_ge(S["rot_out"], T.t + 1)
                for h in range(RH):
                    r = slice(ROT * h, ROT * h + ROT)
                    last = nc.scalar.activation(q_rot[r, h, :], qk_rot[r, 0, :], ACT.Copy)
                last.then_inc(S["qrot_out"], 1)

            def gate_exp(T):
                act.wait_ge(S["gm_out"], T.t + 1)
                past(act, S["ng_out"], T.t)
                nc.scalar.activation(e_g[:, :], gm[:, :], ACT.Exp).then_inc(S["eg_out"], 1)

            def gate_rec(T):
                act.wait_ge(S["ng_out"], T.t + 1)
                nc.scalar.activation(ln_g[:, :], n_g[:, :], ACT.Ln, bias=two[:, 0:1]).then_inc(S["achain"], 1)
                act.wait_ge(S["achain"], T.t + 1)
                past(act, S["th_out"], T.t)
                nc.scalar.activation(rec_g[:, :], ln_g[:, :], ACT.Exp, scale=-1.0).then_inc(S["rec_out"], 1)

            def shared_silu(T):
                act.wait_ge(S["sg_ps"], T.t + 1)
                past(act, S["sha_out"], T.t)
                nc.scalar.activation(sh_s[:, 0:2, :], bank[1][:, 0:2 * P].rearrange("p (a b) -> p a b", a=2), ACT.Silu)
                nc.scalar.activation(sh_s[0:96, 2, :], bank[1][0:96, 2 * P:3 * P], ACT.Silu).then_inc(S["shs_out"], 1)
                nc.scalar.preload_act_table_set("natural_log_exp_and_others")

            def group_sums(T):
                act.wait_ge(S["ret_ps"], T.t + 1)
                past(act, S["stat_ps"], T.t)
                for k, f in enumerate((ACT.Copy, ACT.Square)):
                    for j in range(4):
                        cols = slice(SEQ * j, SEQ * j + SEQ)
                        last = nc.scalar.activation(ret_terms[:, k, cols], bank[6][:, cols], f,
                                                    accum_out=sums[:, 4 * k + j:4 * k + j + 1])
                last.then_inc(S["sums_out"], 1)

            def normalise(T, s, src, dst):
                act.wait_ge(S[f"ln{s + 1}_rstd"], T.t + 1)
                nc.scalar.activation(dst, src, ACT.Identity, bias=ln_bias[s][:, 0:1], scale=rstd[s][:, 0:1]
                                     ).then_inc(S[f"ln{s + 1}_out"], 1)

            def ln1_out(T):
                past(act, S["xT1_ps"], T.t)
                normalise(T, 0, xin[T.p][:, :], xn1[:, :])

            def ln2_out(T):
                past(act, S["xT2_ps"], T.t)
                normalise(T, 1, x1[T.p][:, :], xn2[:, :])

            def ln3_out(T):
                past(act, scat_done[T.p], 16 * TOPK * T.half)
                normalise(T, 2, x2[T.p][:, :], xn3[T.p])

            def residual1(T):
                act.wait_ge(S["wo_ps"], T.t + 1)
                past(act, S["xo_ps"], T.t - 1)
                nc.scalar.activation(x1[T.p][:, :], bank[7][:, 0:D], ACT.Copy).then_inc(S["x1_out"], 1)

            def residual2(T):
                act.wait_ge(S["xo_ps"], T.t + 1)
                past(act, S["shd_ps"], T.t - 1)
                nc.scalar.activation(x2[T.p][:, :], bank[7][:, 0:D], ACT.Copy).then_inc(S["x2_out"], 1)

            def residual3(T):
                act.wait_ge(S["shd_ps"], T.t + 1)
                past(act, x3_done[T.p], 16 * T.half)
                nc.scalar.activation(x3[T.p][:, :], bank[7][:, 0:D], ACT.Copy).then_inc(S["xall_out"], 1)

            def soft_exp(T):
                act.wait_ge(S["sub_out"], T.t + 1)
                past(act, S["av_out"], QCH * (T.t - 1))
                nc.scalar.activation(prob[T.p][:, :], score_sub[:, :], ACT.Exp).then_inc(S["prob_out"], 1)

            def group_norm(T):
                act.wait_ge(S["gaff_out"], T.t + 1)
                past(act, S["my_out"], T.t)
                for j in range(4):
                    last = nc.scalar.activation(
                        y_sb[:, j // 2, SEQ * (j % 2):SEQ * (j % 2) + SEQ], bank[6][:, SEQ * j:SEQ * j + SEQ],
                        ACT.Identity, bias=gshift[:, j:j + 1], scale=gscale[:, j:j + 1])
                last.then_inc(S["y_out"], 1)

            act.wait_ge(S["consts"], 1)
            nc.scalar.preload_act_table_set("natural_log_exp_and_others")

            def step(n, c):
                T = stage_tiles(n, c)
                at(T[4], copy_t, xT3[:, :, :], S["xT3_ps"], S["xT3_sb"])
                at(T[3], soft_exp)
                at(T[1], gate_exp)
                at(T[2], residual1)
                at(T[4], route_exp)
                at(T[4], shared_silu)
                at(T[2], ln2_out)
                at(T[2], copy_t, xT2[:, :, :], S["xT2_ps"], S["xT2_sb"])
                at(T[1], rot_copy)
                at(T[2], kv_copy)
                at(T[4], residual3)
                at(T[1], group_sums)
                at(T[0], ln1_out)
                at(T[3], copy_t, attn_t[:, :, :], S["aT_ps"], S["aT_sb"])
                at(T[1], gate_rec)
                at(T[0], copy_t, xT1[:, :, :], S["xT1_ps"], S["xT1_sb"])
                at(T[3], residual2)
                at(T[1], group_norm)
                at(T[3], ln3_out)
                at(T[0], value_copy)
                at(T[0], pass_copy)

            steps(act, step)

            for p in range(2):
                act.wait_ge(scat_done[p], 16 * TOPK * NT // 2)
            act.wait_ge(S["tail_out"], 1)
            for e in range(1, E, 2):
                r = act.value_load(tail_i[0:1, e:e + 1], min_val=0, max_val=ROWS - P)
                act.dma_start(rows_dram[bass.ds(r, P), :], padding[:, :]).then_inc(S["tail_in"], 16)

            def xT_out(j, p):
                act.wait_ge(S["eT_ps"], j + 1)
                past(act, S["egu_ps"], j - 1)
                nc.scalar.activation(xeT[p].rearrange("p a b -> p (a b)"), bank[p][:, 0:D], ACT.Copy).then_inc(S["eT_sb"], 1)

            def silu(j, p):
                act.wait_ge(S["egu_ps"], j + 1)
                past(act, S["ea_out"], j - 1)
                nc.scalar.activation(he[p], bank[2 + p][:, 0:INNER], ACT.Silu).then_inc(S["eh_out"], 1)

            def weigh(j, half, b):
                act.wait_ge(S["ey_ps"], j + 1)
                act.wait_ge(S["meta_out"], j + 1)
                past(act, add_done[b % 2], 16 * (half + 1))
                nc.scalar.activation(ye[b % 2], bank[6 + b % 2][:, 0:D], ACT.Copy, scale=weight[b][:, 0:1]
                                     ).then_inc(S["ey_out"], 1)

            def expert_step(n, j, b, first=False, turn=True, up=True):
                if up:
                    silu(j + 1, (b + 1) % 2)
                if turn:
                    xT_out(j + 2, b % 2)
                if not first:
                    weigh(j - 1, 2 * n + (b - 1) // 2, (b - 1) % XB)

            xT_out(0, 0)
            silu(0, 0)
            xT_out(1, 1)
            groups(act, NET // XB - 1, lambda n, j, b: expert_step(n, j, b, first=type(j) is int and j == 0), XB)
            for b in range(XB):
                expert_step(NET // XB - 1, NET - XB + b, b, turn=b < XB - 2, up=b < XB - 1)
            weigh(NET - 1, NET // 2 - 1, XB - 1)

        @block.tensor
        def _(pe):
            pe.wait_ge(S["tables_in"], 16 * 10)
            pe.wait_ge(S["ret_weights_in"], 16 * 4)
            pe.wait_ge(S["prep"], 1)
            mm = nc.tensor.matmul

            def bank_free(n, *users):
                for user in users if type(n) is int else users[:1]:
                    for s, v in user:
                        past(pe, s, v)

            def turn(T, src, ready, done):
                pe.wait_ge(ready, T.t + 1)
                for k in range(KC):
                    last = nc.tensor.transpose(bank[0][:, k * P:(k + 1) * P], src[:, k * P:(k + 1) * P], ident[:, :])
                last.then_inc(done, 1)

            def add_bias(dst, c0, cols, stop):
                return mm(dst, ones[0:3, :], bias_parts[:, c0:c0 + cols], start=False, stop=stop)

            def add_rows(dst, x):
                return mm(dst, ident[:, :], x[:, :], start=False, stop=True)

            def queries(T):
                pe.wait_ge(S["xT2_sb"], T.t + 1)
                past(pe, S["prod_out"], QCH * T.t)
                for k in range(KC):
                    mm(bank[5][:, 0:D], xT2[:, k, :], w_xq[:, k, :], start=(k == 0), stop=False)
                add_bias(bank[5][:, 0:D], 0, D, True).then_inc(S["q_ps"], 1)

            def keys_values(T):
                pe.wait_ge(ctx_in[T.p], 16 * (T.half + 1))
                for k in range(KC):
                    mm(bank[6][:, :], ctx_t[T.p][:, k, :], w_xkv[:, k, :], start=(k == 0), stop=False)
                add_bias(bank[6][:, :], D, 2 * D, True).then_inc(S["kv_ps"], 1)

            def logits(T):
                pe.wait_ge(S["xT3_sb"], T.t + 1)
                for k in range(KC):
                    last = mm(bank[3][:, 0:E], xT3[:, k, :], w_route[:, k, :], start=(k == 0), stop=(k == KC - 1))
                last.then_inc(S["logit_ps"], 1)

            def rot_in(T):
                pe.wait_ge(S["xT1_sb"], T.t + 1)
                for f in range(4):
                    for k in range(KC):
                        last = mm(bank[1][:, f * P:(f + 1) * P], w_qk[:, k, f, :], xT1[:, k, :], start=(k == 0), stop=(k == KC - 1))
                last.then_inc(S["qk_ps"], 1)

            def pass_in(T):
                for f in range(2):
                    for k in range(KC):
                        mm(bank[2][:, f * P:(f + 1) * P], w_qk[:, k, 4 + f, :], xT1[:, k, :], start=(k == 0), stop=(k == KC - 1))
                for k in range(KC):
                    last = mm(bank[2][:, D:2 * D], xT1[:, k, :], w_v[:, k, :], start=(k == 0), stop=(k == KC - 1))
                last.then_inc(S["pv_ps"], 1)

            def gate_in(T):
                past(pe, S["mish_out"], T.t)
                for f in range(KC):
                    for k in range(KC):
                        last = mm(bank[4][:, f * P:(f + 1) * P], w_g[:, k, f * P:(f + 1) * P], xT1[:, k, :],
                                  start=(k == 0), stop=(k == KC - 1))
                last.then_inc(S["g_ps"], 1)

            def cross_out(T):
                pe.wait_ge(S["aT_sb"], T.t + 1)
                for k in range(KC):
                    mm(bank[7][:, 0:D], attn_t[:, k, :], w_xo[:, k, :], start=(k == 0), stop=False)
                add_bias(bank[7][:, 0:D], 3 * D, D, False)
                add_rows(bank[7][:, 0:D], x1[T.p]).then_inc(S["xo_ps"], 1)

            def ranks(T):
                pe.wait_ge(S["chosen_out"], T.t + 1)
                mm(bank[3][:, 0:E], before[:, :], chosen[:, :], start=True, stop=True)
                mm(bank[3][:, E:2 * E], ones[:, :], chosen[:, :], start=True, stop=True).then_inc(S["rank_ps"], 1)

            def ret_scores(T):
                pe.wait_ge(S["qrot_out"], T.t + 1)
                pe.wait_ge(S["pass_out"], T.t + 1)
                mm(bank[3][:, :], qk_rot[:, 1, :], q_rot[:, :, :].rearrange("p h t -> p (h t)"), start=True, stop=False)
                mm(bank[3][:, :], k_pass[:, :], q_pass[:, :, :].rearrange("p h t -> p (h t)"), start=False,
                   stop=True).then_inc(S["sc_ps"], 1)

            def shared_in(T, w, b, done):
                pe.wait_ge(S["xT3_sb"], T.t + 1)
                for j, (r0, rows) in enumerate(SHC):
                    for k in range(KC):
                        last = mm(bank[b][0:rows, j * P:(j + 1) * P], w[:, k, r0:r0 + rows], xT3[:, k, :],
                                  start=(k == 0), stop=(k == KC - 1))
                last.then_inc(done, 1)

            def retain(T):
                pe.wait_ge(S["att_out"], T.t + 1)
                pe.wait_ge(S["v_out"], T.t + 1)
                for h in range(RH):
                    last = mm(bank[6][RD * (h % 2):RD * (h % 2) + RD, (h // 2) * P:(h // 2 + 1) * P],
                              v_sb[:, h * RD:(h + 1) * RD], att_t[:, h * P:(h + 1) * P], start=True, stop=True)
                last.then_inc(S["ret_ps"], 1)

            def group_moments(T):
                pe.wait_ge(S["sums_out"], T.t + 1)
                mm(bank[3][:, 0:8], head_mean[:, :], sums[:, :], start=True, stop=True).then_inc(S["stat_ps"], 1)

            def shared_out(T):
                pe.wait_ge(S["sha_out"], T.t + 1)
                for j, (r0, rows) in enumerate(SHC):
                    mm(bank[7][:, 0:D], sh_a[0:rows, j, :], w_sd[0:rows, j, :], start=(j == 0), stop=False)
                add_rows(bank[7][:, 0:D], x2[T.p]).then_inc(S["shd_ps"], 1)

            def ret_out(T):
                pe.wait_ge(S["my_out"], T.t + 1)
                for k in range(KC):
                    mm(bank[7][:, 0:D], my[:, k, :], w_o[:, k, :], start=(k == 0), stop=False)
                add_rows(bank[7][:, 0:D], xin[T.p]).then_inc(S["wo_ps"], 1)

            def step(n, c):
                T = stage_tiles(n, c)
                if type(n) is int and c == 2:
                    pe.wait_ge(S["weights_in"], 16 * 9)

                def read(names, stage, this_step=False):
                    return [(S[name], through(n, c if this_step else c - 1, stage)) for name in names.split()]

                if T[2]:
                    bank_free(n, read("x2_out", 3), read("xall_out", 4), read("x1_out", 2))
                    ret_out(T[2])
                if T[4]:
                    bank_free(n, read("gvar_out", 1), read("att_out", 1), read("rows_out", 4), read("expl_out", 4))
                    logits(T[4])
                    bank_free(n, read("rot_parts", 0), read("shs_out", 4))
                    shared_in(T[4], w_sg, 1, S["sg_ps"])
                if T[2]:
                    bank_free(n, read("y_out", 1), read("kv_out", 2))
                    keys_values(T[2])
                if T[4]:
                    bank_free(n, read("expl_out", 4, True), read("gvar_out", 1), read("att_out", 1), read("rows_out", 4))
                    ranks(T[4])
                    bank_free(n, read("pass_out", 0), read("sha_out", 4))
                    shared_in(T[4], w_su, 2, S["su_ps"])
                if T[2]:
                    bank_free(n, read("xT3_sb", 3), read("xT1_sb", 0), read("aT_sb", 3), read("xT2_sb", 2))
                    turn(T[2], xn2, S["ln2_out"], S["xT2_ps"])
                    queries(T[2])
                if T[1]:
                    bank_free(n, read("rows_out", 4, True), read("expl_out", 4, True), read("gvar_out", 1), read("att_out", 1))
                    ret_scores(T[1])
                if T[4]:
                    bank_free(n, read("x1_out", 2, True), read("x2_out", 3), read("xall_out", 4))
                    shared_out(T[4])
                if T[1]:
                    bank_free(n, read("kv_out", 2, True), read("y_out", 1))
                    retain(T[1])
                    bank_free(n, read("att_out", 1, True), read("rows_out", 4, True), read("expl_out", 4, True), read("gvar_out", 1))
                    group_moments(T[1])
                if T[3]:
                    bank_free(n, read("xT2_sb", 2, True), read("xT3_sb", 3), read("xT1_sb", 0), read("aT_sb", 3))
                    turn(T[3], attn_n, S["attnn_out"], S["aT_ps"])
                if T[0]:
                    bank_free(n, read("aT_sb", 3, True), read("xT2_sb", 2, True), read("xT3_sb", 3), read("xT1_sb", 0))
                    turn(T[0], xn1, S["ln1_out"], S["xT1_ps"])
                if T[3]:
                    bank_free(n, read("xall_out", 4, True), read("x1_out", 2, True), read("x2_out", 3))
                    cross_out(T[3])
                if T[0]:
                    bank_free(n, read("shs_out", 4, True), read("rot_parts", 0))
                    rot_in(T[0])
                    bank_free(n, read("sha_out", 4, True), read("pass_out", 0))
                    pass_in(T[0])
                    gate_in(T[0])
                if T[3]:
                    bank_free(n, read("xT1_sb", 0, True), read("aT_sb", 3, True), read("xT2_sb", 2, True), read("xT3_sb", 3))
                    turn(T[3], xn3[T[3].p], S["ln3_out"], S["xT3_ps"])

            steps(pe, step)

            pe.wait_ge(S["past_out"], 1)
            mm(bank[0][0:1, 0:2 * NET], one, past_it[:, :, :].rearrange("p a b -> p (a b)"), start=True, stop=True
               ).then_inc(S["past_ps"], 1)
            pe.wait_ge(S["expert_w0"], 2 * 16 * E)
            pe.wait_ge(S["xall_out"], NT)
            pe.wait_ge(S["tab_out"], 1)

            def e_turn(j, turn, b):
                p = b % 2
                pe.wait_ge(xe_in[b], 16 * (turn + 1))
                past(pe, S["eT_sb"], j - 1)
                for k in range(KC):
                    last = nc.tensor.transpose(bank[p][:, k * P:(k + 1) * P], xe[b][:, k * P:(k + 1) * P], ident[:, :])
                last.then_inc(S["eT_ps"], 1)

            def expert_of(j):
                return pe.value_load(table[0:1, 0, bass.ds(j, 1)], min_val=0, max_val=E - 1)

            def e_up(j, e, p):
                pe.wait_ge(S["eT_sb"], j + 1)
                past(pe, S["ea_out"], j - 1)
                for k in range(KC):
                    last = mm(bank[2 + p][:, 0:2 * INNER], xeT[p][:, k, :],
                              w_gu[:, bass.ds(e, 1), k, :].rearrange("p e n -> p (e n)"), start=(k == 0), stop=(k == KC - 1))
                last.then_inc(S["egu_ps"], 1)

            def e_turn2(j, p):
                pe.wait_ge(S["ea_out"], j + 1)
                past(pe, S["eaT_sb"], j - 1)
                for k in range(2):
                    last = nc.tensor.transpose(bank[4 + p][0:HI, k * P:(k + 1) * P], ae[p][:, k * HI:(k + 1) * HI], ident[:, :])
                last.then_inc(S["eaT_ps"], 1)

            def e_down(j, e, p):
                pe.wait_ge(S["eaT_sb"], j + 1)
                past(pe, S["ey_out"], j - 1)
                for k in range(2):
                    last = mm(bank[6 + p][:, 0:D], aeT[p][:, k, :],
                              w_d[:, bass.ds(e, 1), k, :].rearrange("p e n -> p (e n)"), start=(k == 0), stop=(k == 1))
                last.then_inc(S["ey_ps"], 1)

            def expert_group(n, last=False):
                first = type(n) is int and n == 0
                ahead = expert_of(GROUP * n + 1)
                for b in range(GROUP):
                    j = GROUP * n + b
                    if not last or b + 1 < GROUP:
                        e_up(j + 1, ahead, (b + 1) % 2)
                    if b + 1 < GROUP and (not last or b + 2 < GROUP):
                        ahead = expert_of(j + 2)
                    if not first or b > 0:
                        behind = expert_of(j - 1)
                    if not last or b + 2 < GROUP:
                        e_turn(j + 2, GROUP // XB * n + (b + 2) // XB, (b + 2) % XB)
                    e_turn2(j, b % 2)
                    if not first or b > 0:
                        e_down(j - 1, behind, (b + 1) % 2)

            e_turn(0, 0, 0)
            e_up(0, expert_of(0), 0)
            e_turn(1, 0, 1)
            expert_group(0)
            with pe.Fori(1, NET // GROUP - 1) as n:
                expert_group(n)
            expert_group(NET // GROUP - 1, last=True)
            e_down(NET - 1, expert_of(NET - 1), 1)

        @block.vector
        def _(dve):
            v = nc.vector
            links = [0]

            def link(ins):
                links[0] += 1
                ins.then_inc(S["chain"], 1)
                dve.wait_ge(S["chain"], links[0])

            dve.wait_ge(S["tables_in"], 16 * 10)
            dve.wait_ge(S["bias_in"], 16)
            link(v.tensor_copy(bias_hi[:, :], bias3[:, :]))
            link(v.tensor_tensor(bias_r[:, :], bias3[:, :], bias_hi[:, :], ALU.subtract))
            link(v.tensor_copy(bias_mid[:, :], bias_r[:, :]))
            link(v.tensor_tensor(bias_r[:, :], bias_r[:, :], bias_mid[:, :], ALU.subtract))
            link(v.tensor_copy(bias_lo[:, :], bias_r[:, :]))
            link(v.tensor_scalar(bias_r[:, :], bias_hi[:, :], eye3[:, 0:1], None, ALU.mult))
            link(v.scalar_tensor_tensor(out=bias_r[:, :], in0=bias_mid[:, :], scalar=eye3[:, 1:2], in1=bias_r[:, :],
                                        op0=ALU.mult, op1=ALU.add))
            link(v.scalar_tensor_tensor(out=bias_parts[:, :], in0=bias_lo[:, :], scalar=eye3[:, 2:3], in1=bias_r[:, :],
                                        op0=ALU.mult, op1=ALU.add))
            link(v.tensor_copy(before[:, :], before_f[:, :]))
            link(v.memset(two[:, :], 2.0))
            dve.wait_ge(S["consts"], 1)
            link(v.tensor_copy(row_base[:, :], region0))
            dve.wait_ge(S["padding_in"], 1)
            v.tensor_copy(padding[:, D + E:RW], small[:, 57:58]).then_inc(S["padding_out"], 1)
            link(v.memset(ones_row[:, :], 1.0))
            v.memset(chosen[:, :], 0.0).then_inc(S["prep"], 1)
            ch = {k: sem(f"chain_{k}") for k in ("ln1", "ln2", "ln3", "ln1_eps", "ln2_eps", "ln3_eps", "gn", "top", "rows", "soft")}

            def ln_stats(T, s, src):
                past(dve, S[f"ln{s + 1}_rstd"], T.t)
                v.bn_stats(stats[s][:, :], src[T.p][:, :]).then_inc(ch[f"ln{s + 1}"], 1)

            def ln1_stats(T):
                alone(dve, xin_in[T.p], 16 * (T.half + 1))
                ln_stats(T, 0, xin)

            def ln2_stats(T):
                dve.wait_ge(S["x1_out"], T.t + 1)
                ln_stats(T, 1, x1)

            def ln3_stats(T):
                dve.wait_ge(S["x2_out"], T.t + 1)
                ln_stats(T, 2, x2)

            def ln_mean(T, s):
                alone(dve, ch[f"ln{s + 1}"], T.t + 1)
                v.bn_aggr(mv[s][:, :], stats[s][:, :]).then_inc(ch[f"ln{s + 1}_eps"], 1)

            def ln_eps(T, s):
                dve.wait_ge(ch[f"ln{s + 1}_eps"], T.t + 1)
                v.tensor_scalar(var_eps[s][:, :], mv[s][:, 1:2], EPS, None, ALU.add).then_inc(S[f"ln{s + 1}_var"], 1)

            def q_prod(T, q):
                if q == 0:
                    dve.wait_ge(S["q_ps"], T.t + 1)
                    dve.wait_ge(S["kv_out"], T.t + 1)
                past(dve, S["score_out"], QCH * T.t + q - 1)
                qq = bank[5][:, q * QH * XD:(q + 1) * QH * XD].rearrange("p (h d) -> p h d", d=XD)
                kk = kv[T.p][:, 0:D].rearrange("p (g d) -> p g d", d=XD)
                v.tensor_tensor(prod[:, q % 2, :].rearrange("p (h g d) -> p h g d", h=QH, g=XH),
                                qq.unsqueeze(2).to_broadcast([P, QH, XH, XD]),
                                kk.unsqueeze(1).to_broadcast([P, QH, XH, XD]), ALU.mult).then_inc(S["prod_out"], 1)

            def q_sum(T, q):
                dve.wait_ge(S["prod_out"], QCH * T.t + q + 1)
                v.tensor_reduce(scores[:, q * QH * XH:(q + 1) * QH * XH],
                                prod[:, q % 2, :].rearrange("p (a d) -> p a d", d=XD), AX_X, ALU.add
                                ).then_inc(S["score_out"], 1)

            def soft_max(T):
                dve.wait_ge(S["score_out"], QCH * (T.t + 1))
                s3 = scores[:, :].rearrange("p (h g) -> p h g", g=XH)
                v.tensor_reduce(score_max[:, :], s3, AX_X, ALU.max).then_inc(ch["soft"], 1)

            def soft_sub(T):
                s3 = scores[:, :].rearrange("p (h g) -> p h g", g=XH)
                dve.wait_ge(ch["soft"], T.t + 1)
                v.tensor_tensor(score_sub[:, :].rearrange("p (h g) -> p h g", g=XH), s3,
                                score_max[:, :].unsqueeze(2).to_broadcast([P, XH, XH]), ALU.subtract
                                ).then_inc(S["sub_out"], 1)

            def soft_sum(T):
                dve.wait_ge(S["prob_out"], T.t + 1)
                v.tensor_reduce(prob_sum[:, :], prob[T.p][:, :].rearrange("p (h g) -> p h g", g=XH), AX_X, ALU.add
                                ).then_inc(S["psum_out"], 1)

            def soft_rec(T):
                dve.wait_ge(S["psum_out"], T.t + 1)
                v.reciprocal(prob_rec[T.p][:, :], prob_sum[:, :]).then_inc(S["prec_out"], 1)

            def a_sum(T, q):
                dve.wait_ge(S["av_out"], QCH * T.t + q + 1)
                v.tensor_reduce(attn[:, q * QH * XD:(q + 1) * QH * XD],
                                av[:, q % 2, :].rearrange("p (a g) -> p a g", g=XH), AX_X, ALU.add
                                ).then_inc(S["attn_out"], 1)

            def a_norm(T):
                dve.wait_ge(S["attn_out"], QCH * (T.t + 1))
                dve.wait_ge(S["prec_out"], T.t + 1)
                v.tensor_tensor(attn_n[:, :].rearrange("p (h d) -> p h d", d=XD),
                                attn[:, :].rearrange("p (h d) -> p h d", d=XD),
                                prob_rec[T.p][:, :].unsqueeze(2).to_broadcast([P, XH, XD]), ALU.mult
                                ).then_inc(S["attnn_out"], 1)

            def rotate(T):
                dve.wait_ge(S["qk_ps"], T.t + 1)
                past(dve, S["rot_out"], T.t)
                b3 = bank[1][:, :].rearrange("p (f t) -> p f t", f=4)
                v.tensor_tensor(cos_part[:, :, :], b3[:, 0:2, :], rot_tab[:, 0:2, :], ALU.mult)
                v.tensor_tensor(sin_part[:, :, :], b3[:, 2:4, :], rot_tab[:, 2:4, :], ALU.mult).then_inc(S["rot_parts"], 1)

            def gate_min(T):
                dve.wait_ge(S["g_ps"], T.t + 1)
                past(dve, S["eg_out"], T.t)
                v.tensor_scalar(gm[:, :], bank[4][:, 0:D], 18.0, None, ALU.min).then_inc(S["gm_out"], 1)

            def gate_n(T):
                dve.wait_ge(S["eg_out"], T.t + 1)
                past(dve, S["th_out"], T.t)
                v.scalar_tensor_tensor(out=n_g[:, :], in0=e_g[:, :], scalar=2.0, in1=e_g[:, :], op0=ALU.add,
                                       op1=ALU.mult).then_inc(S["ng_out"], 1)

            def gate_mish(T):
                dve.wait_ge(S["th_out"], T.t + 1)
                past(dve, S["my_out"], T.t)
                v.tensor_tensor(mish[:, :], bank[4][:, 0:D], th_g[:, :], ALU.mult).then_inc(S["mish_out"], 1)

            def decay(T):
                dve.wait_ge(S["sc_ps"], T.t + 1)
                v.tensor_tensor(att_t[:, :], bank[3][:, :], decay_tab[:, :], ALU.mult).then_inc(S["att_out"], 1)

            def ret_moments(T):
                c = ch["gn"]
                dve.wait_ge(S["stat_ps"], T.t + 1)
                past(dve, S["gaff_out"], T.t)
                v.tensor_copy(moments[:, :], bank[3][:, 0:8]).then_inc(c, 1)

            def var_mean(T):
                c = ch["gn"]
                dve.wait_ge(c, 2 * T.t + 1)
                v.scalar_tensor_tensor(out=neg_msq[:, :], in0=moments[:, 0:4], scalar=-1.0, in1=moments[:, 0:4],
                                       op0=ALU.mult, op1=ALU.mult).then_inc(c, 1)

            def var_out(T):
                c = ch["gn"]
                dve.wait_ge(c, 2 * T.t + 2)
                v.scalar_tensor_tensor(out=gvar[:, :], in0=moments[:, 4:8], scalar=EPS, in1=neg_msq[:, :],
                                       op0=ALU.add, op1=ALU.add).then_inc(S["gvar_out"], 1)

            def route_max(T):
                dve.wait_ge(S["logit_ps"], T.t + 1)
                v.tensor_reduce(neg_max[:, :], bank[3][:, 0:E], AX_X, ALU.max, negate=True).then_inc(S["lmax_out"], 1)

            top, rows = ch["top"], ch["rows"]

            def top_rec(T):
                dve.wait_ge(S["expl_out"], T.t + 1)
                v.reciprocal(rec_l[:, :], sum_l[:, :]).then_inc(top, 1)

            def top_prob(T):
                dve.wait_ge(top, 6 * T.t + 1)
                v.tensor_scalar(row3[T.p][:, D:D + E], exp_l[:, :], rec_l[:, 0:1], None, ALU.mult).then_inc(top, 1)
                v.tensor_copy(row3[T.p][:, D + E:RW], token_no[:, bass.ds(T.t, 1)]).then_inc(top, 1)

            def top_max(T):
                alone(dve, top, 6 * T.t + 3)
                v.max(top8[:, :], row3[T.p][:, D:D + E]).then_inc(top, 1)

            def top_index(T):
                alone(dve, top, 6 * T.t + 4)
                v.max_index(idx8[:, :], top8[:, :], row3[T.p][:, D:D + E]).then_inc(top, 1)

            def top_pick(T):
                dve.wait_ge(top, 6 * T.t + 5)
                v.tensor_tensor(pick[:, :, :], expert_no.unsqueeze(1).to_broadcast([P, TOPK, E]),
                                idx8[:, 0:TOPK].unsqueeze(2).to_broadcast([P, TOPK, E]), ALU.is_equal).then_inc(top, 1)

            def top_chosen(T):
                dve.wait_ge(top, 6 * T.t + 6)
                with nc.allow_low_precision(reason="zeros and ones"):
                    v.tensor_reduce(chosen[:, :], pick[:, :, :].rearrange("p k e -> p e k"), AX_X, ALU.add
                                    ).then_inc(S["chosen_out"], 1)

            def rows_place(T):
                dve.wait_ge(S["rank_ps"], T.t + 1)
                v.tensor_tensor(row_of[:, :], bank[3][:, 0:E], row_base[:, :], ALU.add).then_inc(rows, 1)

            def rows_pick(T):
                dve.wait_ge(rows, 4 * T.t + 1)
                v.tensor_tensor(row_base[:, :], bank[3][:, E:2 * E], row_base[:, :], ALU.add).then_inc(rows, 1)
                v.tensor_tensor(pick_row[:, :, :], pick[:, :, :], row_of[:, :].unsqueeze(1).to_broadcast([P, TOPK, E]),
                                ALU.mult).then_inc(rows, 1)

            def rows_sum(T):
                dve.wait_ge(rows, 4 * T.t + 3)
                v.tensor_reduce(row_f[:, :], pick_row[:, :, :], AX_X, ALU.add).then_inc(rows, 1)

            def rows_out(T):
                past(dve, scat_done[T.p], 16 * TOPK * T.half)
                dve.wait_ge(rows, 4 * T.t + 4)
                v.tensor_copy(row_u[T.p][:, :], row_f[:, :]).then_inc(S["rows_out"], 1)

            def shared_mul(T):
                dve.wait_ge(S["shs_out"], T.t + 1)
                dve.wait_ge(S["su_ps"], T.t + 1)
                v.tensor_tensor(sh_a[:, 0:2, :], bank[2][:, 0:2 * P].rearrange("p (a b) -> p a b", a=2), sh_s[:, 0:2, :], ALU.mult)
                v.tensor_tensor(sh_a[0:96, 2, :], bank[2][0:96, 2 * P:3 * P], sh_s[0:96, 2, :], ALU.mult
                                ).then_inc(S["sha_out"], 1)

            def step(n, c):
                T = stage_tiles(n, c)
                at(T[4], route_max)
                at(T[1], gate_n)
                at(T[2], ln2_stats)
                at(T[4], top_rec)
                at(T[2], ln_mean, 1)
                at(T[4], top_prob)
                at(T[3], soft_sum)
                at(T[4], top_max)
                at(T[4], top_index)
                at(T[2], ln_eps, 1)
                at(T[4], top_pick)
                at(T[3], soft_rec)
                at(T[4], top_chosen)
                at(T[3], a_sum, 0)
                at(T[4], rows_place)
                at(T[4], rows_pick)
                at(T[4], rows_sum)
                at(T[0], ln1_stats)
                at(T[0], ln_mean, 0)
                at(T[4], rows_out)
                at(T[4], shared_mul)
                at(T[3], a_sum, 1)
                at(T[2], q_prod, 0)
                at(T[0], ln_eps, 0)
                at(T[2], q_sum, 0)
                at(T[1], decay)
                at(T[3], a_sum, 2)
                at(T[2], q_prod, 1)
                at(T[3], a_sum, 3)
                at(T[1], ret_moments)
                at(T[3], a_norm)
                at(T[2], q_sum, 1)
                at(T[1], var_mean)
                at(T[2], q_prod, 2)
                at(T[1], var_out)
                at(T[2], q_sum, 2)
                at(T[3], ln3_stats)
                at(T[3], ln_mean, 2)
                at(T[2], q_prod, 3)
                at(T[3], ln_eps, 2)
                at(T[1], gate_mish)
                at(T[2], q_sum, 3)
                at(T[0], rotate)
                at(T[2], soft_max)
                at(T[2], soft_sub)
                at(T[0], gate_min)

            steps(dve, step)

            dve.wait_ge(S["rows_out"], NT)
            v.tensor_copy(tail_i[0:1, :], row_base[0:1, :]).then_inc(S["tail_out"], 1)
            link(v.tensor_tensor(cnt[:, 0:E], row_base[:, :], region0, ALU.subtract))
            link(v.tensor_scalar(cnt[:, :], cnt[:, :], float(P - 1), None, ALU.add))
            link(v.tensor_copy(cnt_i[:, :], cnt[:, :]))
            link(v.tensor_scalar(cnt_i[:, :], cnt_i[:, :], 7, None, ALU.arith_shift_right))
            link(v.tensor_copy(cnt[:, :], cnt_i[:, :]))
            link(v.tensor_tensor_scan(cum[:, :], ones_row[:, :], cnt[:, :], 0.0, ALU.mult, ALU.add))
            v.tensor_tensor(own[:, 0, :], cum[0:E, :], ident[0:E, 0:E], ALU.mult)
            link(v.tensor_tensor(own[:, 1, :], cnt[0:E, :], ident[0:E, 0:E], ALU.mult))
            link(v.tensor_reduce(per_expert[:, :], own[:, :, :], AX_X, ALU.add))
            v.tensor_scalar(past_it[:, 0, :], tile_no[0:E, :], per_expert[:, 0:1], None, ALU.is_ge)
            v.tensor_scalar(past_it[:, 1, :], tile_no[0:E, :], per_expert[:, 0:1], per_expert[:, 1:2], ALU.is_ge, ALU.mult
                            ).then_inc(S["past_out"], 1)
            dve.wait_ge(S["past_ps"], 1)
            expert_ps, before_ps = bank[0][0:1, 0:NET], bank[0][0:1, NET:2 * NET]
            link(v.scalar_tensor_tensor(out=region_of[:, :], in0=expert_ps, scalar=float(REG // P), in1=tile_no[0:1, :],
                                        op0=ALU.mult, op1=ALU.add))
            v.scalar_tensor_tensor(out=past_end[:, :], in0=expert_ps, scalar=float(E), in1=tile_no[0:1, :],
                                   op0=ALU.is_ge, op1=ALU.mult)
            link(v.tensor_tensor(first_row[:, :], region_of[:, :], before_ps, ALU.subtract))
            link(v.tensor_tensor(before_it[:, :], past_end[:, :], before_ps, ALU.max))
            for p in range(2):
                link(v.tensor_scalar(table[0:1, 2 + p, :], before_it[:, :], float(3 - p), None, ALU.add))
                link(v.tensor_scalar(table[0:1, 2 + p, :], table[0:1, 2 + p, :], 1, 4, ALU.arith_shift_right,
                                     ALU.arith_shift_left))
            v.tensor_scalar(table[0:1, 0, :], expert_ps, float(E - 1), None, ALU.min)
            v.tensor_scalar(table[0:1, 1, :], first_row[:, :], float(P), None, ALU.mult).then_inc(S["tab_out"], 1)

            def e_mul(j, p):
                dve.wait_ge(S["eh_out"], j + 1)
                past(dve, S["eaT_ps"], j - 1)
                v.tensor_tensor(ae[p], bank[2 + p][:, INNER:2 * INNER], he[p], ALU.mult).then_inc(S["ea_out"], 1)

            def e_turned(j, p):
                dve.wait_ge(S["eaT_ps"], j + 1)
                past(dve, S["ey_ps"], j - 1)
                v.tensor_copy(aeT[p].rearrange("p a b -> p (a b)"), bank[4 + p][0:HI, 0:D]).then_inc(S["eaT_sb"], 1)

            e_mul(0, 0)

            def expert_step(n, j, p):
                e_turned(j, p)
                e_mul(j + 1, 1 - p)

            groups(dve, (NET - 2) // 2, expert_step)
            e_turned(NET - 2, 0)
            e_mul(NET - 1, 1)
            e_turned(NET - 1, 1)


def layouts(x, ctx_2048, L0_attn_wqkv, L0_attn_wg, L0_attn_wo, L0_attn_gn_weight, L0_attn_gn_bias, L0_xattn_Wq,
            L0_xattn_bq, L0_xattn_Wk, L0_xattn_bk, L0_xattn_Wv, L0_xattn_bv, L0_xattn_Wo, L0_xattn_bo, L0_ffn_w_gate,
            L0_ffn_wg, L0_ffn_wu, L0_ffn_wd, L0_ffn_sg, L0_ffn_su, L0_ffn_sd):
    def chunks(w):
        return w.reshape(KC, P, -1).transpose(1, 0, 2).reshape(P, -1)

    a = {}
    a["x"] = x.reshape(TOKENS, D)
    a["ctx_t"] = ctx_2048.reshape(NT, P, KC, P).transpose(0, 3, 2, 1).reshape(NT * P, KC * P)
    w = L0_attn_wqkv.reshape(RH, 3, RD, D)
    q, k, v = w[:, 0], w[:, 1], w[:, 2]

    def turned(r):
        return r.reshape(RH, ROT // 2, 2, D)[:, :, ::-1, :].reshape(RH, ROT, D)

    six = [q[:, :ROT], k[:, :ROT], turned(q[:, :ROT]), turned(k[:, :ROT]), q[:, ROT:], k[:, ROT:]]
    six = np.stack([s.reshape(P, D) for s in six])
    a["w_qk"] = six.reshape(6, P, KC, P).transpose(3, 2, 0, 1).reshape(P, -1)
    a["w_v"] = chunks(v.reshape(D, D).T)
    a["w_g"] = chunks(L0_attn_wg.T)
    a["w_o"] = chunks(L0_attn_wo.T)
    for name, g in (("gn_w", L0_attn_gn_weight), ("gn_b", L0_attn_gn_bias)):
        a[name] = np.repeat(np.repeat(g.reshape(2, 2).T, RD, axis=0), 2, axis=1)
    a["w_xq"] = chunks(L0_xattn_Wq.T)
    a["w_xkv"] = chunks(np.concatenate([L0_xattn_Wk.T, L0_xattn_Wv.T], axis=1))
    a["w_xo"] = chunks(L0_xattn_Wo.T)
    a["bias"] = np.concatenate([L0_xattn_bq, L0_xattn_bk, L0_xattn_bv, L0_xattn_bo])
    a["w_route"] = chunks(L0_ffn_w_gate.T)
    a["w_sg"], a["w_su"], a["w_sd"] = chunks(L0_ffn_sg), chunks(L0_ffn_su), L0_ffn_sd
    gu = np.concatenate([L0_ffn_wg, L0_ffn_wu], axis=2)
    a["w_gu"] = gu.reshape(E, KC, P, 2 * INNER).transpose(0, 2, 1, 3).reshape(E * P, -1)
    a["w_d"] = L0_ffn_wd.reshape(E, 2, HI, D).transpose(0, 2, 1, 3).reshape(E * HI, -1)
    return a


def kernel(**inputs):
    import concourse.bacc as bacc
    from concourse.bass_utils import run_bass_kernel_spmd

    nc = bacc.Bacc("TRN2", target_bir_lowering=False, num_devices=1)
    arrays = layouts(**{k: np.asarray(a) for k, a in inputs.items()})
    arrays.update(constants())
    arrays = {k: np.ascontiguousarray(a) for k, a in arrays.items()}
    io = {k: nc.dram_tensor(f"in_{k}", a.shape, mybir.dt.from_np(a.dtype), kind="ExternalInput").ap() for k, a in arrays.items()}
    out = nc.dram_tensor("out_x", (TOKENS + P, D), F32, kind="ExternalOutput").ap()
    rows_dram = nc.dram_tensor("expert_rows", (ROWS, RW), F32, kind="Internal").ap()
    build(nc, io, out, rows_dram)
    r = run_bass_kernel_spmd(nc, [{f"in_{k}": a for k, a in arrays.items()}], core_ids=[0])
    return r.results[0]["out_x"][0:TOKENS].reshape(BATCH, SEQ, D)
```
